# Optimizing a Trainium2 kernel written in Bass

```python
import numpy as np
import jax
import jax.numpy as jnp

def _softmax(x, axis=-1):
    return jax.nn.softmax(x, axis=axis)

def _gelu(x):
    return jax.nn.gelu(x, approximate=True)

def _silu(x):
    return jax.nn.silu(x)

def _sigmoid(x):
    return jax.nn.sigmoid(x)

def _layernorm(x, axis=-1, eps=1e-05):
    m = jnp.mean(x, axis=axis, keepdims=True)
    v = jnp.var(x, axis=axis, keepdims=True)
    return (x - m) / jnp.sqrt(v + eps)

def _scatter_add(tgt, idx, src, axis=0):
    return tgt.at[idx].add(src)

def _segment_sum(src, seg, n):
    return jax.ops.segment_sum(src, seg, n)
kernel_name = 'mk_flamingo_gated_d2_seqx_r4_ae9ca8'

def setup_inputs(seed: int=0):
    np.random.seed(seed)
    _w = jnp.asarray

    def _rec_inputs():
        import jax
        import jax.numpy as jnp
        _rk = jax.random.key(seed)
        x = -0.000929 + 1 * jax.random.normal(jax.random.fold_in(_rk, 1), (32, 100, 512), jnp.float32)
        _lenS = 100 - jax.random.randint(jax.random.fold_in(_rk, 7), (32,), 0, max(1, 100 // 4) + 1, jnp.int32)
        _lenS2 = 361 - jax.random.randint(jax.random.fold_in(_rk, 8), (32,), 0, max(1, 361 // 4) + 1, jnp.int32)
        _ctx_2048P = jax.random.normal(jax.random.fold_in(_rk, 11), (32, 16, 512), jnp.float32)
        _ctx_2048c = jax.random.dirichlet(jax.random.fold_in(_rk, 511), 0.3 * jnp.ones((16,), jnp.float32), (32, 361))
        _ctx_2048t = jnp.einsum('bsk,bkd->bsd', _ctx_2048c, _ctx_2048P)
        _ctx_2048t = _ctx_2048t * jax.lax.rsqrt(jnp.mean(jnp.square(_ctx_2048t)) + 1e-12) * 0.953939
        ctx_2048 = 2.81802e-05 + 1.00001 * (_ctx_2048t + 0.3 * jax.random.normal(jax.random.fold_in(_rk, 611), (32, 361, 512), jnp.float32))
        _validS = jnp.arange(100)[None, :] < _lenS[:, None]
        _validS2 = jnp.arange(361)[None, :] < _lenS2[:, None]
        _causal = jnp.tril(jnp.ones((100, 100), dtype=bool))
        mask_BxSx4224_bf0 = jnp.logical_not(jnp.ones((32, 100, 1056), dtype=bool))
        _g = jax.random.normal(jax.random.fold_in(_rk, 9001), (2, 2), jnp.float32)
        _g = jnp.sign(_g) * jnp.maximum(jnp.abs(_g), 1.0) + (_g == 0) * 1.0
        g_xattn = _g[0]
        g_ffn = _g[1]
        return (x, ctx_2048, mask_BxSx4224_bf0, g_xattn, g_ffn)
    x, ctx_2048, mask_BxSx4224_bf0, g_xattn, g_ffn = _rec_inputs()

    def _L0_xattn_setup():
        import jax, jax.numpy as jnp
        import numpy as np
        from jax import lax
        LN_EPS = 1e-05
        key = jax.random.key(seed)
        ks = jax.random.split(key, 8)
        B, S, T, D = (4, 128, 512, 512)
        scale = 0.02
        return {'Z': jax.random.normal(ks[0], (B, S, D), dtype=jnp.float32), 'kv': jax.random.normal(ks[1], (B, T, D), dtype=jnp.float32), 'decay': jnp.float32(0.9), 'W_in': jax.random.normal(ks[2], (D, D), dtype=jnp.float32) * scale, 'b_in': jnp.zeros((D,), dtype=jnp.float32), 'W_out': jax.random.normal(ks[3], (D, D), dtype=jnp.float32) * scale, 'b_out': jnp.zeros((D,), dtype=jnp.float32), 'gamma': jnp.ones((D,), dtype=jnp.float32), 'beta': jnp.zeros((D,), dtype=jnp.float32)}
    _L0_xattn_all = _L0_xattn_setup()
    _L0_xattn_in = {k: v for k, v in _L0_xattn_all.items() if k in ('decay', 'W_in', 'b_in', 'W_out', 'b_out', 'gamma', 'beta')}
    del _L0_xattn_all

    def _L0_ffn_setup():
        import jax, jax.numpy as jnp
        import numpy as np
        H = 512
        I = 352
        E = 16
        K = 2
        N_SHARED = 2
        IS = I * N_SHARED
        ROUTED_SCALE = 1.0
        CAPACITY = 256

        def _moe_forward(hidden_states, gate_w, w_gate, w_up, w_down, ws_gate, ws_up, ws_down):
            B, S, _ = hidden_states.shape
            x = hidden_states.reshape(-1, H)
            T = x.shape[0]
            logits = jnp.einsum('th,eh->te', x.astype(jnp.float32), gate_w.astype(jnp.float32))
            scores = jax.nn.softmax(logits, axis=-1)
            topk_w, topk_idx = jax.lax.top_k(scores, K)
            topk_w = (topk_w * ROUTED_SCALE).astype(x.dtype)
            flat_idx = topk_idx.reshape(-1)
            order = jnp.argsort(flat_idx)
            sorted_e = flat_idx[order]
            sorted_t = order // K
            counts = jnp.bincount(flat_idx, length=E)
            starts = jnp.cumsum(counts) - counts
            pos = jnp.arange(T * K) - starts[sorted_e]
            buf = jnp.zeros((E, CAPACITY, H), x.dtype).at[sorted_e, pos].set(x[sorted_t], mode='drop')
            g = jax.nn.silu(jnp.einsum('ech,ehi->eci', buf, w_gate))
            u = jnp.einsum('ech,ehi->eci', buf, w_up)
            expert_out = jnp.einsum('eci,eih->ech', g * u, w_down)
            gathered = expert_out[sorted_e, pos]
            out_flat = jnp.zeros((T * K, H), x.dtype).at[order].set(gathered)
            y = (out_flat.reshape(T, K, H) * topk_w[..., None]).sum(axis=1)
            sh = jnp.einsum('ti,ih->th', jax.nn.silu(x @ ws_gate) * (x @ ws_up), ws_down)
            return (y + sh).reshape(B, S, H)
        key = jax.random.key(seed)
        ks = jax.random.split(key, 8)
        B, S = (2, 256)
        scale = 0.02
        return {'hidden_states': jax.random.normal(ks[0], (B, S, H), jnp.float32), 'gate_w': jax.random.normal(ks[1], (E, H), jnp.float32) * scale, 'w_gate': jax.random.normal(ks[2], (E, H, I), jnp.float32) * scale, 'w_up': jax.random.normal(ks[3], (E, H, I), jnp.float32) * scale, 'w_down': jax.random.normal(ks[4], (E, I, H), jnp.float32) * scale, 'ws_gate': jax.random.normal(ks[5], (H, IS), jnp.float32) * scale, 'ws_up': jax.random.normal(ks[6], (H, IS), jnp.float32) * scale, 'ws_down': jax.random.normal(ks[7], (IS, H), jnp.float32) * scale}
    _L0_ffn_all = _L0_ffn_setup()
    _L0_ffn_in = {k: v for k, v in _L0_ffn_all.items() if k in ('gate_w', 'w_gate', 'w_up', 'w_down', 'ws_gate', 'ws_up', 'ws_down')}
    del _L0_ffn_all

    def _L1_xattn_setup():
        import jax, jax.numpy as jnp
        import numpy as np
        import math
        DIM = 512
        B, Q_LEN, KV_LEN = (8, 128, 1024)
        key = jax.random.key(seed)
        ks = jax.random.split(key, 8)
        x = jax.random.normal(ks[0], (B, Q_LEN, DIM), dtype=jnp.float32)
        mask = jnp.zeros((B, Q_LEN, KV_LEN + Q_LEN), dtype=bool)
        k_cache = jax.random.normal(ks[1], (B, KV_LEN, DIM), dtype=jnp.float32)
        v_cache = jax.random.normal(ks[2], (B, KV_LEN, DIM), dtype=jnp.float32)
        scale = 1.0 / math.sqrt(DIM)
        wq = jax.random.normal(ks[3], (DIM, DIM), dtype=jnp.float32) * scale
        wk = jax.random.normal(ks[4], (DIM, DIM), dtype=jnp.float32) * scale
        wv = jax.random.normal(ks[5], (DIM, DIM), dtype=jnp.float32) * scale
        wo = jax.random.normal(ks[6], (DIM, DIM), dtype=jnp.float32) * scale
        return {'x': x, 'mask': mask, 'k_cache': k_cache, 'v_cache': v_cache, 'wq': wq, 'wk': wk, 'wv': wv, 'wo': wo}
    _L1_xattn_all = _L1_xattn_setup()
    _L1_xattn_in = {k: v for k, v in _L1_xattn_all.items() if k in ('wq', 'wk', 'wv', 'wo')}
    del _L1_xattn_all

    def _L1_ffn_setup():
        import jax, jax.numpy as jnp
        import numpy as np
        _FP8_MAX = 448.0
        _BLOCK = 32
        _EPS = 1e-30

        def _mx_dequant(t):
            rows, feat = t.shape
            blocks = t.reshape(rows, feat // _BLOCK, _BLOCK)
            max_abs = jnp.max(jnp.abs(blocks), axis=-1)
            scales = jnp.maximum(max_abs / _FP8_MAX, _EPS)
            q = (blocks / scales[..., None]).astype(jnp.float8_e4m3fn).astype(jnp.float32)
            return (q * scales[..., None]).reshape(rows, feat)

        def _mx_linear(x2d, w):
            return _mx_dequant(x2d) @ _mx_dequant(w).T
        key = jax.random.key(seed)
        k1, k2, k3, k4 = jax.random.split(key, 4)
        B, S, H, I = (2, 256, 512, 2048)
        return {'x': jax.random.normal(k1, (B, S, H), dtype=jnp.float32), 'gate_w': jax.random.normal(k2, (I, H), dtype=jnp.float32) * 0.02, 'up_w': jax.random.normal(k3, (I, H), dtype=jnp.float32) * 0.02, 'down_w': jax.random.normal(k4, (H, I), dtype=jnp.float32) * 0.02}
    _L1_ffn_all = _L1_ffn_setup()
    _L1_ffn_in = {k: v for k, v in _L1_ffn_all.items() if k in ('gate_w', 'up_w', 'down_w')}
    del _L1_ffn_all
    return {'x': x, 'ctx_2048': ctx_2048, 'mask_BxSx4224_bf0': mask_BxSx4224_bf0, 'g_xattn': g_xattn, 'g_ffn': g_ffn, 'L0_xattn_decay': _L0_xattn_in['decay'], 'L0_xattn_W_in': _L0_xattn_in['W_in'], 'L0_xattn_b_in': _L0_xattn_in['b_in'], 'L0_xattn_W_out': _L0_xattn_in['W_out'], 'L0_xattn_b_out': _L0_xattn_in['b_out'], 'L0_xattn_gamma': _L0_xattn_in['gamma'], 'L0_xattn_beta': _L0_xattn_in['beta'], 'L0_ffn_gate_w': _L0_ffn_in['gate_w'], 'L0_ffn_w_gate': _L0_ffn_in['w_gate'], 'L0_ffn_w_up': _L0_ffn_in['w_up'], 'L0_ffn_w_down': _L0_ffn_in['w_down'], 'L0_ffn_ws_gate': _L0_ffn_in['ws_gate'], 'L0_ffn_ws_up': _L0_ffn_in['ws_up'], 'L0_ffn_ws_down': _L0_ffn_in['ws_down'], 'L1_xattn_wq': _L1_xattn_in['wq'], 'L1_xattn_wk': _L1_xattn_in['wk'], 'L1_xattn_wv': _L1_xattn_in['wv'], 'L1_xattn_wo': _L1_xattn_in['wo'], 'L1_ffn_gate_w': _L1_ffn_in['gate_w'], 'L1_ffn_up_w': _L1_ffn_in['up_w'], 'L1_ffn_down_w': _L1_ffn_in['down_w']}

def reference(x, ctx_2048, mask_BxSx4224_bf0, g_xattn, g_ffn, L0_xattn_decay, L0_xattn_W_in, L0_xattn_b_in, L0_xattn_W_out, L0_xattn_b_out, L0_xattn_gamma, L0_xattn_beta, L0_ffn_gate_w, L0_ffn_w_gate, L0_ffn_w_up, L0_ffn_w_down, L0_ffn_ws_gate, L0_ffn_ws_up, L0_ffn_ws_down, L1_xattn_wq, L1_xattn_wk, L1_xattn_wv, L1_xattn_wo, L1_ffn_gate_w, L1_ffn_up_w, L1_ffn_down_w):
    import jax
    import jax.numpy as jnp

    def _L0_xattn_ref(Z, kv, decay, W_in, b_in, W_out, b_out, gamma, beta):
        import jax, jax.numpy as jnp
        import numpy as np
        from jax import lax
        LN_EPS = 1e-05
        B, T, D = kv.shape
        K = jax.nn.sigmoid(decay)
        x = jnp.einsum('btd,ed->bte', kv, W_in) + b_in

        def scan_fn(s, xt):
            s = K * s + xt
            return (s, s)
        s0 = jnp.zeros((B, D), dtype=kv.dtype)
        _, states = lax.scan(scan_fn, s0, jnp.swapaxes(x, 0, 1))
        states = jnp.swapaxes(states, 0, 1)
        proj = jnp.einsum('btd,ed->bte', states, W_out) + b_out
        summary = jnp.mean(proj, axis=1, keepdims=True)
        y = Z + summary
        mu = jnp.mean(y, axis=-1, keepdims=True)
        var = jnp.mean((y - mu) ** 2, axis=-1, keepdims=True)
        return (y - mu) / jnp.sqrt(var + LN_EPS) * gamma + beta

    def _L0_ffn_ref(hidden_states, gate_w, w_gate, w_up, w_down, ws_gate, ws_up, ws_down):
        import jax, jax.numpy as jnp
        import numpy as np
        H = 512
        I = 352
        E = 16
        K = 2
        N_SHARED = 2
        IS = I * N_SHARED
        ROUTED_SCALE = 1.0
        CAPACITY = 256

        def _moe_forward(hidden_states, gate_w, w_gate, w_up, w_down, ws_gate, ws_up, ws_down):
            B, S, _ = hidden_states.shape
            x = hidden_states.reshape(-1, H)
            T = x.shape[0]
            logits = jnp.einsum('th,eh->te', x.astype(jnp.float32), gate_w.astype(jnp.float32))
            scores = jax.nn.softmax(logits, axis=-1)
            topk_w, topk_idx = jax.lax.top_k(scores, K)
            topk_w = (topk_w * ROUTED_SCALE).astype(x.dtype)
            flat_idx = topk_idx.reshape(-1)
            order = jnp.argsort(flat_idx)
            sorted_e = flat_idx[order]
            sorted_t = order // K
            counts = jnp.bincount(flat_idx, length=E)
            starts = jnp.cumsum(counts) - counts
            pos = jnp.arange(T * K) - starts[sorted_e]
            buf = jnp.zeros((E, CAPACITY, H), x.dtype).at[sorted_e, pos].set(x[sorted_t], mode='drop')
            g = jax.nn.silu(jnp.einsum('ech,ehi->eci', buf, w_gate))
            u = jnp.einsum('ech,ehi->eci', buf, w_up)
            expert_out = jnp.einsum('eci,eih->ech', g * u, w_down)
            gathered = expert_out[sorted_e, pos]
            out_flat = jnp.zeros((T * K, H), x.dtype).at[order].set(gathered)
            y = (out_flat.reshape(T, K, H) * topk_w[..., None]).sum(axis=1)
            sh = jnp.einsum('ti,ih->th', jax.nn.silu(x @ ws_gate) * (x @ ws_up), ws_down)
            return (y + sh).reshape(B, S, H)
        return _moe_forward(hidden_states, gate_w, w_gate, w_up, w_down, ws_gate, ws_up, ws_down)

    def _L1_xattn_ref(x, mask, k_cache, v_cache, wq, wk, wv, wo):
        import jax, jax.numpy as jnp
        import numpy as np
        import math
        DIM = 512
        B, Q_LEN, KV_LEN = (8, 128, 1024)
        q = jnp.einsum('bsd,ed->bse', x, wq)
        k_new = jnp.einsum('bsd,ed->bse', x, wk)
        v_new = jnp.einsum('bsd,ed->bse', x, wv)
        k = jnp.concatenate([k_cache, k_new], axis=1)
        v = jnp.concatenate([v_cache, v_new], axis=1)
        scale = 1.0 / math.sqrt(q.shape[-1])
        scores = jnp.einsum('bqd,bkd->bqk', q, k) * scale
        attn = jax.nn.softmax(scores, axis=-1)
        out = jnp.einsum('bqk,bkd->bqd', attn, v)
        return jnp.einsum('bqd,ed->bqe', out, wo)

    def _L1_ffn_ref(x, gate_w, up_w, down_w):
        import jax, jax.numpy as jnp
        import numpy as np
        _FP8_MAX = 448.0
        _BLOCK = 32
        _EPS = 1e-30

        def _mx_dequant(t):
            rows, feat = t.shape
            blocks = t.reshape(rows, feat // _BLOCK, _BLOCK)
            max_abs = jnp.max(jnp.abs(blocks), axis=-1)
            scales = jnp.maximum(max_abs / _FP8_MAX, _EPS)
            q = (blocks / scales[..., None]).astype(jnp.float8_e4m3fn).astype(jnp.float32)
            return (q * scales[..., None]).reshape(rows, feat)

        def _mx_linear(x2d, w):
            return _mx_dequant(x2d) @ _mx_dequant(w).T
        B, S, H = x.shape
        x2d = x.reshape(B * S, H)
        gate = _mx_linear(x2d, gate_w)
        up = _mx_linear(x2d, up_w)
        h = jax.nn.silu(gate) * up
        out = _mx_linear(h, down_w)
        return out.reshape(B, S, H)
    x = x + jnp.tanh(g_xattn[0]) * _L0_xattn_ref(_layernorm(x, axis=-1), ctx_2048, L0_xattn_decay, L0_xattn_W_in, L0_xattn_b_in, L0_xattn_W_out, L0_xattn_b_out, L0_xattn_gamma, L0_xattn_beta)
    x = x + jnp.tanh(g_ffn[0]) * _L0_ffn_ref(_layernorm(x, axis=-1), L0_ffn_gate_w, L0_ffn_w_gate, L0_ffn_w_up, L0_ffn_w_down, L0_ffn_ws_gate, L0_ffn_ws_up, L0_ffn_ws_down)
    x = x + jnp.tanh(g_xattn[1]) * _L1_xattn_ref(_layernorm(x, axis=-1), mask_BxSx4224_bf0, ctx_2048, ctx_2048, L1_xattn_wq, L1_xattn_wk, L1_xattn_wv, L1_xattn_wo)
    x = x + jnp.tanh(g_ffn[1]) * _L1_ffn_ref(_layernorm(x, axis=-1), L1_ffn_gate_w, L1_ffn_up_w, L1_ffn_down_w)
    return x

_drawn_inputs = setup_inputs


def setup_inputs(seed=0):
    import zlib

    import numpy as np

    out = dict(_drawn_inputs(seed))
    spreads = {'g_ffn': (-1.0, 0.6),
     'L0_xattn_b_in': (0.0, 0.1),
     'L0_xattn_b_out': (0.0, 0.1),
     'L0_xattn_gamma': (1.0, 0.2),
     'L0_xattn_beta': (0.0, 0.1)}
    factors = {'L0_ffn_gate_w': 8.0,
     'L0_ffn_w_gate': 8.0,
     'L0_ffn_w_up': 8.0,
     'L0_ffn_w_down': 8.0,
     'L0_ffn_ws_gate': 8.0,
     'L0_ffn_ws_up': 8.0,
     'L0_ffn_ws_down': 8.0,
     'L1_xattn_wq': 5.312,
     'L1_xattn_wk': 8.0,
     'L1_xattn_wv': 8.0,
     'L1_ffn_gate_w': 8.0,
     'L1_ffn_up_w': 8.0,
     'L1_ffn_down_w': 8.0}
    for name, (base, spread) in spreads.items():
        noise = np.random.default_rng([zlib.crc32(name.encode()), seed]).standard_normal(out[name].shape)
        drawn = base * np.exp(spread * noise) if base else spread * noise
        out[name] = jnp.asarray(drawn.astype(out[name].dtype))
    for name, factor in factors.items():
        out[name] = (out[name] * factor).astype(out[name].dtype)
    return out
```

```python
from contextlib import ExitStack

import concourse.bass as bass
from concourse import mybir

F32 = mybir.dt.float32
BF16 = mybir.dt.bfloat16
U32 = mybir.dt.uint32
I32 = mybir.dt.int32
ALU = mybir.AluOpType
ACT = mybir.ActivationFunctionType
AX = mybir.AxisListType

P = 128
B, S, D = 32, 100, 512
TOK = B * S
NT = TOK // P
DC = D // P
CTX = 361
CT = [(0, 128), (128, 128), (256, CTX - 256)]
LAST = CTX - 256
E, I, CAP = 16, 352, 256
IC = [(0, 128), (128, 128), (256, I - 256)]
IS = 704
SC = [(128 * m, min(128, IS - 128 * m)) for m in range(6)]
F = 2048
GT = 5
NG = NT // GT
LN_EPS = 1e-5
FP8_MAX, MX_EPS, MXB = 448.0, 1e-30, 32
HI, LO = 0, 1
PAIRS = [(HI, HI), (HI, LO), (LO, HI)]


class Steps:

    def __init__(self, eng, sem):
        self.eng, self.sem, self.n, self.base = eng, sem, 0, 0

    def did(self, ins):
        ins.then_inc(self.sem, 1)
        self.n += 1

    def settle(self, alone=False):
        self.eng.wait_ge(self.sem, self.base + self.n)
        if alone:
            apart(self.eng)


def apart(eng):
    eng.nop(nofuse=True)


def repeat(eng, steps, count, body, unroll=1, tail=0):
    for t in range(unroll):
        n0 = steps.n
        body(t, t)
        per = steps.n - n0
    end = unroll + (count - unroll - tail) // unroll * unroll
    if end > unroll:
        n1 = steps.n
        with eng.Fori(unroll, end - unroll + 1, unroll) as t:
            steps.base = (t - unroll) * per
            for k in range(unroll):
                body(t + k if k else t, k)
        steps.base, steps.n = 0, n1 + (end - unroll) * per
    for t in range(end, count):
        body(t, t % unroll)


def later(t, n):
    return not isinstance(t, int) or t >= n


def wide(ap, n):
    return ap.unsqueeze(2).to_broadcast([ap.shape[0], ap.shape[1], n])


def blocks(ap, n=MXB):
    return ap.rearrange("p (b n) -> p b n", n=n)


def mx_scales(dve, st, src, amax, scale, inv):
    st.did(dve.tensor_reduce(amax, blocks(src), axis=AX.X, op=ALU.max, apply_absolute_value=True))
    st.settle()
    st.did(dve.tensor_scalar(scale, amax, 1.0 / FP8_MAX, MX_EPS, ALU.mult, ALU.max))
    st.settle()
    st.did(dve.reciprocal(inv, scale))
    st.settle()


def mx_round(dve, st, src, inv, r, m):
    st.did(dve.tensor_tensor(blocks(r), blocks(src), wide(inv, MXB), ALU.mult))
    st.settle()
    st.did(dve.tensor_scalar(m.bitcast(U32), r.bitcast(U32), 0x7F800000, 0xFFFFFFFF,
                             ALU.bitwise_and, ALU.bitwise_and))
    st.settle()
    st.did(dve.tensor_scalar(m, m, 2.0 ** -6, 1.5 * 2.0 ** 20, ALU.max, ALU.mult))
    st.settle()
    st.did(dve.tensor_tensor(r, r, m, ALU.add))
    st.settle()


def program(nc, x, ctx, g_xattn, g_ffn, decay, W_in, b_in, W_out, b_out, gamma, beta,
            gate_w, w_gate, w_up, w_down, ws_gate, ws_up, ws_down,
            wq, wk, wv, wo, gate2, up2, down2, out):
    x1_d = nc.dram_tensor("x1_d", (TOK, D), F32, kind="Internal").ap()
    x2_d = nc.dram_tensor("x2_d", (TOK, D), F32, kind="Internal").ap()
    x3_d = nc.dram_tensor("x3_d", (TOK, D), F32, kind="Internal").ap()
    xT_d = nc.dram_tensor("xT_d", (NT * P, 2 * D), BF16, kind="Internal").ap()
    slots_d = nc.dram_tensor("slots_d", (E * CAP, 2 * D), BF16, kind="Internal").ap()
    eout_d = nc.dram_tensor("eout_d", (E * CAP, D), F32, kind="Internal").ap()
    x_f = x.rearrange("b s d -> (b s) d")
    out_f = out.rearrange("b s d -> (b s) d")
    with ExitStack() as keep:
        def sb(name, shape, dt=F32):
            return keep.enter_context(nc.sbuf_tensor(name, shape, dt))

        g = {}
        g["ident"] = sb("ident", [P, P])
        g["identb"] = sb("identb", [P, P], BF16)
        g["gains"] = sb("gains", [P, 4])
        g["gateT"] = sb("gateT", [P, 2, DC, F], BF16)
        g["upT"] = sb("upT", [P, 2, DC, F], BF16)
        g["downT"] = sb("downT", [P, 2, 16, DC, P], BF16)
        g["bank"] = [keep.enter_context(nc.psum_tensor(f"bank{i}", [P, 512], F32)) for i in range(8)]
        with ExitStack() as first:
            def sbf(name, shape, dt=F32):
                return first.enter_context(nc.sbuf_tensor(name, shape, dt))
            g["gidx"] = sbf("gidx", [P, NT, 2], U32)
            g["topw"] = sbf("topw", [P, NT, 2])
            with ExitStack() as l0:
                g["summary"] = l0.enter_context(nc.sbuf_tensor("summary", [B, 3, D], BF16))
                with nc.cleanup_on_exit():
                    summary_phase(nc, g, ctx, g_xattn, g_ffn, decay, W_in, b_in, W_out, b_out,
                                  gate2, up2, down2, slots_d)
                with nc.cleanup_on_exit():
                    route_phase(nc, g, x_f, gamma, beta, gate_w, x1_d, xT_d, slots_d)
            with nc.cleanup_on_exit():
                expert_phase(nc, g, w_gate, w_up, w_down, slots_d, eout_d)
            with nc.cleanup_on_exit():
                shared_phase(nc, g, ws_gate, ws_up, ws_down, xT_d, eout_d, x1_d, x2_d)
        with nc.cleanup_on_exit():
            attention_phase(nc, g, ctx, wq, wk, wv, wo, x2_d, x3_d)
        with nc.cleanup_on_exit():
            mx_phase(nc, g, x3_d, out_f)


def summary_phase(nc, g, ctx, g_xattn, g_ffn, decay, W_in, b_in, W_out, b_out,
                  gate2, up2, down2, slots_d):
    ident, identb, gains, bank = g["ident"], g["identb"], g["gains"], g["bank"]
    summary = g["summary"]
    WIN = 2 * P - 1
    with ExitStack() as es:
        def sb(name, shape, dt=F32):
            return es.enter_context(nc.sbuf_tensor(name, shape, dt))

        def sem(name):
            return nc.alloc_semaphore(f"summary_{name}")

        crow = [sb(f"crow{k}", [P, 3, D]) for k in range(2)]
        chl = [sb(f"chl{k}", [P, 2, 3, D], BF16) for k in range(2)]
        window = sb("window", [P, 2, 3, WIN], BF16)
        wrow = sb("wrow", [P, CTX])
        kcol = sb("kcol", [P, 2])
        krow = sb("krow", [P, CTX])
        diag = sb("diag", [P, 3, CTX])
        picked = sb("picked", [P, CTX])
        wsum = sb("wsum", [P, 4])
        wstage = sb("wstage", [P, 3, D])
        wr, wm = sb("wr", [P, 3, D]), sb("wm", [P, 3, D])
        dq = sb("dq", [P, 3, D])
        amax, scale, inv = (sb(n, [P, 48]) for n in ("amax", "scale", "inv"))
        zeros = sb("zeros", [P, 2 * D], BF16)
        bias2 = sb("bias2", [B, 2, D])
        WT = [sb(f"WT{k}", [P, DC, D]) for k in range(2)]
        sumrow = sb("sumrow", [B, 3, D])
        sumT = sb("sumT", [P, DC, B])
        left = sb("left", [B, D])
        slots_zero, gains_in, bias_in, sq_in = sem("slots_zero"), sem("gains_in"), sem("bias_in"), sem("sq_in")
        row_a = [sem(f"row_a{k}") for k in range(2)]
        wst_in = sem("wst_in")
        pool_c, dve_c, act_tanh = sem("pool_c"), sem("dve_c"), sem("act_tanh")
        zero_set = sem("zero_set")
        win_ready = sem("win_ready")
        row_hi, row_lo, row_mm = sem("row_hi"), sem("row_lo"), sem("row_mm")
        round_done, dq_done, wT_ps, wT_hi, wT_lo = (sem(n) for n in (
            "round_done", "dq_done", "wT_ps", "wT_hi", "wT_lo"))
        sq_ps, sq_ev, fin_ps, fin_act, fin_dve = (sem(n) for n in (
            "sq_ps", "sq_ev", "fin_ps", "fin_act", "fin_dve"))
        sqs = [crow[0], crow[1]]
        downv = down2.rearrange("(p r) (a n) -> p (r a) n", r=4, n=D)
        with nc.Block() as block:
            @block.sync
            def _(sp):
                for n, src in enumerate((g_xattn, g_ffn)):
                    sp.dma_start(gains[:, 2 * n:2 * n + 2],
                                 src.rearrange("(a n) -> a n", a=1).to_broadcast([P, 2])).then_inc(gains_in, 16)
                sp.dma_start(kcol[:, 0:1],
                             decay.rearrange("(a n) -> a n", a=1).to_broadcast([P, 1])).then_inc(gains_in, 16)
                for n, src in enumerate((b_in, b_out)):
                    sp.dma_start(bias2[:, n, :],
                                 src.rearrange("(a n) -> a n", a=1).to_broadcast([B, D])).then_inc(bias_in, 16)
                for n, src in enumerate((W_in, W_out)):
                    sp.dma_start(sqs[n][:, :, :],
                                 src[0:384, :].rearrange("(c p) n -> p c n", p=P)).then_inc(sq_in, 16)
                    sp.dma_start(dq[:, n, :], src[384:512, :]).then_inc(sq_in, 16)
                sp.wait_ge(zero_set, 1)
                for n in range(4):
                    sp.dma_start(slots_d[n * 1024:(n + 1) * 1024, :].rearrange("(a p) n -> p a n", p=P),
                                 zeros[:, :].unsqueeze(1).to_broadcast([P, 8, 2 * D])).then_inc(slots_zero, 16)
                sp.wait_ge(sq_ps, 8)

                def load(t, _):
                    if later(t, 1):
                        sp.wait_ge(round_done, t)
                    sp.dma_start(wstage[:, 0, :], gate2[bass.ds(t * P, P), :]).then_inc(wst_in, 16)
                    sp.dma_start(wstage[:, 1, :], up2[bass.ds(t * P, P), :]).then_inc(wst_in, 16)
                    sp.dma_start(wstage[:, 2, :], downv[:, bass.ds(t, 1), :].rearrange("p a n -> p (a n)")
                                 ).then_inc(wst_in, 16)
                    for k in range(2):
                        b = 2 * t + k
                        if later(t, 1):
                            sp.wait_ge(row_hi, 2 * t - 1 + k)
                            sp.wait_ge(row_lo, 2 * t - 1 + k)
                        row = ctx[bass.ds(b, 1), :, :].rearrange("a t d -> (a t) d")
                        sp.dma_start(crow[k][:, 0:2, :],
                                     row[0:256, :].rearrange("(c p) d -> p c d", p=P)).then_inc(row_a[k], 16)
                        sp.dma_start(crow[k][0:LAST, 2, :], row[256:CTX, :]).then_inc(row_a[k], 16)
                repeat(sp, Steps(sp, None), 16, load)
                sp.wait_ge(slots_zero, 64)

            @block.gpsimd
            def _(pool):
                st = Steps(pool, pool_c)
                st.did(pool.memset(zeros[:, :], 0.0))
                st.did(pool.memset(ident[:, :], 0.0))
                st.did(pool.memset(diag[:, :, :], 0.0))
                st.did(pool.memset(window[:, :, :, :], 0.0))
                st.settle()
                pool.affine_select(out=ident[:, :], in_=ident[:, :], compare_op=ALU.not_equal, fill=1.0,
                                   base=0, pattern=[[-1, P]], channel_multiplier=1).then_inc(zero_set, 1)
                pool.affine_select(out=diag[:, :, :], in_=diag[:, :, :], compare_op=ALU.not_equal, fill=1.0,
                                   base=1 - CTX, pattern=[[P, 3], [1, CTX]], channel_multiplier=1
                                   ).then_inc(zero_set, 1)
                pool.wait_ge(zero_set, 2)
                pool.tensor_copy(identb[:, :], ident[:, :]).then_inc(zero_set, 1)

                def part(t, _):
                    for k in range(2):
                        pool.wait_ge(row_hi, 2 * t + k + 1)
                        if later(t, 1):
                            pool.wait_ge(row_mm, 2 * t - 1 + k)
                        pool.tensor_tensor(chl[k][:, LO, 0:2, :], crow[k][:, 0:2, :], chl[k][:, HI, 0:2, :],
                                           ALU.subtract)
                        pool.tensor_tensor(chl[k][0:LAST, LO, 2, :], crow[k][0:LAST, 2, :],
                                           chl[k][0:LAST, HI, 2, :], ALU.subtract).then_inc(row_lo, 1)
                    pool.wait_ge(round_done, t + 1)
                    if later(t, 1):
                        pool.wait_ge(wT_ps, 3 * t)
                    pool.tensor_tensor(blocks(dq[:, :, :].rearrange("p a n -> p (a n)")),
                                       blocks(wr[:, :, :].rearrange("p a n -> p (a n)")),
                                       wide(scale[:, :], MXB), ALU.mult).then_inc(dq_done, 1)
                pool.wait_ge(sq_ps, 8)
                repeat(pool, Steps(pool, None), 16, part)

            @block.scalar
            def _(act):
                act.wait_ge(gains_in, 48)
                act.activation(gains[:, :], gains[:, :], ACT.Tanh).then_inc(act_tanh, 1)
                act.activation(kcol[:, 1:2], kcol[:, 0:1], ACT.Tanh, scale=0.5).then_inc(act_tanh, 1)
                for n in range(8):
                    act.wait_ge(sq_ps, n + 1)
                    act.activation(WT[n // 4][:, n % 4, :], bank[n % 4][:, :], ACT.Copy).then_inc(sq_ev, 1)

                def part(t, _):
                    for k in range(2):
                        act.wait_ge(row_a[k], t * 32 + 32)
                        if later(t, 1):
                            act.wait_ge(row_mm, 2 * t - 1 + k)
                        act.activation(chl[k][:, HI, 0:2, :], crow[k][:, 0:2, :], ACT.Copy)
                        act.activation(chl[k][0:LAST, HI, 2, :], crow[k][0:LAST, 2, :], ACT.Copy
                                       ).then_inc(row_hi, 1)
                    for n in range(3):
                        act.wait_ge(wT_ps, 3 * t + n + 1)
                        src = bank[1 + n][:, :].rearrange("p (c i) -> p c i", c=DC)
                        if n < 2:
                            dst = (g["gateT"], g["upT"])[n][:, HI, :, bass.ds(t * P, P)]
                        else:
                            dst = g["downT"][:, HI, bass.ds(t, 1), :, :].rearrange("p a c i -> p (a c) i")
                        act.activation(dst, src, ACT.Copy).then_inc(wT_hi, 1)
                repeat(act, Steps(act, None), 16, part)
                act.wait_ge(row_mm, B)
                act.activation(sumrow[:, 0, :], bank[0][0:B, :], ACT.Copy).then_inc(fin_act, 1)
                for n in range(2):
                    act.wait_ge(fin_ps, 1 + 2 * n)
                    act.activation(sumT[:, :, :], bank[4 + n][:, 0:DC * B].rearrange("p (c b) -> p c b", c=DC),
                                   ACT.Copy).then_inc(fin_act, 1)

            @block.vector
            def _(dve):
                st = Steps(dve, dve_c)
                st.did(dve.memset(krow[:, :], 1.0))
                dve.wait_ge(act_tanh, 2)
                st.did(dve.tensor_scalar(kcol[:, 0:1], kcol[:, 1:2], 0.5, 0.5, ALU.mult, ALU.add))
                st.settle()
                st.did(dve.tensor_scalar(picked[:, :], krow[:, :], kcol[:, 0:1], None, ALU.mult))
                st.settle()
                st.did(dve.tensor_tensor_scan(wrow[:, :], picked[:, :], krow[:, :], 0.0, ALU.mult, ALU.add))
                st.settle()
                st.did(dve.tensor_scalar(wrow[:, :], wrow[:, :], 1.0 / CTX, None, ALU.mult))
                st.settle()
                dve.wait_ge(zero_set, 2)
                for c in range(3):
                    st.did(dve.tensor_tensor(picked[:, :], wrow[:, :], diag[:, c, :], ALU.mult))
                    st.settle()
                    st.did(dve.tensor_reduce(wsum[:, c:c + 1], picked[:, :], axis=AX.X, op=ALU.add))
                    st.settle()
                st.did(dve.tensor_reduce(wsum[:, 3:4], wrow[:, :], axis=AX.X, op=ALU.add))
                st.did(dve.tensor_copy(window[:, HI, :, P - 1], wsum[:, 0:3]))
                st.settle()
                dve.tensor_tensor(window[:, LO, :, P - 1], wsum[:, 0:3], window[:, HI, :, P - 1],
                                  ALU.subtract).then_inc(win_ready, 1)

                def part(t, _):
                    dve.wait_ge(wst_in, t * 48 + 48)
                    if later(t, 1):
                        dve.wait_ge(dq_done, t)
                    flat = wstage[:, :, :].rearrange("p a n -> p (a n)")
                    r, m = (v[:, :, :].rearrange("p a n -> p (a n)") for v in (wr, wm))
                    mx_scales(dve, st, flat, amax[:, :], scale[:, :], inv[:, :])
                    mx_round(dve, st, flat, inv[:, :], r, m)
                    dve.tensor_tensor(r, r, m, ALU.subtract).then_inc(round_done, 1)
                    for n in range(3):
                        dve.wait_ge(wT_hi, 3 * t + n + 1)
                        src = bank[1 + n][:, :].rearrange("p (c i) -> p c i", c=DC)
                        if n < 2:
                            w = (g["gateT"], g["upT"])[n]
                            hi, lo = (w[:, h, :, bass.ds(t * P, P)] for h in (HI, LO))
                        else:
                            hi, lo = (g["downT"][:, h, bass.ds(t, 1), :, :].rearrange("p a c i -> p (a c) i")
                                      for h in (HI, LO))
                        dve.tensor_tensor(lo, src, hi, ALU.subtract).then_inc(wT_lo, 1)
                repeat(dve, st, 16, part)
                dve.wait_ge(bias_in, 32)
                st.did(dve.tensor_scalar(bias2[:, 0, :], bias2[:, 0, :], wsum[0:B, 3:4], None, ALU.mult))
                st.settle()
                for n in range(2):
                    dve.wait_ge(fin_ps, 2 + 2 * n)
                    dve.tensor_tensor(sumrow[:, 1 + n, :], bank[6 + n][0:B, :], bias2[:, n, :],
                                      ALU.add).then_inc(fin_dve, 1)
                dve.wait_ge(fin_dve, 2)
                st.did(dve.tensor_copy(summary[:, 0, :], sumrow[:, 2, :]))
                st.settle()
                st.did(dve.tensor_tensor(left[:, :], sumrow[:, 2, :], summary[:, 0, :], ALU.subtract))
                st.settle()
                st.did(dve.tensor_copy(summary[:, 1, :], left[:, :]))
                st.settle()
                st.did(dve.tensor_tensor(summary[:, 2, :], left[:, :], summary[:, 1, :], ALU.subtract))

            @block.tensor
            def _(pe):
                pe.wait_ge(sq_in, 64)
                pe.wait_ge(zero_set, 1)
                for n in range(2):
                    for c in range(DC):
                        if n:
                            pe.wait_ge(sq_ev, c + 1)
                        for r in range(DC):
                            rows = sqs[n][:, r, :] if r < 3 else dq[:, n, :]
                            ins = pe.transpose(bank[c][:, r * P:(r + 1) * P], rows[:, c * P:(c + 1) * P],
                                               ident[:, :])
                        ins.then_inc(sq_ps, 1)
                pe.wait_ge(sq_ev, 8)
                pe.wait_ge(win_ready, 1)

                def part(t, _, last=False):
                    for k in range(2):
                        pe.wait_ge(row_hi, 2 * t + k + 1)
                        pe.wait_ge(row_lo, 2 * t + k + 1)
                        n = 0
                        for c, (_, rows) in enumerate(CT):
                            for a, w in PAIRS:
                                at = t * -2 + (P - 1 - k)
                                ins = pe.matmul(bank[0][:, :], window[0:rows, w, c, bass.ds(at, P)],
                                                chl[k][0:rows, a, c, :],
                                                start=isinstance(t, int) and t == 0 and k == 0 and n == 0,
                                                stop=isinstance(t, int) and t == 15 and k == 1 and n == 8,
                                                skip_group_check=True)
                                n += 1
                        ins.then_inc(row_mm, 1)
                    pe.wait_ge(dq_done, t + 1)
                    for n in range(3):
                        if later(t, 1):
                            pe.wait_ge(wT_lo, 3 * t - 2 + n)
                        for c in range(DC):
                            ins = pe.transpose(bank[1 + n][:, c * P:(c + 1) * P], dq[:, n, c * P:(c + 1) * P],
                                               ident[:, :])
                        ins.then_inc(wT_ps, 1)
                repeat(pe, Steps(pe, None), 16, part, tail=1)
                for n in range(2):
                    if n == 0:
                        pe.wait_ge(fin_act, 1)
                    else:
                        pe.wait_ge(fin_dve, 1)
                    for c in range(DC):
                        ins = pe.transpose(bank[4 + n][:, c * B:(c + 1) * B], sumrow[:, n, c * P:(c + 1) * P],
                                           ident[0:B, 0:B])
                    ins.then_inc(fin_ps, 1)
                    pe.wait_ge(fin_act, 2 + n)
                    for c in range(DC):
                        ins = pe.matmul(bank[6 + n][0:B, :], sumT[:, c, :], WT[n][:, c, :],
                                        start=c == 0, stop=c == DC - 1)
                    ins.then_inc(fin_ps, 1)


def row_stats(dve, st, src, stats, mv, count, done=None):
    for j in range(count):
        st.did(dve.bn_stats(stats[:, j, :], src(j)))
    st.settle(alone=True)
    for j in range(count - 1):
        st.did(dve.bn_aggr(mv[:, j, :], stats[:, j, :]))
    dve.bn_aggr(mv[:, count - 1, :], stats[:, count - 1, :]).then_inc(done, 1)


def rsqrt(pool, st, rstd, mv, power, done):
    st.did(pool.tensor_scalar(rstd, mv, LN_EPS, None, ALU.add))
    st.settle()
    pool.tensor_tensor(rstd, rstd, power, ALU.pow).then_inc(done, 1)


def route_phase(nc, g, x_f, gamma, beta, gate_w, x1_d, xT_d, slots_d):
    ident, gains, bank, summary = g["ident"], g["gains"], g["bank"], g["summary"]
    gidx, topw = g["gidx"], g["topw"]
    with ExitStack() as es:
        def sb(name, shape, dt=F32):
            return es.enter_context(nc.sbuf_tensor(name, shape, dt))

        def sem(name):
            return nc.alloc_semaphore(f"route_{name}")

        xt, y, xb = sb("xt", [P, GT, D]), sb("y", [P, GT, D]), sb("xb", [P, GT, D])
        x1, xn = sb("x1", [P, GT, D]), sb("xn", [P, GT, D])
        rows = sb("rows", [P, GT, 2, D], BF16)
        xT = sb("xT", [P, GT, 2, DC, P], BF16)
        gamma_b, beta_b = sb("gamma_b", [P, D]), sb("beta_b", [P, D])
        own = sb("own", [B, TOK], BF16)
        before, ones = sb("before", [P, P], BF16), sb("ones", [P, P], BF16)
        iota_i, iota_f = sb("iota_i", [P, E], I32), sb("iota_f", [P, E])
        gw = sb("gw", [E, D])
        gwT = sb("gwT", [P, 2, DC, E], BF16)
        stats, mv = sb("stats", [P, GT, 6]), sb("mv", [P, GT, 2])
        rstd, power = sb("rstd", [P, GT]), sb("power", [P, GT])
        nmax, esum, rsum = sb("nmax", [P, GT]), sb("esum", [P, GT]), sb("rsum", [P, GT])
        probs = sb("probs", [P, GT, E])
        top8, top8i = sb("top8", [P, GT, 8]), sb("top8i", [P, GT, 8], U32)
        chosen = sb("chosen", [P, GT * 2])
        hot, hit = sb("hot", [P, GT * 2, E]), sb("hit", [P, GT * 2, E])
        picks = sb("picks", [P, GT, E], BF16)
        counts = sb("counts", [P, GT + 1, E], BF16)
        pos, slot, over = sb("pos", [P, GT * 2]), sb("slot", [P, GT * 2]), sb("over", [P, GT * 2])
        sidx = sb("sidx", [P, GT * 2], U32)
        x_in, gb_in = sem("x_in"), sem("gb_in")
        made, pool_c, dve_c = sem("made"), sem("pool_c"), sem("dve_c2")
        gw_ps, gw_hi = sem("gw_ps"), sem("gw_hi")
        stat_done, rstd_done, xb_done = sem("stat_done"), sem("rstd_done"), sem("xb_done")
        own_ps, x1_done, xn_done = sem("own_ps"), sem("x1_done"), sem("xn_done")
        rows_hi, rows_lo, scattered = sem("rows_hi"), sem("rows_lo"), sem("scattered")
        xT_ps, xT_hi, xT_lo = sem("xT_ps"), sem("xT_hi"), sem("xT_lo")
        x1_out, xT_out = sem("x1_out"), sem("xT_out")
        logit_ps, nmax_done, exp_done = sem("logit_ps"), sem("nmax_done"), sem("exp_done")
        picks_done, rank_ps, sidx_done, y_read = sem("picks_done"), sem("rank_ps"), sem("sidx_done"), sem("y_read")
        rowsof = x_f.rearrange("(t p) d -> p t d", p=P)
        x1of = x1_d.rearrange("(t p) d -> p t d", p=P)
        xTof = xT_d.rearrange("(t p) d -> p t d", p=P)
        with nc.Block() as block:
            @block.sync
            def _(sp):
                for dst, src in ((gamma_b, gamma), (beta_b, beta)):
                    sp.dma_start(dst[:, :], src.rearrange("(a n) -> a n", a=1).to_broadcast([P, D])
                                 ).then_inc(gb_in, 16)
                sp.dma_start(gw[:, :], gate_w).then_inc(gb_in, 16)
                sp.dma_start(xt[:, :, :], rowsof[:, 0:GT, :]).then_inc(x_in, 16)

                def part(t, _):
                    sp.wait_ge(x1_done, t + 1)
                    sp.dma_start(x1of[:, bass.ds(t * GT, GT), :], x1[:, :, :]).then_inc(x1_out, 16)
                    if not (isinstance(t, int) and t == NG - 1):
                        sp.dma_start(xt[:, :, :], rowsof[:, bass.ds(t * GT + GT, GT), :]).then_inc(x_in, 16)
                    sp.wait_ge(xT_hi, t * GT + GT)
                    sp.wait_ge(xT_lo, t * GT + GT)
                    sp.dma_start(xTof[:, bass.ds(t * GT, GT), :],
                                 xT[:, :, :, :, :].rearrange("p t h c q -> p t (h c q)")).then_inc(xT_out, 16)
                repeat(sp, Steps(sp, None), NG, part, tail=1)
                sp.wait_ge(x1_out, NG * 16)
                sp.wait_ge(xT_out, NG * 16)

            @block.gpsimd
            def _(pool):
                st = Steps(pool, pool_c)
                st.did(pool.memset(power[:, :], -0.5))
                st.did(pool.memset(own[:, :], 1.0))
                st.did(pool.memset(before[:, :], 1.0))
                st.did(pool.memset(ones[:, :], 1.0))
                st.did(pool.memset(counts[:, :, :], 0.0))
                st.did(pool.iota(iota_i[:, :], pattern=[[1, E]], base=0, channel_multiplier=0))
                st.settle()
                st.did(pool.tensor_copy(iota_f[:, :], iota_i[:, :]))
                st.did(pool.affine_select(out=own[:, :], in_=own[:, :], compare_op=ALU.is_ge, fill=0.0,
                                          base=0, pattern=[[1, TOK]], channel_multiplier=-S))
                st.settle()
                st.did(pool.affine_select(out=own[:, :], in_=own[:, :], compare_op=ALU.is_ge, fill=0.0,
                                          base=S - 1, pattern=[[-1, TOK]], channel_multiplier=S))
                pool.affine_select(out=before[:, :], in_=before[:, :], compare_op=ALU.is_ge, fill=0.0,
                                   base=-1, pattern=[[1, P]], channel_multiplier=-1).then_inc(made, 1)
                pool.wait_ge(gb_in, 48)
                pool.tensor_scalar(gamma_b[:, :], gamma_b[:, :], gains[:, 0:1], None, ALU.mult).then_inc(made, 1)
                pool.tensor_scalar(beta_b[:, :], beta_b[:, :], gains[:, 0:1], None, ALU.mult).then_inc(made, 1)
                pool.wait_ge(made, 3)

                def part(t, _):
                    for n in range(3):
                        pool.wait_ge(stat_done, t * 3 + n + 1)
                        apart(pool)
                        rsqrt(pool, st, rstd[:, :], mv[:, :, 1], power[:, :], rstd_done)
                        if n == 0:
                            pool.wait_ge(x_in, t * 16 + 16)
                            pool.tensor_tensor(xb[:, :, :], xt[:, :, :],
                                               beta_b[:, :].unsqueeze(1).to_broadcast([P, GT, D]),
                                               ALU.add).then_inc(xb_done, 1)
                    pool.wait_ge(rows_hi, t + 1)
                    pool.tensor_tensor(rows[:, :, LO, :], xn[:, :, :], rows[:, :, HI, :],
                                       ALU.subtract).then_inc(rows_lo, 1)
                    pool.wait_ge(rows_lo, t + 1)
                    pool.wait_ge(sidx_done, t + 1)
                    apart(pool)
                    for j in range(GT):
                        for k in range(2):
                            pool.indirect_dma_start(
                                slots_d, bass.IndirectOffsetOnAxis(ap=sidx[:, 2 * j + k:2 * j + k + 1], axis=0),
                                rows[:, j, :, :].rearrange("p h d -> p (h d)"), None,
                                bounds_check=E * CAP - 1, oob_is_err=False).then_inc(scattered, 16)
                repeat(pool, st, NG, part)
                pool.wait_ge(scattered, NG * GT * 32)

            @block.scalar
            def _(act):
                act.wait_ge(gw_ps, 1)
                act.activation(gwT[:, HI, :, :], bank[7][:, 0:DC * E].rearrange("p (c e) -> p c e", c=DC),
                               ACT.Copy).then_inc(gw_hi, 1)

                def part(t, _):
                    act.wait_ge(xn_done, t + 1)
                    if later(t, 1):
                        act.wait_ge(scattered, t * (GT * 32))
                    act.activation(rows[:, :, HI, :], xn[:, :, :], ACT.Copy).then_inc(rows_hi, 1)
                    for j in range(GT):
                        act.wait_ge(xT_ps, t * GT + j + 1)
                        if later(t, 1):
                            act.wait_ge(xT_out, t * 16)
                            act.wait_ge(logit_ps, t)
                        act.activation(xT[:, j, HI, :, :].rearrange("p c q -> p (c q)"), bank[j][:, :],
                                       ACT.Copy).then_inc(xT_hi, 1)
                    act.wait_ge(nmax_done, t + 1)
                    for j in range(GT):
                        ins = act.activation(probs[:, j, :], bank[5][:, j * E:(j + 1) * E], ACT.Exp,
                                             bias=nmax[:, j:j + 1], accum_out=esum[:, j:j + 1])
                    ins.then_inc(exp_done, 1)
                repeat(act, Steps(act, None), NG, part)

            @block.vector
            def _(dve):
                st = Steps(dve, dve_c)
                dve.wait_ge(gw_hi, 1)
                st.did(dve.tensor_tensor(gwT[:, LO, :, :], bank[7][:, 0:DC * E].rearrange("p (c e) -> p c e", c=DC),
                                         gwT[:, HI, :, :], ALU.subtract))
                dve.wait_ge(made, 3)

                def part(t, _):
                    dve.wait_ge(x_in, t * 16 + 16)
                    row_stats(dve, st, lambda j: xt[:, j, :], stats, mv, GT, stat_done)
                    dve.wait_ge(rstd_done, 3 * t + 1)
                    for j in range(GT):
                        st.did(dve.tensor_scalar(y[:, j, :], xt[:, j, :], mv[:, j, 0:1], rstd[:, j:j + 1],
                                                 ALU.subtract, ALU.mult))
                    st.settle()
                    for j in range(GT):
                        dve.wait_ge(own_ps, t * GT + j + 1)
                        st.did(dve.tensor_tensor(y[:, j, :], y[:, j, :], bank[j][:, :], ALU.add))
                    st.settle()
                    row_stats(dve, st, lambda j: y[:, j, :], stats, mv, GT, stat_done)
                    dve.wait_ge(rstd_done, 3 * t + 2)
                    for j in range(GT):
                        st.did(dve.tensor_scalar(y[:, j, :], y[:, j, :], mv[:, j, 0:1], rstd[:, j:j + 1],
                                                 ALU.subtract, ALU.mult))
                    st.settle()
                    st.did(dve.tensor_tensor(y[:, :, :], y[:, :, :],
                                             gamma_b[:, :].unsqueeze(1).to_broadcast([P, GT, D]), ALU.mult))
                    st.settle()
                    dve.wait_ge(xb_done, t + 1)
                    if later(t, 1):
                        dve.wait_ge(x1_out, t * 16)
                    dve.tensor_tensor(x1[:, :, :], y[:, :, :], xb[:, :, :], ALU.add).then_inc(x1_done, 1)
                    dve.wait_ge(x1_done, t + 1)
                    row_stats(dve, st, lambda j: x1[:, j, :], stats, mv, GT, stat_done)
                    dve.wait_ge(rstd_done, 3 * t + 3)
                    for j in range(GT):
                        ins = dve.tensor_scalar(xn[:, j, :], x1[:, j, :], mv[:, j, 0:1], rstd[:, j:j + 1],
                                                ALU.subtract, ALU.mult)
                        if j < GT - 1:
                            st.did(ins)
                    ins.then_inc(xn_done, 1)
                    for j in range(GT):
                        dve.wait_ge(xT_hi, t * GT + j + 1)
                        dve.tensor_tensor(xT[:, j, LO, :, :].rearrange("p c q -> p (c q)"), bank[j][:, :],
                                          xT[:, j, HI, :, :].rearrange("p c q -> p (c q)"),
                                          ALU.subtract).then_inc(xT_lo, 1)
                    dve.wait_ge(logit_ps, t + 1)
                    dve.tensor_reduce(nmax[:, :], bank[5][:, 0:GT * E].rearrange("p (j e) -> p j e", e=E),
                                      axis=AX.X, op=ALU.max, negate=True).then_inc(nmax_done, 1)
                    dve.wait_ge(exp_done, t + 1)
                    st.did(dve.reciprocal(rsum[:, :], esum[:, :]))
                    st.settle()
                    st.did(dve.tensor_tensor(probs[:, :, :], probs[:, :, :], wide(rsum[:, :], E), ALU.mult))
                    st.settle(alone=True)
                    for j in range(GT):
                        st.did(dve.max(top8[:, j, :], probs[:, j, :]))
                    st.settle(alone=True)
                    for j in range(GT):
                        st.did(dve.max_index(top8i[:, j, :], top8[:, j, :], probs[:, j, :]))
                    st.did(dve.tensor_copy(topw[:, bass.ds(t * GT, GT), :], top8[:, :, 0:2]))
                    st.settle()
                    st.did(dve.tensor_copy(chosen[:, :].rearrange("p (j k) -> p j k", k=2), top8i[:, :, 0:2]))
                    st.settle()
                    st.did(dve.tensor_tensor(hot[:, :, :], iota_f[:, :].unsqueeze(1).to_broadcast([P, GT * 2, E]),
                                             wide(chosen[:, :], E), ALU.is_equal))
                    st.settle()
                    pair = hot[:, :, :].rearrange("p (j k) e -> p j k e", k=2)
                    st.did(dve.tensor_tensor(picks[:, :, :], pair[:, :, 0, :], pair[:, :, 1, :], ALU.add))
                    if later(t, 1):
                        st.did(dve.tensor_copy(counts[:, 0, :], counts[:, GT, :]))
                    else:
                        st.did(dve.tensor_copy(counts[:, GT, :], counts[:, 0, :]))
                    st.settle()
                    for j in range(GT):
                        ins = dve.tensor_tensor(counts[:, j + 1, :], counts[:, j, :], picks[:, j, :], ALU.add)
                        if j < GT - 1:
                            st.did(ins)
                            st.settle()
                    ins.then_inc(picks_done, 1)
                    dve.wait_ge(rank_ps, t + 1)
                    rank = bank[6][:, 0:GT * E].rearrange("p (j e) -> p j e", e=E)
                    hits = hit[:, :, :].rearrange("p (j k) e -> p j k e", k=2)
                    for k in range(2):
                        st.did(dve.tensor_tensor(hits[:, :, k, :], pair[:, :, k, :], rank, ALU.mult))
                    st.settle()
                    st.did(dve.tensor_reduce(pos[:, :], hit[:, :, :], axis=AX.X, op=ALU.add))
                    st.settle()
                    st.did(dve.tensor_scalar(slot[:, :], pos[:, :], float(CAP - 1), None, ALU.min))
                    st.did(dve.tensor_scalar(over[:, :], pos[:, :], float(CAP), float(E * CAP),
                                             ALU.is_ge, ALU.mult))
                    st.settle()
                    st.did(dve.scalar_tensor_tensor(out=slot[:, :], in0=chosen[:, :], scalar=float(CAP),
                                                    in1=slot[:, :], op0=ALU.mult, op1=ALU.add))
                    st.settle()
                    st.did(dve.tensor_copy(gidx[:, bass.ds(t * GT, GT), :],
                                           slot[:, :].rearrange("p (j k) -> p j k", k=2)))
                    if later(t, 1):
                        dve.wait_ge(scattered, t * (GT * 32))
                    dve.tensor_tensor(sidx[:, :], slot[:, :], over[:, :], ALU.add).then_inc(sidx_done, 1)
                repeat(dve, st, NG, part)

            @block.tensor
            def _(pe):
                pe.wait_ge(gb_in, 48)
                for c in range(DC):
                    ins = pe.transpose(bank[7][:, c * E:(c + 1) * E], gw[:, c * P:(c + 1) * P], ident[0:E, 0:E])
                ins.then_inc(gw_ps, 1)
                pe.wait_ge(made, 1)

                def part(t, _):
                    for j in range(GT):
                        if later(t, 1):
                            pe.wait_ge(xT_lo, t * GT - GT + j + 1)
                        for n in range(3):
                            ins = pe.matmul(bank[j][:, :], own[:, bass.ds(t * (GT * P) + j * P, P)],
                                            summary[:, n, :], start=n == 0, stop=n == 2)
                        ins.then_inc(own_ps, 1)
                    pe.wait_ge(xn_done, t + 1)
                    for j in range(GT):
                        for c in range(DC):
                            ins = pe.transpose(bank[j][:, c * P:(c + 1) * P], xn[:, j, c * P:(c + 1) * P],
                                               ident[:, :])
                        ins.then_inc(xT_ps, 1)
                    for j in range(GT):
                        pe.wait_ge(xT_hi, t * GT + j + 1)
                        pe.wait_ge(xT_lo, t * GT + j + 1)
                        if j == 0 and later(t, 1):
                            pe.wait_ge(exp_done, t)
                        n = 0
                        for c in range(DC):
                            for a, w in PAIRS:
                                ins = pe.matmul(bank[5][:, j * E:(j + 1) * E], xT[:, j, a, c, :],
                                                gwT[:, w, c, :], start=n == 0, stop=n == 11)
                                n += 1
                    ins.then_inc(logit_ps, 1)
                    pe.wait_ge(picks_done, t + 1)
                    pe.matmul(bank[6][:, 0:GT * E], before[:, :], picks[:, :, :].rearrange("p j e -> p (j e)"),
                              start=True, stop=False)
                    pe.matmul(bank[6][:, 0:GT * E], ones[:, :], counts[:, 0:GT, :].rearrange("p j e -> p (j e)"),
                              start=False, stop=True).then_inc(rank_ps, 1)
                repeat(pe, Steps(pe, None), NG, part)


def last_of(t, count):
    return isinstance(t, int) and t == count - 1


def expert_phase(nc, g, w_gate, w_up, w_down, slots_d, eout_d):
    identb, bank = g["identb"], g["bank"]
    with ExitStack() as es:
        def sb(name, shape, dt=F32):
            return es.enter_context(nc.sbuf_tensor(name, shape, dt))

        def sem(name):
            return nc.alloc_semaphore(f"expert_{name}")

        gu_raw = sb("gu_raw", [P, 2, DC, I])
        down_raw = sb("down_raw", [P, 3, D])
        gu = [sb(f"gu{k}", [P, 2, 2, DC, I], BF16) for k in range(2)]
        dn = [sb(f"dn{k}", [P, 2, 3, D], BF16) for k in range(2)]
        xs = [sb(f"xs{k}", [P, 2, 2, D], BF16) for k in range(2)]
        xsT = [sb(f"xsT{k}", [P, 2, DC, CAP], BF16) for k in range(2)]
        act_g = [sb(f"act_g{k}", [P, CAP]) for k in range(2)]
        h = [sb(f"h{k}", [P, CAP]) for k in range(2)]
        hT = sb("hT", [P, 2, 3, CAP], BF16)
        eo = [sb(f"eo{k}", [P, D]) for k in range(2)]
        gu_in, down_in = sem("gu_in"), sem("down_in")
        xs_in = [sem(f"xs_in{k}") for k in range(2)]
        gu_hi, gu_lo, dn_hi, dn_lo = sem("gu_hi"), sem("gu_lo"), sem("dn_hi"), sem("dn_lo")
        xs_ps, xsT_done, xsT_done_v = sem("xs_ps"), sem("xsT_done"), sem("xsT_done_v")
        gu_ps, silu_done, h_done, hT_hi, hT_lo = (sem(n) for n in (
            "gu_ps", "silu_done", "h_done", "hT_hi", "hT_lo"))
        out_ps, eo_done = sem("out_ps"), sem("eo_done")
        eo_out = [sem(f"eo_out{k}") for k in range(2)]
        with nc.Block() as block:
            @block.sync
            def _(sp):
                def load_xs(t, k):
                    sp.dma_start(xs[k][:, :, :, :].rearrange("p s h d -> p s (h d)"),
                                 slots_d[bass.ds(t * CAP, CAP), :].rearrange("(s p) d -> p s d", p=P)
                                 ).then_inc(xs_in[k], 16)

                def load_w(t):
                    for n, w in enumerate((w_gate, w_up)):
                        sp.dma_start(gu_raw[:, n, :, :],
                                     w[bass.ds(t, 1), :, :].rearrange("a (c p) i -> p (a c) i", p=P)
                                     ).then_inc(gu_in, 16)

                def load_down(t):
                    rows = w_down[bass.ds(t, 1), :, :].rearrange("a i d -> (a i) d")
                    sp.dma_start(down_raw[:, 0:2, :], rows[0:256, :].rearrange("(c p) d -> p c d", p=P)
                                 ).then_inc(down_in, 16)
                    sp.dma_start(down_raw[0:I - 256, 2, :], rows[256:I, :]).then_inc(down_in, 16)
                load_w(0)
                load_xs(0, 0)
                load_down(0)
                load_xs(1, 1)

                def part(t, k):
                    if not last_of(t, E):
                        sp.wait_ge(gu_hi, t + 1)
                        sp.wait_ge(gu_lo, t + 1)
                        load_w(t + 1)
                        sp.wait_ge(dn_hi, t + 1)
                        sp.wait_ge(dn_lo, t + 1)
                        load_down(t + 1)
                    if not isinstance(t, int) or t < E - 2:
                        sp.wait_ge(xs_ps, 2 * t + 2)
                        load_xs(t + 2, k)
                    for s in range(2):
                        sp.wait_ge(eo_done, 2 * t + s + 1)
                        sp.dma_start(eout_d[bass.ds(t * CAP + s * P, P), :], eo[s][:, :]).then_inc(eo_out[s], 16)
                repeat(sp, Steps(sp, None), E, part, unroll=2, tail=2)
                for s in range(2):
                    sp.wait_ge(eo_out[s], E * 16)

            @block.gpsimd
            def _(pool):
                def part(t, k):
                    pool.wait_ge(dn_hi, t + 1)
                    if later(t, 2):
                        pool.wait_ge(out_ps, 2 * t - 2)
                    pool.tensor_tensor(dn[k][:, LO, 0:2, :], down_raw[:, 0:2, :], dn[k][:, HI, 0:2, :], ALU.subtract)
                    pool.tensor_tensor(dn[k][0:I - 256, LO, 2, :], down_raw[0:I - 256, 2, :],
                                       dn[k][0:I - 256, HI, 2, :], ALU.subtract).then_inc(dn_lo, 1)
                repeat(pool, Steps(pool, None), E, part, unroll=2)

            @block.scalar
            def _(act):
                def split(t, k):
                    act.wait_ge(gu_in, t * 32 + 32)
                    if later(t, 2):
                        act.wait_ge(gu_ps, 3 * t - 3)
                    act.activation(gu[k][:, HI, :, :, :], gu_raw[:, :, :, :], ACT.Copy).then_inc(gu_hi, 1)
                    act.wait_ge(down_in, t * 32 + 32)
                    if later(t, 2):
                        act.wait_ge(out_ps, 2 * t - 2)
                    act.activation(dn[k][:, HI, 0:2, :], down_raw[:, 0:2, :], ACT.Copy)
                    act.activation(dn[k][0:I - 256, HI, 2, :], down_raw[0:I - 256, 2, :], ACT.Copy
                                   ).then_inc(dn_hi, 1)
                split(0, 0)

                def part(t, k):
                    act.wait_ge(xs_ps, 2 * t + 1)
                    if later(t, 2):
                        act.wait_ge(gu_ps, 3 * t - 3)
                    act.activation(xsT[k][:, :, :, 0:P].rearrange("p h c q -> p (h c) q"),
                                   bank[2][:, :].bitcast(BF16).rearrange("p (c q) -> p c q", q=P),
                                   ACT.Copy).then_inc(xsT_done, 1)
                    for m, (_, rows) in enumerate(IC):
                        act.wait_ge(gu_ps, 3 * t + m + 1)
                        if later(t, 1) or m >= 2:
                            act.wait_ge(h_done, 3 * t + m - 1)
                        act.activation(act_g[(k + m) % 2][0:rows, :], bank[(k + m) % 2][0:rows, 0:CAP], ACT.Silu
                                       ).then_inc(silu_done, 1)
                        act.wait_ge(h_done, 3 * t + m + 1)
                        if later(t, 1):
                            act.wait_ge(out_ps, 2 * t)
                        act.activation(hT[0:rows, HI, m, :], h[(k + m) % 2][0:rows, :], ACT.Copy).then_inc(hT_hi, 1)
                    if not last_of(t, E):
                        split(t + 1, 1 - k)
                    for s in range(2):
                        act.wait_ge(out_ps, 2 * t + s + 1)
                        if later(t, 1):
                            act.wait_ge(eo_out[s], t * 16)
                        act.activation(eo[s][:, :], bank[4 + s][:, :], ACT.Copy).then_inc(eo_done, 1)
                repeat(act, Steps(act, None), E, part, unroll=2, tail=2)

            @block.vector
            def _(dve):
                def split(t, k):
                    dve.wait_ge(gu_hi, t + 1)
                    dve.tensor_tensor(gu[k][:, LO, :, :, :].rearrange("p n c i -> p (n c i)"),
                                      gu_raw[:, :, :, :].rearrange("p n c i -> p (n c i)"),
                                      gu[k][:, HI, :, :, :].rearrange("p n c i -> p (n c i)"),
                                      ALU.subtract).then_inc(gu_lo, 1)
                split(0, 0)

                def part(t, k):
                    dve.wait_ge(xs_ps, 2 * t + 2)
                    if later(t, 2):
                        dve.wait_ge(gu_ps, 3 * t - 3)
                    dve.tensor_copy(xsT[k][:, :, :, P:CAP].rearrange("p h c q -> p (h c) q"),
                                    bank[3][:, :].bitcast(BF16).rearrange("p (c q) -> p c q", q=P)
                                    ).then_inc(xsT_done_v, 1)
                    for m, (_, rows) in enumerate(IC):
                        dve.wait_ge(silu_done, 3 * t + m + 1)
                        if later(t, 1) or m >= 2:
                            dve.wait_ge(hT_hi, 3 * t + m - 1)
                            dve.wait_ge(hT_lo, 3 * t + m - 1)
                        dve.tensor_tensor(h[(k + m) % 2][0:rows, :], act_g[(k + m) % 2][0:rows, :],
                                          bank[(k + m) % 2][0:rows, CAP:2 * CAP], ALU.mult).then_inc(h_done, 1)
                        dve.wait_ge(hT_hi, 3 * t + m + 1)
                        if later(t, 1):
                            dve.wait_ge(out_ps, 2 * t)
                        dve.tensor_tensor(hT[0:rows, LO, m, :], h[(k + m) % 2][0:rows, :], hT[0:rows, HI, m, :],
                                          ALU.subtract).then_inc(hT_lo, 1)
                    if not last_of(t, E):
                        split(t + 1, 1 - k)
                repeat(dve, Steps(dve, None), E, part, unroll=2, tail=2)

            @block.tensor
            def _(pe):
                def turn(t, k):
                    pe.wait_ge(xs_in[k], t * 8 + 16 if k == 0 else t * 8 + 8)
                    for s in range(2):
                        if later(t, 1):
                            pe.wait_ge((xsT_done, xsT_done_v)[s], t)
                        for q in range(2 * DC):
                            ins = pe.transpose(bank[2 + s][:, q * 64:(q + 1) * 64].bitcast(BF16),
                                               xs[k][:, s, q // DC, (q % DC) * P:(q % DC + 1) * P], identb[:, :])
                        ins.then_inc(xs_ps, 1)
                turn(0, 0)

                def part(t, k):
                    pe.wait_ge(xsT_done, t + 1)
                    pe.wait_ge(xsT_done_v, t + 1)
                    pe.wait_ge(gu_hi, t + 1)
                    pe.wait_ge(gu_lo, t + 1)
                    for m, (i0, rows) in enumerate(IC):
                        if later(t, 1) or m >= 2:
                            pe.wait_ge(h_done, 3 * t + m - 1)
                        for u in range(2):
                            n = 0
                            for c in range(DC):
                                for a, w in PAIRS:
                                    ins = pe.matmul(bank[(k + m) % 2][0:rows, u * CAP:(u + 1) * CAP],
                                                    gu[k][:, w, u, c, i0:i0 + rows], xsT[k][:, a, c, :],
                                                    start=n == 0, stop=n == 11)
                                    n += 1
                        ins.then_inc(gu_ps, 1)
                    if not last_of(t, E):
                        turn(t + 1, 1 - k)
                    pe.wait_ge(hT_hi, 3 * t + 3)
                    pe.wait_ge(hT_lo, 3 * t + 3)
                    pe.wait_ge(dn_lo, t + 1)
                    for s in range(2):
                        if later(t, 1):
                            pe.wait_ge(eo_done, 2 * t + s - 1)
                        n = 0
                        for c, (_, rows) in enumerate(IC):
                            for a, w in PAIRS:
                                ins = pe.matmul(bank[4 + s][:, :], hT[0:rows, a, c, s * P:(s + 1) * P],
                                                dn[k][0:rows, w, c, :], start=n == 0, stop=n == 8)
                                n += 1
                        ins.then_inc(out_ps, 1)
                repeat(pe, Steps(pe, None), E, part, unroll=2, tail=2)


def shared_phase(nc, g, ws_gate, ws_up, ws_down, xT_d, eout_d, x1_d, x2_d):
    gains, bank, gidx, topw = g["gains"], g["bank"], g["gidx"], g["topw"]
    SUBS = [(0, 3), (3, 2)]
    with ExitStack() as es:
        def sb(name, shape, dt=F32):
            return es.enter_context(nc.sbuf_tensor(name, shape, dt))

        def sem(name):
            return nc.alloc_semaphore(f"shared_{name}")

        gs, us = (sb(n, [P, 2, DC, IS], BF16) for n in ("gs", "us"))
        ds_ = sb("ds_", [P, 2, 6, D], BF16)
        with ExitStack() as es2:
            raw = es2.enter_context(nc.sbuf_tensor("raw", [P, 2, DC, IS], F32))
            raw_d = es2.enter_context(nc.sbuf_tensor("raw_d", [P, 6, D], F32))
            raw_in = [nc.alloc_semaphore(f"raw_in{n}") for n in range(3)]
            raw_hi = nc.alloc_semaphore("raw_hi")
            with nc.Block() as block:
                @block.sync
                def _(sp):
                    for n, w in enumerate((ws_gate, ws_up)):
                        sp.dma_start(raw[:, n, :, :], w.rearrange("(c p) i -> p c i", p=P)).then_inc(raw_in[n], 16)
                    sp.dma_start(raw_d[:, 0:5, :], ws_down[0:640, :].rearrange("(c p) d -> p c d", p=P)
                                 ).then_inc(raw_in[2], 16)
                    sp.dma_start(raw_d[0:64, 5, :], ws_down[640:IS, :]).then_inc(raw_in[2], 16)

                @block.scalar
                def _(act):
                    for n, w in enumerate((gs, us)):
                        act.wait_ge(raw_in[n], 16)
                        act.activation(w[:, HI, :, :], raw[:, n, :, :], ACT.Copy).then_inc(raw_hi, 1)
                    act.wait_ge(raw_in[2], 32)
                    act.activation(ds_[:, HI, 0:5, :], raw_d[:, 0:5, :], ACT.Copy)
                    act.activation(ds_[0:64, HI, 5, :], raw_d[0:64, 5, :], ACT.Copy).then_inc(raw_hi, 1)

                @block.vector
                def _(dve):
                    for n, w in enumerate((gs, us)):
                        dve.wait_ge(raw_hi, n + 1)
                        dve.tensor_tensor(w[:, LO, :, :], raw[:, n, :, :], w[:, HI, :, :], ALU.subtract)
                    dve.wait_ge(raw_hi, 3)
                    dve.tensor_tensor(ds_[:, LO, 0:5, :], raw_d[:, 0:5, :], ds_[:, HI, 0:5, :], ALU.subtract)
                    dve.tensor_tensor(ds_[0:64, LO, 5, :], raw_d[0:64, 5, :], ds_[0:64, HI, 5, :], ALU.subtract)
        xg = sb("xg", [P, GT, 2, DC, P], BF16)
        sg = [sb(f"sg{k}", [P, 3 * P]) for k in range(2)]
        hs = [sb(f"hs{k}", [P, 3 * P]) for k in range(2)]
        hT = sb("hsT", [P, 2, 6, GT * P], BF16)
        fetched = sb("fetched", [P, GT, 2, D])
        at = sb("at", [P, GT, 2], U32)
        xr = sb("xr", [P, GT, D])
        mix = [sb(f"mix{k}", [P, D]) for k in range(2)]
        xg_in, x1_in, x2_out = sem("xg_in"), sem("x1_in"), sem("x2_out")
        gu_ps, silu_done, h_done, hT_hi, hT_lo = (sem(n) for n in (
            "sgu_ps", "ssilu_done", "sh_done", "shT_hi", "shT_lo"))
        out_ps, x2_done, dve_c = sem("sout_ps"), sem("x2_done"), sem("dve_c4")
        at_done, at_c = sem("at_done"), sem("at_c")
        got = [sem(f"got{j}") for j in range(GT)]
        xof = xT_d.rearrange("(t p) d -> p t d", p=P)
        x1of = x1_d.rearrange("(t p) d -> p t d", p=P)
        x2of = x2_d.rearrange("(t p) d -> p t d", p=P)
        with nc.Block() as block:
            @block.sync
            def _(sp):
                sp.dma_start(xg[:, :, :, :, :].rearrange("p t h c q -> p t (h c q)"), xof[:, 0:GT, :]
                             ).then_inc(xg_in, 16)

                def part(t, _):
                    if later(t, 1):
                        sp.wait_ge(x2_out, t * 16)
                    sp.dma_start(xr[:, :, :], x1of[:, bass.ds(t * GT, GT), :]).then_inc(x1_in, 16)
                    if not last_of(t, NG):
                        sp.wait_ge(gu_ps, t * 12 + 12)
                        sp.dma_start(xg[:, :, :, :, :].rearrange("p t h c q -> p t (h c q)"),
                                     xof[:, bass.ds(t * GT + GT, GT), :]).then_inc(xg_in, 16)
                    sp.wait_ge(x2_done, t * GT + GT)
                    sp.dma_start(x2of[:, bass.ds(t * GT, GT), :], xr[:, :, :]).then_inc(x2_out, 16)
                repeat(sp, Steps(sp, None), NG, part, tail=1)
                sp.wait_ge(x2_out, NG * 16)

            @block.gpsimd
            def _(pool):
                st = Steps(pool, at_c)

                def part(t, _):
                    if later(t, 1):
                        for j in range(GT):
                            pool.wait_ge(got[j], t * 32)
                    st.did(pool.tensor_copy(at[:, :, :], gidx[:, bass.ds(t * GT, GT), :]))
                    st.settle(alone=True)
                    for j in range(GT):
                        if later(t, 1):
                            pool.wait_ge(x2_done, t * GT - GT + j + 1)
                            apart(pool)
                        for n in range(2):
                            pool.indirect_dma_start(
                                fetched[:, j, n, :], None, eout_d,
                                bass.IndirectOffsetOnAxis(ap=at[:, j, n:n + 1], axis=0),
                                bounds_check=E * CAP - 1, oob_is_err=False).then_inc(got[j], 16)
                repeat(pool, st, NG, part)

            @block.scalar
            def _(act):
                def part(t, _):
                    for u, (t0, tn) in enumerate(SUBS):
                        for m, (_, rows) in enumerate(SC):
                            q = 6 * u + m
                            act.wait_ge(gu_ps, t * 12 + q + 1)
                            if later(t, 1) or q >= 2:
                                act.wait_ge(h_done, t * 12 + q - 1)
                            act.activation(sg[q % 2][0:rows, 0:tn * P], bank[2 * (q % 2)][0:rows, 0:tn * P],
                                           ACT.Silu).then_inc(silu_done, 1)
                            act.wait_ge(h_done, t * 12 + q + 1)
                            if later(t, 1):
                                act.wait_ge(out_ps, t * GT)
                            act.activation(hT[0:rows, HI, m, t0 * P:(t0 + tn) * P], hs[q % 2][0:rows, 0:tn * P],
                                           ACT.Copy).then_inc(hT_hi, 1)
                repeat(act, Steps(act, None), NG, part)

            @block.vector
            def _(dve):
                st = Steps(dve, dve_c)

                def part(t, _):
                    for u, (t0, tn) in enumerate(SUBS):
                        for m, (_, rows) in enumerate(SC):
                            q = 6 * u + m
                            dve.wait_ge(silu_done, t * 12 + q + 1)
                            if later(t, 1) or q >= 2:
                                dve.wait_ge(hT_hi, t * 12 + q - 1)
                                dve.wait_ge(hT_lo, t * 12 + q - 1)
                            dve.tensor_tensor(hs[q % 2][0:rows, 0:tn * P], sg[q % 2][0:rows, 0:tn * P],
                                              bank[2 * (q % 2) + 1][0:rows, 0:tn * P], ALU.mult
                                              ).then_inc(h_done, 1)
                            dve.wait_ge(hT_hi, t * 12 + q + 1)
                            if later(t, 1):
                                dve.wait_ge(out_ps, t * GT)
                            dve.tensor_tensor(hT[0:rows, LO, m, t0 * P:(t0 + tn) * P], hs[q % 2][0:rows, 0:tn * P],
                                              hT[0:rows, HI, m, t0 * P:(t0 + tn) * P], ALU.subtract
                                              ).then_inc(hT_lo, 1)
                    dve.wait_ge(x1_in, t * 16 + 16)
                    for j in range(GT):
                        combine(t, t * GT + j, j)

                def combine(t, i, j):
                    dve.wait_ge(out_ps, t * GT + j + 1)
                    dve.wait_ge(got[j], t * 32 + 32)
                    src = mix[j % 2]
                    st.did(dve.scalar_tensor_tensor(out=src[:, :], in0=fetched[:, j, 0, :],
                                                    scalar=topw[:, bass.ds(i, 1), 0], in1=bank[4 + j % 3][:, :],
                                                    op0=ALU.mult, op1=ALU.add))
                    st.settle()
                    st.did(dve.scalar_tensor_tensor(out=src[:, :], in0=fetched[:, j, 1, :],
                                                    scalar=topw[:, bass.ds(i, 1), 1], in1=src[:, :],
                                                    op0=ALU.mult, op1=ALU.add))
                    st.settle()
                    dve.scalar_tensor_tensor(out=xr[:, j, :], in0=src[:, :], scalar=gains[:, 2:3],
                                             in1=xr[:, j, :], op0=ALU.mult, op1=ALU.add).then_inc(x2_done, 1)
                repeat(dve, st, NG, part)

            @block.tensor
            def _(pe):
                def part(t, _):
                    pe.wait_ge(xg_in, t * 16 + 16)
                    for u, (t0, tn) in enumerate(SUBS):
                        for m, (i0, rows) in enumerate(SC):
                            q = 6 * u + m
                            if later(t, 1) or q >= 2:
                                pe.wait_ge(h_done, t * 12 + q - 1)
                            for v, w_ in enumerate((gs, us)):
                                n = 0
                                for c in range(DC):
                                    for a, w in PAIRS:
                                        ins = pe.matmul(
                                            bank[2 * (q % 2) + v][0:rows, 0:tn * P].rearrange(
                                                "r (t q) -> r t q", q=P),
                                            w_[:, w, c, i0:i0 + rows], xg[:, t0:t0 + tn, a, c, :],
                                            start=n == 0, stop=n == 11)
                                        n += 1
                            ins.then_inc(gu_ps, 1)
                    for j in range(GT):
                        u = 0 if j < 3 else 1
                        pe.wait_ge(hT_hi, t * 12 + 6 * u + 6)
                        pe.wait_ge(hT_lo, t * 12 + 6 * u + 6)
                        if later(t, 1) or j >= 3:
                            pe.wait_ge(x2_done, t * GT + (-1, 0, -2, 1, 2)[j])
                        n = 0
                        for c, (_, rows) in enumerate(SC):
                            for a, w in PAIRS:
                                ins = pe.matmul(bank[4 + j % 3][:, :], hT[0:rows, a, c, j * P:(j + 1) * P],
                                                ds_[0:rows, w, c, :], start=n == 0, stop=n == 17)
                                n += 1
                        ins.then_inc(out_ps, 1)
                repeat(pe, Steps(pe, None), NG, part)


def attention_phase(nc, g, ctx, wq, wk, wv, wo, x2_d, x3_d):
    ident, gains, bank = g["ident"], g["gains"], g["bank"]
    NB = 4
    GR = B // NB
    SCALE = float(D) ** -0.5
    KEYS = CTX + S
    VC = CT + [(CTX, S)]
    with ExitStack() as es:
        def sb(name, shape, dt=F32):
            return es.enter_context(nc.sbuf_tensor(name, shape, dt))

        def sem(name):
            return nc.alloc_semaphore(f"attention_{name}")

        wT = [sb(f"{n}T", [P, 2, DC, D], BF16) for n in ("wq", "wk", "wv", "wo")]
        wqT, wkT, wvT, woT = wT
        with ExitStack() as es2:
            raw = es2.enter_context(nc.sbuf_tensor("wraw", [P, 4, DC, D], F32))
            raw_in = [nc.alloc_semaphore(f"wraw_in{n}") for n in range(4)]
            t_ps, t_hi, t_lo = (nc.alloc_semaphore(n) for n in ("t_ps", "t_hi", "t_lo"))
            with nc.Block() as block:
                @block.sync
                def _(sp):
                    for n, w in enumerate((wq, wk, wv, wo)):
                        sp.dma_start(raw[:, n, :, :], w.rearrange("(c p) d -> p c d", p=P)).then_inc(raw_in[n], 16)

                @block.tensor
                def _(pe):
                    for q in range(16):
                        n, c = q // 4, q % 4
                        if c == 0:
                            pe.wait_ge(raw_in[n], 16)
                        if q >= 4:
                            pe.wait_ge(t_lo, q - 3)
                        for r in range(DC):
                            ins = pe.transpose(bank[c][:, r * P:(r + 1) * P], raw[:, n, r, c * P:(c + 1) * P],
                                               ident[:, :])
                        ins.then_inc(t_ps, 1)

                @block.scalar
                def _(act):
                    for q in range(16):
                        act.wait_ge(t_ps, q + 1)
                        act.activation(wT[q // 4][:, HI, q % 4, :], bank[q % 4][:, :], ACT.Copy).then_inc(t_hi, 1)

                @block.vector
                def _(dve):
                    for q in range(16):
                        dve.wait_ge(t_hi, q + 1)
                        dve.tensor_tensor(wT[q // 4][:, LO, q % 4, :], bank[q % 4][:, :],
                                          wT[q // 4][:, HI, q % 4, :], ALU.subtract).then_inc(t_lo, 1)

        crow = [sb(f"arow{k}", [P, 3, D]) for k in range(2)]
        V = sb("V", [P, 2, 3, D], BF16)
        Vn = [sb(f"Vn{k}", [S, 2, D], BF16) for k in range(2)]
        KT = sb("KT", [P, 2, DC, CTX], BF16)
        xin = [sb(f"xin{k}", [S, D]) for k in range(2)]
        xres = [sb(f"xres{k}", [S, D]) for k in range(2)]
        xn = sb("axn", [S, NB, D])
        xgT = sb("xgT", [P, 2, DC, NB * S], BF16)
        qT, nkT = sb("qT", [P, 2, DC, NB * S], BF16), sb("nkT", [P, 2, DC, NB * S], BF16)
        prob = sb("prob", [S, KEYS + LAST - S])
        pT = sb("pT", [P, 2, 4, S], BF16)
        o = sb("o", [S, D])
        oT = sb("oT", [P, 2, DC, S], BF16)
        nmax, esum, rinv = (sb(n, [S, 2]) for n in ("anmax", "aesum", "arinv"))
        stats, mv, rstd, power = sb("astats", [S, 6]), sb("amv", [S, 2]), sb("arstd", [S, 1]), sb("apower", [S, 1])
        crow_in, xin_in, xres_in, x3_out = ([sem(f"{n}{k}") for k in range(2)] for n in (
            "acrow_in", "xin_in", "xres_in", "x3_out"))
        dve_c, pool_c, const_set = sem("dve_c5"), sem("pool_c5"), sem("const_set")
        stat_done, rstd_done, xn_done = sem("astat_done"), sem("arstd_done"), sem("axn_done")
        x_ps, xg_hi, xg_lo = sem("x_ps"), sem("xg_hi"), sem("xg_lo")
        qk_ps, qk_hi, qk_lo = sem("qk_ps"), sem("qk_hi"), sem("qk_lo")
        kT_ps, kT_hi, kT_lo = sem("kT_ps"), sem("kT_hi"), sem("kT_lo")
        vn_ps, vn_hi, vn_lo = sem("vn_ps"), sem("vn_hi"), sem("vn_lo")
        v_hi, v_lo = sem("v_hi"), sem("v_lo")
        s_ps, nmax_done, exp_done, rinv_done = sem("s_ps"), sem("anmax_done"), sem("aexp_done"), sem("rinv_done")
        pT_ps, pT_hi, pT_lo = sem("pT_ps"), sem("pT_hi"), sem("pT_lo")
        pv_ps, o_done = sem("pv_ps"), sem("o_done")
        oT_ps, oT_hi, oT_lo = sem("oT_ps"), sem("oT_hi"), sem("oT_lo")
        wo_ps, x3_done = sem("wo_ps"), sem("x3_done")

        def beyond(b, n):
            return not isinstance(b, int) or b >= n

        def dma_count(b, k, each=16):
            return b * (each // 2) + (each if k == 0 else each // 2)

        with nc.Block() as block:
            @block.sync
            def _(sp):
                def load_ctx(b, k):
                    row = ctx[bass.ds(b, 1), :, :].rearrange("a t d -> (a t) d")
                    sp.dma_start(crow[k][:, 0:2, :], row[0:256, :].rearrange("(c p) d -> p c d", p=P)
                                 ).then_inc(crow_in[k], 16)
                    sp.dma_start(crow[k][0:LAST, 2, :], row[256:CTX, :]).then_inc(crow_in[k], 16)

                def load_x(dst, b, k, signal):
                    sp.dma_start(dst[k][:, :], x2_d[bass.ds(b * S, S), :]).then_inc(signal[k], 16)

                for b in range(2):
                    load_x(xin, b, b, xin_in)
                for b in range(2):
                    load_ctx(b, b)
                    load_x(xres, b, b, xres_in)
                for b in range(2, NB + 2):
                    sp.wait_ge(xn_done, b - 1)
                    load_x(xin, b, b % 2, xin_in)

                def part(t, _):
                    for i in range(NB):
                        b, k = t * NB + i, i % 2
                        if i in (1, 2) and not last_of(t, GR):
                            sp.wait_ge(xn_done, t * NB + NB + i)
                            load_x(xin, t * NB + NB + 1 + i, (1 + i) % 2, xin_in)
                        if i == 3 and not (isinstance(t, int) and t >= GR - 2):
                            for n in range(2):
                                sp.wait_ge(xn_done, t * NB + 2 * NB - 1 + n)
                                load_x(xin, t * NB + 2 * NB + n, n, xin_in)
                        if not (last_of(t, GR) and i >= 2):
                            sp.wait_ge(v_hi, b + 1)
                            sp.wait_ge(v_lo, b + 1)
                            sp.wait_ge(kT_ps, b * DC + DC)
                            load_ctx(b + 2, k)
                        sp.wait_ge(x3_done, b + 1)
                        sp.dma_start(x3_d[bass.ds(b * S, S), :], xres[k][:, :]).then_inc(x3_out[k], 16)
                        if not (last_of(t, GR) and i >= 2):
                            sp.wait_ge(x3_out[k], dma_count(b, k))
                            load_x(xres, b + 2, k, xres_in)
                repeat(sp, Steps(sp, None), GR, part, tail=2)
                for k in range(2):
                    sp.wait_ge(x3_out[k], B // 2 * 16)

            @block.gpsimd
            def _(pool):
                st = Steps(pool, pool_c)
                pool.memset(power[:, :], -0.5)
                pool.memset(prob[:, KEYS:], 0.0).then_inc(const_set, 1)
                pool.wait_ge(const_set, 1)

                def norm(n):
                    pool.wait_ge(stat_done, n + 1)
                    apart(pool)
                    rsqrt(pool, st, rstd[:, :], mv[:, 1:2], power[:, :], rstd_done)

                def values(b, k):
                    pool.wait_ge(v_hi, b + 1)
                    pool.tensor_tensor(V[:, LO, 0:2, :], crow[k][:, 0:2, :], V[:, HI, 0:2, :], ALU.subtract)
                    pool.tensor_tensor(V[0:LAST, LO, 2, :], crow[k][0:LAST, 2, :], V[0:LAST, HI, 2, :],
                                       ALU.subtract).then_inc(v_lo, 1)
                for n in range(NB):
                    norm(n)
                values(0, 0)

                def part(t, _):
                    for i in range(NB):
                        if not last_of(t, GR):
                            for n in ((0,), (1,), (2, 3), ())[i]:
                                norm(t * NB + NB + n)
                        if not (last_of(t, GR) and i == NB - 1):
                            values(t * NB + i + 1, (i + 1) % 2)
                repeat(pool, st, GR, part, tail=1)

            @block.scalar
            def _(act):
                def keys_hi(b):
                    for c in range(DC):
                        act.wait_ge(kT_ps, b * DC + c + 1)
                        if c == 0 and beyond(b, 1):
                            act.wait_ge(s_ps, b)
                        act.activation(KT[:, HI, c, :], bank[1 + c % 2][:, 0:CTX], ACT.Copy).then_inc(kT_hi, 1)

                def rows_hi(t):
                    for i in range(NB):
                        act.wait_ge(x_ps, t * NB + i + 1)
                        act.activation(xgT[:, HI, :, i * S:(i + 1) * S],
                                       bank[1 + i % 2][:, 0:DC * S].rearrange("p (c s) -> p c s", c=DC),
                                       ACT.Copy).then_inc(xg_hi, 1)

                def project_hi(t):
                    for q in range(8):
                        act.wait_ge(qk_ps, t * 8 + q + 1)
                        act.activation((qT, nkT)[q // DC][:, HI, q % DC, :], bank[(3, 5)[q % 2]][:, 0:NB * S],
                                       ACT.Copy).then_inc(qk_hi, 1)

                def new_values_hi(b, k):
                    act.wait_ge(vn_ps, b + 1)
                    act.activation(Vn[k][:, HI, :], bank[3][0:S, :], ACT.Copy).then_inc(vn_hi, 1)

                def values_hi(b, k):
                    act.wait_ge(crow_in[k], dma_count(b, k, 32))
                    if beyond(b, 1):
                        act.wait_ge(pv_ps, b)
                    act.activation(V[:, HI, 0:2, :], crow[k][:, 0:2, :], ACT.Copy)
                    act.activation(V[0:LAST, HI, 2, :], crow[k][0:LAST, 2, :], ACT.Copy).then_inc(v_hi, 1)

                def attended_hi(b):
                    act.wait_ge(oT_ps, b + 1)
                    if beyond(b, 1):
                        act.wait_ge(wo_ps, b)
                    act.activation(oT[:, HI, :, :].rearrange("p c s -> p (c s)"), bank[6][:, 0:DC * S],
                                   ACT.Copy).then_inc(oT_hi, 1)
                rows_hi(0)
                project_hi(0)
                keys_hi(0)
                new_values_hi(0, 0)
                values_hi(0, 0)
                act.wait_ge(const_set, 1)

                def part(t, _):
                    for i in range(NB):
                        b, k = t * NB + i, i % 2
                        act.wait_ge(nmax_done, b + 1)
                        if beyond(b, 1):
                            act.wait_ge(pT_ps, b)
                        act.activation(prob[:, 0:KEYS], bank[0][0:S, 0:KEYS], ACT.Exp, scale=SCALE,
                                       bias=nmax[:, k:k + 1], accum_out=esum[:, k:k + 1]).then_inc(exp_done, 1)
                        if i == NB - 1 and not last_of(t, GR):
                            rows_hi(t + 1)
                        if beyond(b, 1):
                            attended_hi(b - 1)
                        if not (last_of(t, GR) and i == NB - 1):
                            keys_hi(b + 1)
                        if i == NB - 1 and not last_of(t, GR):
                            project_hi(t + 1)
                        act.wait_ge(pT_ps, b + 1)
                        if beyond(b, 1):
                            act.wait_ge(pv_ps, b)
                        act.activation(pT[:, HI, 0:2, :].rearrange("p c s -> p (c s)"), bank[4][:, 0:2 * S], ACT.Copy)
                        act.activation(pT[0:LAST, HI, 2:4, :].rearrange("p c s -> p (c s)"),
                                       bank[4][0:LAST, 2 * S:4 * S], ACT.Copy).then_inc(pT_hi, 1)
                        if not (last_of(t, GR) and i == NB - 1):
                            new_values_hi(b + 1, (i + 1) % 2)
                        act.wait_ge(pv_ps, b + 1)
                        act.wait_ge(rinv_done, b + 1)
                        act.activation(o[:, :], bank[5][0:S, :], ACT.Copy, scale=rinv[:, k:k + 1]).then_inc(o_done, 1)
                        if not (last_of(t, GR) and i == NB - 1):
                            values_hi(b + 1, (i + 1) % 2)
                repeat(act, Steps(act, None), GR, part, tail=1)
                attended_hi(B - 1)

            @block.vector
            def _(dve):
                st = Steps(dve, dve_c)

                def norm(n, k, slot):
                    dve.wait_ge(xin_in[k], dma_count(n, k))
                    st.did(dve.bn_stats(stats[:, :], xin[k][:, :]))
                    st.settle(alone=True)
                    dve.bn_aggr(mv[:, :], stats[:, :]).then_inc(stat_done, 1)
                    dve.wait_ge(rstd_done, n + 1)
                    dve.wait_ge(stat_done, n + 1)
                    if beyond(n, NB):
                        dve.wait_ge(x_ps, n - NB + 1)
                    dve.tensor_scalar(xn[:, slot, :], xin[k][:, :], mv[:, 0:1], rstd[:, 0:1],
                                      ALU.subtract, ALU.mult).then_inc(xn_done, 1)

                def keys_lo(b):
                    for c in range(DC):
                        dve.wait_ge(kT_hi, b * DC + c + 1)
                        dve.tensor_tensor(KT[:, LO, c, :], bank[1 + c % 2][:, 0:CTX], KT[:, HI, c, :],
                                          ALU.subtract).then_inc(kT_lo, 1)

                def rows_lo(t):
                    for i in range(NB):
                        dve.wait_ge(xg_hi, t * NB + i + 1)
                        dve.tensor_tensor(xgT[:, LO, :, i * S:(i + 1) * S],
                                          bank[1 + i % 2][:, 0:DC * S].rearrange("p (c s) -> p c s", c=DC),
                                          xgT[:, HI, :, i * S:(i + 1) * S], ALU.subtract).then_inc(xg_lo, 1)

                def project_lo(t):
                    for q in range(8):
                        dve.wait_ge(qk_hi, t * 8 + q + 1)
                        w = (qT, nkT)[q // DC]
                        dve.tensor_tensor(w[:, LO, q % DC, :], bank[(3, 5)[q % 2]][:, 0:NB * S],
                                          w[:, HI, q % DC, :], ALU.subtract).then_inc(qk_lo, 1)

                def new_values_lo(b, k):
                    dve.wait_ge(vn_hi, b + 1)
                    dve.tensor_tensor(Vn[k][:, LO, :], bank[3][0:S, :], Vn[k][:, HI, :],
                                      ALU.subtract).then_inc(vn_lo, 1)

                def attended_lo(b):
                    dve.wait_ge(oT_hi, b + 1)
                    dve.tensor_tensor(oT[:, LO, :, :].rearrange("p c s -> p (c s)"), bank[6][:, 0:DC * S],
                                      oT[:, HI, :, :].rearrange("p c s -> p (c s)"), ALU.subtract).then_inc(oT_lo, 1)

                def add(b, k):
                    dve.wait_ge(wo_ps, b + 1)
                    dve.wait_ge(xres_in[k], dma_count(b, k))
                    dve.scalar_tensor_tensor(out=xres[k][:, :], in0=bank[7][0:S, :], scalar=gains[0:S, 1:2],
                                             in1=xres[k][:, :], op0=ALU.mult, op1=ALU.add).then_inc(x3_done, 1)
                for n in range(NB):
                    norm(n, n % 2, n)
                rows_lo(0)
                project_lo(0)
                keys_lo(0)
                new_values_lo(0, 0)

                def part(t, _):
                    for i in range(NB):
                        b, k = t * NB + i, i % 2
                        dve.wait_ge(s_ps, b + 1)
                        if beyond(b, 2):
                            dve.wait_ge(exp_done, b - 1)
                        st.did(dve.tensor_reduce(nmax[:, k:k + 1], bank[0][0:S, 0:KEYS], axis=AX.X, op=ALU.max,
                                                 negate=True))
                        st.settle()
                        dve.tensor_scalar(nmax[:, k:k + 1], nmax[:, k:k + 1], SCALE, None, ALU.mult
                                          ).then_inc(nmax_done, 1)
                        if i == NB - 1 and not last_of(t, GR):
                            rows_lo(t + 1)
                        if beyond(b, 1):
                            attended_lo(b - 1)
                        if not (last_of(t, GR) and i == NB - 1):
                            keys_lo(b + 1)
                        if beyond(b, 1):
                            add(b - 1, 1 - k)
                        if i == NB - 1 and not last_of(t, GR):
                            project_lo(t + 1)
                        dve.wait_ge(exp_done, b + 1)
                        if beyond(b, 2):
                            dve.wait_ge(o_done, b - 1)
                        dve.reciprocal(rinv[:, k:k + 1], esum[:, k:k + 1]).then_inc(rinv_done, 1)
                        dve.wait_ge(pT_hi, b + 1)
                        dve.tensor_tensor(pT[:, LO, 0:2, :].rearrange("p c s -> p (c s)"), bank[4][:, 0:2 * S],
                                          pT[:, HI, 0:2, :].rearrange("p c s -> p (c s)"), ALU.subtract)
                        dve.tensor_tensor(pT[0:LAST, LO, 2:4, :].rearrange("p c s -> p (c s)"),
                                          bank[4][0:LAST, 2 * S:4 * S],
                                          pT[0:LAST, HI, 2:4, :].rearrange("p c s -> p (c s)"),
                                          ALU.subtract).then_inc(pT_lo, 1)
                        if not (last_of(t, GR) and i == NB - 1):
                            new_values_lo(b + 1, (i + 1) % 2)
                        if not last_of(t, GR):
                            for n in ((0,), (1,), (2, 3), ())[i]:
                                norm(t * NB + NB + n, n % 2, n)
                repeat(dve, st, GR, part, tail=1)
                attended_lo(B - 1)
                add(B - 1, 1)

            @block.tensor
            def _(pe):
                def turn_rows(t):
                    for i in range(NB):
                        pe.wait_ge(xn_done, t * NB + i + 1)
                        if i >= 2:
                            pe.wait_ge(xg_lo, t * NB + i - 1)
                        for c in range(DC):
                            ins = pe.transpose(bank[1 + i % 2][:, c * S:(c + 1) * S], xn[:, i, c * P:(c + 1) * P],
                                               ident[0:S, 0:S])
                        ins.then_inc(x_ps, 1)

                def turn_keys(b, k):
                    pe.wait_ge(crow_in[k], dma_count(b, k, 32))
                    for c in range(DC):
                        if c >= 2:
                            pe.wait_ge(kT_lo, b * DC + c - 1)
                        for r, (t0, rows) in enumerate(CT):
                            ins = pe.transpose(bank[1 + c % 2][:, t0:t0 + rows],
                                               crow[k][0:rows, r, c * P:(c + 1) * P], ident[0:rows, 0:rows])
                        ins.then_inc(kT_ps, 1)

                def project(t):
                    pe.wait_ge(xg_hi, t * NB + NB)
                    pe.wait_ge(xg_lo, t * NB + NB)
                    for q in range(8):
                        if q >= 2:
                            pe.wait_ge(qk_lo, t * 8 + q - 1)
                        w = (wqT, wkT)[q // DC]
                        n = 0
                        for c in range(DC):
                            for a, h in PAIRS:
                                ins = pe.matmul(bank[(3, 5)[q % 2]][:, 0:NB * S],
                                                w[:, h, c, (q % DC) * P:(q % DC + 1) * P], xgT[:, a, c, :],
                                                start=n == 0, stop=n == 11)
                                n += 1
                        ins.then_inc(qk_ps, 1)

                def new_values(b, i):
                    n = 0
                    for c in range(DC):
                        for a, h in PAIRS:
                            ins = pe.matmul(bank[3][0:S, :], xgT[:, a, c, i * S:(i + 1) * S], wvT[:, h, c, :],
                                            start=n == 0, stop=n == 11)
                            n += 1
                    ins.then_inc(vn_ps, 1)

                def turn_attended(b):
                    pe.wait_ge(o_done, b + 1)
                    if beyond(b, 1):
                        pe.wait_ge(oT_lo, b)
                    for c in range(DC):
                        ins = pe.transpose(bank[6][:, c * S:(c + 1) * S], o[:, c * P:(c + 1) * P], ident[0:S, 0:S])
                    ins.then_inc(oT_ps, 1)

                def output(b):
                    pe.wait_ge(oT_hi, b + 1)
                    pe.wait_ge(oT_lo, b + 1)
                    if beyond(b, 1):
                        pe.wait_ge(x3_done, b)
                    n = 0
                    for c in range(DC):
                        for a, h in PAIRS:
                            ins = pe.matmul(bank[7][0:S, :], oT[:, a, c, :], woT[:, h, c, :],
                                            start=n == 0, stop=n == 11)
                            n += 1
                    ins.then_inc(wo_ps, 1)
                turn_rows(0)
                project(0)
                pe.wait_ge(xg_lo, NB)
                turn_keys(0, 0)
                pe.wait_ge(qk_lo, 8)
                new_values(0, 0)

                def part(t, _):
                    for i in range(NB):
                        b, k = t * NB + i, i % 2
                        if i == 0:
                            pe.wait_ge(qk_hi, t * 8 + 8)
                            pe.wait_ge(qk_lo, t * 8 + 8)
                        pe.wait_ge(kT_hi, b * DC + DC)
                        pe.wait_ge(kT_lo, b * DC + DC)
                        if beyond(b, 1):
                            pe.wait_ge(exp_done, b)
                        for at, n_, keys in ((0, CTX, KT), (CTX, S, nkT)):
                            n = 0
                            for c in range(DC):
                                for a, h in PAIRS:
                                    rhs = keys[:, h, c, :] if n_ == CTX else keys[:, h, c, i * S:(i + 1) * S]
                                    ins = pe.matmul(bank[0][0:S, at:at + n_], qT[:, a, c, i * S:(i + 1) * S], rhs,
                                                    start=n == 0, stop=n == 11)
                                    n += 1
                        ins.then_inc(s_ps, 1)
                        if i == NB - 1 and not last_of(t, GR):
                            turn_rows(t + 1)
                            pe.wait_ge(xg_lo, t * NB + 2 * NB)
                        if beyond(b, 1):
                            turn_attended(b - 1)
                        if not (last_of(t, GR) and i == NB - 1):
                            turn_keys(b + 1, (i + 1) % 2)
                        if beyond(b, 1):
                            output(b - 1)
                        if i == NB - 1 and not last_of(t, GR):
                            pe.wait_ge(vn_lo, b + 1)
                            project(t + 1)
                        pe.wait_ge(exp_done, b + 1)
                        if beyond(b, 1):
                            pe.wait_ge(pT_lo, b)
                        for r, (t0, rows) in enumerate(VC):
                            rows = LAST if r == 3 else rows
                            ins = pe.transpose(bank[4][0:rows, r * S:(r + 1) * S], prob[:, t0:t0 + rows],
                                               ident[0:S, 0:S])
                        ins.then_inc(pT_ps, 1)
                        if not (last_of(t, GR) and i == NB - 1):
                            if i == NB - 1:
                                pe.wait_ge(qk_lo, t * 8 + 16)
                            else:
                                pe.wait_ge(vn_lo, b + 1)
                            new_values(b + 1, (i + 1) % NB)
                        pe.wait_ge(pT_hi, b + 1)
                        pe.wait_ge(pT_lo, b + 1)
                        pe.wait_ge(v_lo, b + 1)
                        pe.wait_ge(vn_lo, b + 1)
                        if beyond(b, 1):
                            pe.wait_ge(o_done, b)
                        n = 0
                        for r, (_, rows) in enumerate(VC):
                            for a, h in PAIRS:
                                rhs = Vn[k][:, h, :] if r == 3 else V[0:rows, h, r, :]
                                ins = pe.matmul(bank[5][0:S, :], pT[0:rows, a, r, :], rhs,
                                                start=n == 0, stop=n == 11)
                                n += 1
                        ins.then_inc(pv_ps, 1)
                repeat(pe, Steps(pe, None), GR, part, tail=1)
                turn_attended(B - 1)
                output(B - 1)


def mx_phase(nc, g, x3_d, out_f):
    ident, gains, bank = g["ident"], g["gains"], g["bank"]
    gateT, upT, downT = g["gateT"], g["upT"], g["downT"]
    HF = F // 2
    with ExitStack() as es:
        def sb(name, shape, dt=F32):
            return es.enter_context(nc.sbuf_tensor(name, shape, dt))

        def sem(name):
            return nc.alloc_semaphore(f"mx_{name}")

        xin = [sb(f"mxin{k}", [P, D]) for k in range(2)]
        xres = [sb(f"mxres{k}", [P, D]) for k in range(2)]
        xn, xr, xm, xq = (sb(n, [P, D]) for n in ("mxn", "mxr", "mxm", "mxq"))
        xqT = [sb(f"xqT{k}", [P, 2, DC, P], BF16) for k in range(2)]
        xamax, xscale, xinv = (sb(n, [P, D // MXB]) for n in ("xamax", "xscale", "xinv"))
        stats, mv, rstd, power = sb("mstats", [P, 6]), sb("mmv", [P, 2]), sb("mrstd", [P, 1]), sb("mpower", [P, 1])
        act_g = [sb(f"mact{k}", [P, D]) for k in range(2)]
        hraw, hr, hm, hq = (sb(n, [P, HF]) for n in ("hraw", "hr", "hm", "hq"))
        hamax, hscale, hinv = (sb(n, [P, HF // MXB]) for n in ("hamax", "hscale", "hinv"))
        hT = sb("mhT", [P, 2, 8, P], BF16)
        xin_in, xres_in, out_sent = ([sem(f"{n}{k}") for k in range(2)] for n in (
            "mxin_in", "mxres_in", "out_sent"))
        dve_c, pool_c, power_set = sem("dve_c6"), sem("pool_c6"), sem("power_set")
        stat_done, rstd_done, xn_done = sem("mstat"), sem("mrstd_done"), sem("mxn_done")
        xround_done, xdq_done, x_ps, xq_hi, xq_lo = (sem(n) for n in (
            "xround_done", "xdq_done", "mx_ps", "xq_hi", "xq_lo"))
        gu_ps, silu_done, h_done = sem("mgu_ps"), sem("msilu"), sem("mh_done")
        hround_done, hdq_done, hT_ps, hT_hi, hT_lo = (sem(n) for n in (
            "hround_done", "hdq_done", "mhT_ps", "mhT_hi", "mhT_lo"))
        y_ps, y_done = sem("y_ps"), sem("y_done")

        def dma_count(t, k):
            return t * 8 + (16 if k == 0 else 8)

        with nc.Block() as block:
            @block.sync
            def _(sp):
                def load(dst, t, k, signal):
                    sp.dma_start(dst[k][:, :], x3_d[bass.ds(t * P, P), :]).then_inc(signal[k], 16)
                for k in range(2):
                    load(xin, k, k, xin_in)
                    load(xres, k, k, xres_in)

                def part(t, k):
                    if not isinstance(t, int) or t < NT - 2:
                        sp.wait_ge(xn_done, t + 1)
                        load(xin, t + 2, k, xin_in)
                    sp.wait_ge(y_done, t + 1)
                    sp.dma_start(out_f[bass.ds(t * P, P), :], xres[k][:, :]).then_inc(out_sent[k], 16)
                    if not isinstance(t, int) or t < NT - 2:
                        sp.wait_ge(out_sent[k], dma_count(t, k))
                        load(xres, t + 2, k, xres_in)
                repeat(sp, Steps(sp, None), NT, part, unroll=2, tail=3)
                sp.wait_ge(out_sent[0], (NT + 1) // 2 * 16)
                sp.wait_ge(out_sent[1], NT // 2 * 16)

            @block.gpsimd
            def _(pool):
                st = Steps(pool, pool_c)
                pool.memset(power[:, :], -0.5).then_inc(power_set, 1)
                pool.wait_ge(power_set, 1)

                def rows(t):
                    pool.wait_ge(stat_done, t + 1)
                    apart(pool)
                    rsqrt(pool, st, rstd[:, :], mv[:, 1:2], power[:, :], rstd_done)
                    pool.wait_ge(xround_done, t + 1)
                    if later(t, 1):
                        pool.wait_ge(x_ps, t)
                    pool.tensor_tensor(blocks(xq[:, :]), blocks(xr[:, :]), wide(xscale[:, :], MXB),
                                       ALU.mult).then_inc(xdq_done, 1)
                rows(0)

                def part(t, _):
                    if not last_of(t, NT):
                        rows(t + 1)
                    for j in range(2):
                        q = 2 * t + j
                        pool.wait_ge(hround_done, q + 1)
                        if later(t, 1) or j:
                            pool.wait_ge(hT_ps, 2 * q)
                        pool.tensor_tensor(blocks(hq[:, :]), blocks(hr[:, :]), wide(hscale[:, :], MXB),
                                           ALU.mult).then_inc(hdq_done, 1)
                repeat(pool, st, NT, part, tail=1)

            @block.scalar
            def _(act):
                def rows_hi(t, k):
                    act.wait_ge(x_ps, t + 1)
                    act.activation(xqT[k][:, HI, :, :].rearrange("p c s -> p (c s)"), bank[7][:, :],
                                   ACT.Copy).then_inc(xq_hi, 1)

                def hidden_hi(q):
                    for v in range(2):
                        act.wait_ge(hT_ps, 2 * q + v + 1)
                        act.activation(hT[:, HI, 4 * v:4 * v + 4, :].rearrange("p c s -> p (c s)"),
                                       bank[4 + v][:, :], ACT.Copy).then_inc(hT_hi, 1)
                rows_hi(0, 0)

                def part(t, k):
                    for j in range(2):
                        q = 2 * t + j
                        for v in range(2):
                            act.wait_ge(gu_ps, 2 * q + v + 1)
                            act.activation(act_g[v][:, :], bank[v][:, :], ACT.Silu).then_inc(silu_done, 1)
                            if v == 0 and j == 1 and not last_of(t, NT):
                                rows_hi(t + 1, 1 - k)
                        if later(t, 1) or j:
                            hidden_hi(q - 1)
                repeat(act, Steps(act, None), NT, part, unroll=2, tail=1)
                hidden_hi(2 * NT - 1)

            @block.vector
            def _(dve):
                st = Steps(dve, dve_c)

                def rows(t, k):
                    dve.wait_ge(xin_in[k], dma_count(t, k))
                    st.did(dve.bn_stats(stats[:, :], xin[k][:, :]))
                    st.settle(alone=True)
                    dve.bn_aggr(mv[:, :], stats[:, :]).then_inc(stat_done, 1)
                    dve.wait_ge(rstd_done, t + 1)
                    dve.tensor_scalar(xn[:, :], xin[k][:, :], mv[:, 0:1], rstd[:, 0:1],
                                      ALU.subtract, ALU.mult).then_inc(xn_done, 1)
                    dve.wait_ge(xn_done, t + 1)
                    if later(t, 1):
                        dve.wait_ge(xdq_done, t)
                    mx_scales(dve, st, xn[:, :], xamax[:, :], xscale[:, :], xinv[:, :])
                    mx_round(dve, st, xn[:, :], xinv[:, :], xr[:, :], xm[:, :])
                    dve.tensor_tensor(xr[:, :], xr[:, :], xm[:, :], ALU.subtract).then_inc(xround_done, 1)

                def rows_lo(t, k):
                    dve.wait_ge(xq_hi, t + 1)
                    dve.tensor_tensor(xqT[k][:, LO, :, :].rearrange("p c s -> p (c s)"), bank[7][:, :],
                                      xqT[k][:, HI, :, :].rearrange("p c s -> p (c s)"),
                                      ALU.subtract).then_inc(xq_lo, 1)

                def hidden_lo(q):
                    for v in range(2):
                        dve.wait_ge(hT_hi, 2 * q + v + 1)
                        dve.tensor_tensor(hT[:, LO, 4 * v:4 * v + 4, :].rearrange("p c s -> p (c s)"),
                                          bank[4 + v][:, :],
                                          hT[:, HI, 4 * v:4 * v + 4, :].rearrange("p c s -> p (c s)"),
                                          ALU.subtract).then_inc(hT_lo, 1)

                def add(t, k):
                    dve.wait_ge(y_ps, t + 1)
                    dve.wait_ge(xres_in[k], dma_count(t, k))
                    row = xres[k][:, :].rearrange("p (q r) -> p r q", r=4)
                    dve.scalar_tensor_tensor(out=row, in0=bank[6][:, :].rearrange("p (r q) -> p r q", r=4),
                                             scalar=gains[:, 3:4], in1=row, op0=ALU.mult, op1=ALU.add
                                             ).then_inc(y_done, 1)
                rows(0, 0)
                rows_lo(0, 0)

                def part(t, k):
                    for j in range(2):
                        q = 2 * t + j
                        for v in range(2):
                            dve.wait_ge(silu_done, 2 * q + v + 1)
                            dve.tensor_tensor(hraw[:, v * D:(v + 1) * D], act_g[v][:, :], bank[2 + v][:, :],
                                              ALU.mult).then_inc(h_done, 1)
                            if v == 0 and j == 0 and not last_of(t, NT):
                                rows(t + 1, 1 - k)
                            if v == 0 and j == 1:
                                if not last_of(t, NT):
                                    rows_lo(t + 1, 1 - k)
                                if later(t, 1):
                                    add(t - 1, 1 - k)
                        if later(t, 1) or j:
                            hidden_lo(q - 1)
                            dve.wait_ge(hdq_done, q)
                        dve.wait_ge(h_done, 2 * q + 2)
                        mx_scales(dve, st, hraw[:, :], hamax[:, :], hscale[:, :], hinv[:, :])
                        mx_round(dve, st, hraw[:, :], hinv[:, :], hr[:, :], hm[:, :])
                        dve.tensor_tensor(hr[:, :], hr[:, :], hm[:, :], ALU.subtract).then_inc(hround_done, 1)
                repeat(dve, st, NT, part, unroll=2, tail=1)
                hidden_lo(2 * NT - 1)
                add(NT - 1, (NT - 1) % 2)

            @block.tensor
            def _(pe):
                def turn_rows(t):
                    pe.wait_ge(xdq_done, t + 1)
                    if later(t, 1):
                        pe.wait_ge(xq_lo, t)
                    for c in range(DC):
                        ins = pe.transpose(bank[7][:, c * P:(c + 1) * P], xq[:, c * P:(c + 1) * P], ident[:, :])
                    ins.then_inc(x_ps, 1)

                def gate_up(t, k, j, v):
                    q = 2 * t + j
                    if later(t, 1) or j:
                        pe.wait_ge(h_done, 2 * q + v - 1)
                    i0 = j * HF + v * D
                    for u, w in enumerate((gateT, upT)):
                        n = 0
                        for c in range(DC):
                            for a, h in PAIRS:
                                ins = pe.matmul(bank[2 * u + v][:, :], xqT[k][:, a, c, :], w[:, h, c, i0:i0 + D],
                                                start=n == 0, stop=n == 11)
                                n += 1
                    ins.then_inc(gu_ps, 1)

                def turn_hidden(q):
                    pe.wait_ge(hdq_done, q + 1)
                    for v in range(2):
                        if later(q, 1):
                            pe.wait_ge(hT_lo, 2 * q - 1 + v)
                        for c in range(4):
                            at = (4 * v + c) * P
                            ins = pe.transpose(bank[4 + v][:, c * P:(c + 1) * P], hq[:, at:at + P], ident[:, :])
                        ins.then_inc(hT_ps, 1)

                def down(t, j):
                    pe.wait_ge(hT_hi, 4 * t + 2 * j + 2)
                    pe.wait_ge(hT_lo, 4 * t + 2 * j + 2)
                    if j == 0 and later(t, 1):
                        pe.wait_ge(y_done, t)
                    n = 0
                    for c in range(8):
                        for a, h in PAIRS:
                            ins = pe.matmul(bank[6][:, :].rearrange("p (r q) -> p r q", r=4), hT[:, a, c, :],
                                            downT[:, h, 2 * j + c // 4:16:4, c % 4, :],
                                            start=n == 0 and j == 0, stop=n == 23 and j == 1)
                            n += 1
                    if j == 1:
                        ins.then_inc(y_ps, 1)
                turn_rows(0)

                def part(t, k):
                    pe.wait_ge(xq_hi, t + 1)
                    pe.wait_ge(xq_lo, t + 1)
                    for j in range(2):
                        gate_up(t, k, j, 0)
                        if later(t, 1):
                            down(t - 1, j)
                        if j == 1 and not last_of(t, NT):
                            turn_rows(t + 1)
                        gate_up(t, k, j, 1)
                        if later(t, 1) or j:
                            turn_hidden(2 * t + j - 1)
                repeat(pe, Steps(pe, None), NT, part, unroll=2, tail=1)
                down(NT - 1, 0)
                turn_hidden(2 * NT - 1)
                down(NT - 1, 1)


_INS = ["x", "ctx_2048", "g_xattn", "g_ffn", "L0_xattn_decay", "L0_xattn_W_in", "L0_xattn_b_in",
        "L0_xattn_W_out", "L0_xattn_b_out", "L0_xattn_gamma", "L0_xattn_beta", "L0_ffn_gate_w",
        "L0_ffn_w_gate", "L0_ffn_w_up", "L0_ffn_w_down", "L0_ffn_ws_gate", "L0_ffn_ws_up",
        "L0_ffn_ws_down", "L1_xattn_wq", "L1_xattn_wk", "L1_xattn_wv", "L1_xattn_wo",
        "L1_ffn_gate_w", "L1_ffn_up_w", "L1_ffn_down_w"]


def kernel(**inputs):
    import numpy as np
    import concourse.bacc as bacc
    from concourse.bass_utils import run_bass_kernel_spmd

    nc = bacc.Bacc("TRN2", target_bir_lowering=False, num_devices=1)
    arrays, args = {}, []
    for name in _INS:
        a = np.ascontiguousarray(inputs[name])
        if a.ndim == 0:
            a = a.reshape(1)
        arrays[f"in_{name}"] = a
        args.append(nc.dram_tensor(f"in_{name}", a.shape, mybir.dt.from_np(a.dtype), kind="ExternalInput").ap())
    out = nc.dram_tensor("out_0", (B, S, D), F32, kind="ExternalOutput").ap()
    program(nc, *args, out)
    r = run_bass_kernel_spmd(nc, [arrays], core_ids=[0])
    return r.results[0]["out_0"]
```

```python
from contextlib import ExitStack

import concourse.bass as bass
from concourse import mybir

F32 = mybir.dt.float32
BF16 = mybir.dt.bfloat16
U32 = mybir.dt.uint32
I32 = mybir.dt.int32
ALU = mybir.AluOpType
ACT = mybir.ActivationFunctionType
AX = mybir.AxisListType

P = 128
B, S, D = 32, 100, 512
TOK = B * S
NT = TOK // P
DC = D // P
CTX = 361
CT = [(0, 128), (128, 128), (256, CTX - 256)]
LAST = CTX - 256
E, I, CAP = 16, 352, 256
IC = [(0, 128), (128, 128), (256, I - 256)]
IS = 704
SC = [(128 * m, min(128, IS - 128 * m)) for m in range(6)]
F = 2048
GT = 5
NG = NT // GT
LN_EPS = 1e-5
FP8_MAX, MX_EPS, MXB = 448.0, 1e-30, 32
HI, LO = 0, 1
PAIRS = [(HI, HI), (HI, LO), (LO, HI)]


class Steps:

    def __init__(self, eng, sem):
        self.eng, self.sem, self.n, self.base = eng, sem, 0, 0

    def did(self, ins):
        ins.then_inc(self.sem, 1)
        self.n += 1

    def settle(self, alone=False):
        self.eng.wait_ge(self.sem, self.base + self.n)
        if alone:
            apart(self.eng)


def apart(eng):
    eng.nop(nofuse=True)


def repeat(eng, steps, count, body, unroll=1, head=0, tail=0):
    start = max(head, unroll)
    for t in range(start):
        n0 = steps.n
        body(t, t % unroll)
        per = steps.n - n0
    end = start + (count - start - tail) // unroll * unroll
    if end > start:
        n1 = steps.n
        with eng.Fori(start, end - unroll + 1, unroll) as t:
            steps.base = (t - start) * per
            for k in range(unroll):
                body(t + k if k else t, k)
        steps.base, steps.n = 0, n1 + (end - start) * per
    for t in range(end, count):
        body(t, t % unroll)


def later(t, n):
    return not isinstance(t, int) or t >= n


def wide(ap, n):
    return ap.unsqueeze(2).to_broadcast([ap.shape[0], ap.shape[1], n])


def blocks(ap, n=MXB):
    return ap.rearrange("p (b n) -> p b n", n=n)


def mx_scales(dve, st, src, amax, scale, inv):
    st.did(dve.tensor_reduce(amax, blocks(src), axis=AX.X, op=ALU.max, apply_absolute_value=True))
    st.settle()
    st.did(dve.tensor_scalar(scale, amax, 1.0 / FP8_MAX, MX_EPS, ALU.mult, ALU.max))
    st.settle()
    st.did(dve.reciprocal(inv, scale))
    st.settle()


def mx_round(dve, st, src, inv, r, m):
    st.did(dve.tensor_tensor(blocks(r), blocks(src), wide(inv, MXB), ALU.mult))
    st.settle()
    st.did(dve.tensor_scalar(m.bitcast(U32), r.bitcast(U32), 0x7F800000, 0xFFFFFFFF,
                             ALU.bitwise_and, ALU.bitwise_and))
    st.settle()
    st.did(dve.tensor_scalar(m, m, 2.0 ** -6, 1.5 * 2.0 ** 20, ALU.max, ALU.mult))
    st.settle()
    st.did(dve.tensor_tensor(r, r, m, ALU.add))
    st.settle()


def program(nc, x, ctx, g_xattn, g_ffn, decay, W_in, b_in, W_out, b_out, gamma, beta,
            gate_w, w_gate, w_up, w_down, ws_gate, ws_up, ws_down,
            wq, wk, wv, wo, gate2, up2, down2, out):
    x1_d = nc.dram_tensor("x1_d", (TOK, D), F32, kind="Internal").ap()
    x2_d = nc.dram_tensor("x2_d", (TOK, D), F32, kind="Internal").ap()
    x3_d = nc.dram_tensor("x3_d", (TOK, D), F32, kind="Internal").ap()
    xs_d = nc.dram_tensor("xs_d", (TOK, D), F32, kind="Internal").ap()
    pick_d = nc.dram_tensor("pick_d", (TOK, 4), U32, kind="Internal").ap()
    slots_d = nc.dram_tensor("slots_d", (E * CAP, 2 * D), BF16, kind="Internal").ap()
    eout_d = nc.dram_tensor("eout_d", (E * CAP, D), F32, kind="Internal").ap()
    x_f = x.rearrange("b s d -> (b s) d")
    out_f = out.rearrange("b s d -> (b s) d")
    with ExitStack() as keep:
        def sb(name, shape, dt=F32):
            return keep.enter_context(nc.sbuf_tensor(name, shape, dt))

        g = {}
        g["ident"] = sb("ident", [P, P])
        g["identb"] = sb("identb", [P, P], BF16)
        g["gains"] = sb("gains", [P, 4])
        g["gateT"] = sb("gateT", [P, 2, DC, F], BF16)
        g["upT"] = sb("upT", [P, 2, DC, F], BF16)
        g["bank"] = [keep.enter_context(nc.psum_tensor(f"bank{i}", [P, 512], F32)) for i in range(8)]
        with ExitStack() as l0:
            g["summary"] = l0.enter_context(nc.sbuf_tensor("summary", [B, 3, D], BF16))
            with nc.cleanup_on_exit():
                summary_phase(nc, g, ctx, g_xattn, g_ffn, decay, W_in, b_in, W_out, b_out,
                              gate2, up2, slots_d)
            with nc.cleanup_on_exit():
                route_phase(nc, g, x_f, gamma, beta, gate_w, ws_gate, ws_up, ws_down,
                            x1_d, xs_d, pick_d, slots_d)
        g["downT"] = sb("downT", [P, 2, 16, DC, P], BF16)
        with nc.cleanup_on_exit():
            expert_phase(nc, g, w_gate, w_up, w_down, down2, slots_d, eout_d)
        with nc.cleanup_on_exit():
            attention_phase(nc, g, ctx, wq, wk, wv, wo, xs_d, pick_d, eout_d, x2_d, x3_d)
        with nc.cleanup_on_exit():
            mx_phase(nc, g, x3_d, out_f)


def summary_phase(nc, g, ctx, g_xattn, g_ffn, decay, W_in, b_in, W_out, b_out,
                  gate2, up2, slots_d):
    ident, identb, gains, bank = g["ident"], g["identb"], g["gains"], g["bank"]
    summary = g["summary"]
    with ExitStack() as es:
        def sb(name, shape, dt=F32):
            return es.enter_context(nc.sbuf_tensor(name, shape, dt))

        def sem(name):
            return nc.alloc_semaphore(f"summary_{name}")

        crow = [sb(f"crow{k}", [P, 3, D]) for k in range(4)]
        wrow = sb("wrow", [P, CTX])
        kcol = sb("kcol", [P, 2])
        krow = sb("krow", [P, CTX])
        diag = sb("diag", [P, 3, CTX])
        picked = sb("picked", [P, CTX])
        wsum = sb("wsum", [P, 4])
        wstage = [sb(f"wstage{k}", [P, 2, D]) for k in range(2)]
        wr = [sb(f"wr{k}", [P, 2, D]) for k in range(2)]
        wm = sb("wm", [P, 2, D])
        dq = [sb(f"dq{k}", [P, 2, D]) for k in range(2)]
        scale = [sb(f"scale{k}", [P, 32]) for k in range(2)]
        amax, inv = sb("amax", [P, 32]), sb("inv", [P, 32])
        zeros = sb("zeros", [P, D], BF16)
        bias2 = sb("bias2", [B, 2, D])
        WT = [sb(f"WT{k}", [P, DC, D]) for k in range(2)]
        sumrow = sb("sumrow", [B, 2, D])
        sumT = [sb(f"sumT{n}", [P, DC, B]) for n in range(2)]
        left = sb("left", [B, D])
        slots_zero, gains_in, bias_in, sq_in = sem("slots_zero"), sem("gains_in"), sem("bias_in"), sem("sq_in")
        row_a = [sem(f"row_a{k}") for k in range(4)]
        wst_in = [sem(f"wst_in{k}") for k in range(2)]
        pool_c, dve_c, act_tanh = sem("pool_c"), sem("dve_c"), sem("act_tanh")
        zero_set = sem("zero_set")
        win_ready = sem("win_ready")
        row_mm = sem("row_mm")
        round_done, dq_done, wT_ps, wT_hi, wT_lo = (sem(n) for n in (
            "round_done", "dq_done", "wT_ps", "wT_hi", "wT_lo"))
        sq_ps, sq_ev, fin_ps, fin_act, fin_dve = (sem(n) for n in (
            "sq_ps", "sq_ev", "fin_ps", "fin_act", "fin_dve"))
        sqs = [sb(f"square{n}", [P, DC, D]) for n in range(2)]
        with nc.Block() as block:
            @block.sync
            def _(sp):
                for n, src in enumerate((g_xattn, g_ffn)):
                    sp.dma_start(gains[:, 2 * n:2 * n + 2],
                                 src.rearrange("(a n) -> a n", a=1).to_broadcast([P, 2])).then_inc(gains_in, 16)
                sp.dma_start(kcol[:, 0:1],
                             decay.rearrange("(a n) -> a n", a=1).to_broadcast([P, 1])).then_inc(gains_in, 16)
                for n, src in enumerate((b_in, b_out)):
                    sp.dma_start(bias2[:, n, :],
                                 src.rearrange("(a n) -> a n", a=1).to_broadcast([B, D])).then_inc(bias_in, 16)

                def load(t, k):
                    if later(t, 2):
                        sp.wait_ge(round_done, t - 1)
                    sp.dma_start(wstage[k][:, 0, :], gate2[bass.ds(t * P, P), :]).then_inc(wst_in[k], 16)
                    sp.dma_start(wstage[k][:, 1, :], up2[bass.ds(t * P, P), :]).then_inc(wst_in[k], 16)
                    for i in range(2):
                        b = 2 * t + i
                        if later(t, 2):
                            sp.wait_ge(row_mm, 2 * t - 3 + i)
                        row = ctx[bass.ds(b, 1), :, :].rearrange("a t d -> (a t) d")
                        sp.dma_start(crow[2 * k + i][:, 0:2, :],
                                     row[0:256, :].rearrange("(c p) d -> p c d", p=P)).then_inc(row_a[2 * k + i], 16)
                        sp.dma_start(crow[2 * k + i][0:LAST, 2, :], row[256:CTX, :]).then_inc(row_a[2 * k + i], 16)
                    if isinstance(t, int) and t == 0:
                        sp.wait_ge(zero_set, 1)
                    sp.dma_start(slots_d.rearrange("r (h n) -> (r h) n", h=2)[bass.ds(t * 2 * CAP, 2 * CAP), :]
                                 .rearrange("(a p) n -> p a n", p=P),
                                 zeros[:, :].unsqueeze(1).to_broadcast([P, 2 * CAP // P, D])
                                 ).then_inc(slots_zero, 16)
                    if isinstance(t, int) and t == 1:
                        for n, src in enumerate((W_in, W_out)):
                            sp.dma_start(sqs[n][:, :, :], src.rearrange("(c p) n -> p c n", p=P)).then_inc(sq_in, 16)
                repeat(sp, Steps(sp, None), 16, load, unroll=2)
                sp.wait_ge(slots_zero, E * 16)

            @block.gpsimd
            def _(pool):
                st = Steps(pool, pool_c)
                st.did(pool.memset(zeros[:, :], 0.0))
                st.did(pool.memset(ident[:, :], 0.0))
                st.did(pool.memset(diag[:, :, :], 0.0))
                st.settle()
                pool.affine_select(out=ident[:, :], in_=ident[:, :], compare_op=ALU.not_equal, fill=1.0,
                                   base=0, pattern=[[-1, P]], channel_multiplier=1).then_inc(zero_set, 1)
                pool.affine_select(out=diag[:, :, :], in_=diag[:, :, :], compare_op=ALU.not_equal, fill=1.0,
                                   base=1 - CTX, pattern=[[P, 3], [1, CTX]], channel_multiplier=1
                                   ).then_inc(zero_set, 1)
                pool.wait_ge(zero_set, 2)
                pool.tensor_copy(identb[:, :], ident[:, :]).then_inc(zero_set, 1)

                def part(t, k):
                    pool.wait_ge(round_done, t + 1)
                    if later(t, 2):
                        pool.wait_ge(wT_ps, 2 * t - 2)
                    pool.tensor_tensor(blocks(dq[k][:, :, :].rearrange("p a n -> p (a n)")),
                                       blocks(wr[k][:, :, :].rearrange("p a n -> p (a n)")),
                                       wide(scale[k][:, :], MXB), ALU.mult).then_inc(dq_done, 1)
                repeat(pool, Steps(pool, None), 16, part, unroll=2)

            @block.scalar
            def _(act):
                act.wait_ge(gains_in, 48)
                act.activation(gains[:, :], gains[:, :], ACT.Tanh).then_inc(act_tanh, 1)
                act.activation(kcol[:, 1:2], kcol[:, 0:1], ACT.Tanh, scale=0.5).then_inc(act_tanh, 1)

                def part(t, _):
                    for n in range(2):
                        act.wait_ge(wT_ps, 2 * t + n + 1)
                        act.activation((g["gateT"], g["upT"])[n][:, HI, :, bass.ds(t * P, P)],
                                       bank[1 + n][:, :].rearrange("p (c i) -> p c i", c=DC),
                                       ACT.Copy).then_inc(wT_hi, 1)
                    if isinstance(t, int) and t == 14:
                        for n in range(8):
                            act.wait_ge(sq_ps, n + 1)
                            act.activation(WT[n // 4][:, n % 4, :], bank[4 + n % 4][:, :], ACT.Copy
                                           ).then_inc(sq_ev, 1)
                repeat(act, Steps(act, None), 16, part, unroll=2, tail=2)
                act.wait_ge(row_mm, B)
                act.activation(sumT[0][:, :, :], bank[0][:, 0:DC * B].rearrange("p (c b) -> p c b", c=DC),
                               ACT.Copy).then_inc(fin_act, 1)
                act.wait_ge(fin_ps, 2)
                act.activation(sumT[1][:, :, :], bank[5][:, 0:DC * B].rearrange("p (c b) -> p c b", c=DC),
                               ACT.Copy).then_inc(fin_act, 1)

            @block.vector
            def _(dve):
                st = Steps(dve, dve_c)
                st.did(dve.memset(krow[:, :], 1.0))
                dve.wait_ge(act_tanh, 2)
                st.did(dve.tensor_scalar(kcol[:, 0:1], kcol[:, 1:2], 0.5, 0.5, ALU.mult, ALU.add))
                st.settle()
                st.did(dve.tensor_scalar(picked[:, :], krow[:, :], kcol[:, 0:1], None, ALU.mult))
                st.settle()
                st.did(dve.tensor_tensor_scan(wrow[:, :], picked[:, :], krow[:, :], 0.0, ALU.mult, ALU.add))
                st.settle()
                st.did(dve.tensor_scalar(wrow[:, :], wrow[:, :], 1.0 / CTX, None, ALU.mult))
                st.settle()
                dve.wait_ge(zero_set, 2)
                for c in range(3):
                    st.did(dve.tensor_tensor(picked[:, :], wrow[:, :], diag[:, c, :], ALU.mult))
                    st.settle()
                    st.did(dve.tensor_reduce(wsum[:, c:c + 1], picked[:, :], axis=AX.X, op=ALU.add))
                    st.settle()
                st.did(dve.tensor_reduce(wsum[:, 3:4], wrow[:, :], axis=AX.X, op=ALU.add))
                st.settle()
                dve.nop(nofuse=True).then_inc(win_ready, 1)

                def low(t):
                    for n in range(2):
                        dve.wait_ge(wT_hi, 2 * t + n + 1)
                        w = (g["gateT"], g["upT"])[n]
                        dve.tensor_tensor(w[:, LO, :, bass.ds(t * P, P)],
                                          bank[1 + n][:, :].rearrange("p (c i) -> p c i", c=DC),
                                          w[:, HI, :, bass.ds(t * P, P)], ALU.subtract).then_inc(wT_lo, 1)

                def part(t, k):
                    dve.wait_ge(wst_in[k], t * 16 + (32 if k == 0 else 16))
                    if later(t, 2):
                        dve.wait_ge(dq_done, t - 1)
                    flat, r, m = (v[:, :, :].rearrange("p a n -> p (a n)") for v in (wstage[k], wr[k], wm))
                    mx_scales(dve, st, flat, amax[:, :], scale[k][:, :], inv[:, :])
                    mx_round(dve, st, flat, inv[:, :], r, m)
                    dve.tensor_tensor(r, r, m, ALU.subtract).then_inc(round_done, 1)
                    if later(t, 1):
                        low(t - 1)
                    dve.wait_ge(round_done, t + 1)
                repeat(dve, st, 16, part, unroll=2)
                low(15)
                dve.wait_ge(bias_in, 32)
                st.did(dve.tensor_scalar(bias2[:, 0, :], bias2[:, 0, :], wsum[0:B, 3:4], None, ALU.mult))
                st.settle()
                for n in range(2):
                    dve.wait_ge(fin_ps, 1 + 2 * n)
                    dve.tensor_tensor(sumrow[:, n, :], bank[6 + n][0:B, :], bias2[:, n, :],
                                      ALU.add).then_inc(fin_dve, 1)
                dve.wait_ge(fin_dve, 2)
                st.did(dve.tensor_copy(summary[:, 0, :], sumrow[:, 1, :]))
                st.settle()
                st.did(dve.tensor_tensor(left[:, :], sumrow[:, 1, :], summary[:, 0, :], ALU.subtract))
                st.settle()
                st.did(dve.tensor_copy(summary[:, 1, :], left[:, :]))
                st.settle()
                st.did(dve.tensor_tensor(summary[:, 2, :], left[:, :], summary[:, 1, :], ALU.subtract))

            @block.tensor
            def _(pe):
                pe.wait_ge(zero_set, 1)
                pe.wait_ge(win_ready, 1)

                def part(t, k):
                    for i in range(2):
                        pe.wait_ge(row_a[2 * k + i], t * 16 + (32 if k == 0 else 16))
                        for c in range(DC):
                            for r, (_, rows) in enumerate(CT):
                                ins = pe.matmul(bank[0][:, bass.ds(2 * t + (c * B + i), 1)],
                                                crow[2 * k + i][0:rows, r, c * P:(c + 1) * P], wsum[0:rows, r:r + 1],
                                                start=r == 0, stop=r == len(CT) - 1)
                        ins.then_inc(row_mm, 1)
                    pe.wait_ge(dq_done, t + 1)
                    for n in range(2):
                        if later(t, 1):
                            pe.wait_ge(wT_lo, 2 * t - 1 + n)
                        for c in range(DC):
                            ins = pe.transpose(bank[1 + n][:, c * P:(c + 1) * P], dq[k][:, n, c * P:(c + 1) * P],
                                               ident[:, :])
                        ins.then_inc(wT_ps, 1)
                    if isinstance(t, int) and t == 14:
                        squares()

                def squares():
                    pe.wait_ge(sq_in, 32)
                    for n in range(2):
                        for c in range(DC):
                            if n:
                                pe.wait_ge(sq_ev, c + 1)
                            for r in range(DC):
                                ins = pe.transpose(bank[4 + c][:, r * P:(r + 1) * P],
                                                   sqs[n][:, r, c * P:(c + 1) * P], ident[:, :])
                            ins.then_inc(sq_ps, 1)
                repeat(pe, Steps(pe, None), 16, part, unroll=2, tail=2)
                pe.wait_ge(sq_ev, 8)
                for n in range(2):
                    if n:
                        pe.wait_ge(fin_dve, 1)
                        for c in range(DC):
                            ins = pe.transpose(bank[5][:, c * B:(c + 1) * B], sumrow[:, 0, c * P:(c + 1) * P],
                                               ident[0:B, 0:B])
                        ins.then_inc(fin_ps, 1)
                    pe.wait_ge(fin_act, 1 + n)
                    for c in range(DC):
                        ins = pe.matmul(bank[6 + n][0:B, :], sumT[n][:, c, :], WT[n][:, c, :],
                                        start=c == 0, stop=c == DC - 1)
                    ins.then_inc(fin_ps, 1)


def row_stats(dve, st, src, stats, mv, count, done=None):
    for j in range(count):
        st.did(dve.bn_stats(stats[:, j, :], src(j)))
    st.settle(alone=True)
    for j in range(count - 1):
        st.did(dve.bn_aggr(mv[:, j, :], stats[:, j, :]))
    dve.bn_aggr(mv[:, count - 1, :], stats[:, count - 1, :]).then_inc(done, 1)


def rsqrt(pool, st, rstd, mv, power, done):
    st.did(pool.tensor_scalar(rstd, mv, LN_EPS, None, ALU.add))
    st.settle()
    pool.tensor_tensor(rstd, rstd, power, ALU.pow).then_inc(done, 1)


def last_of(t, count):
    return isinstance(t, int) and t == count - 1


def route_phase(nc, g, x_f, gamma, beta, gate_w, ws_gate, ws_up, ws_down, x1_d, xs_d, pick_d, slots_d):
    ident, gains, bank, summary = g["ident"], g["gains"], g["bank"], g["summary"]
    SUBS = [(0, 3), (3, 2)]
    NQ = 12
    TURN = (0, 1, 2, 3, 6)
    RANK = P
    with ExitStack() as es:
        def sb(name, shape, dt=F32):
            return es.enter_context(nc.sbuf_tensor(name, shape, dt))

        def sem(name):
            return nc.alloc_semaphore(f"route_{name}")

        x, y, xr = sb("x", [P, GT, D]), sb("y", [P, GT, D]), sb("xr", [P, GT, D])
        rows = sb("rows", [P, GT, 2, D], BF16)
        xT = sb("xT", [P, GT, 2, DC, P], BF16)
        gamma_b, beta_b = sb("gamma_b", [P, D]), sb("beta_b", [P, D])
        own = sb("own", [B, TOK], BF16)
        before, ones = sb("before", [P, P], BF16), sb("ones", [P, P], BF16)
        iota_i, iota_f = sb("iota_i", [P, E], I32), sb("iota_f", [P, E])
        gw = sb("gw", [E, D])
        gwT = sb("gwT", [P, 2, DC, E], BF16)
        stats, mv = sb("stats", [P, GT, 6]), sb("mv", [P, GT, 2])
        rstd, power = sb("rstd", [P, GT]), sb("power", [P, GT])
        nmax, esum, rsum = sb("nmax", [P, GT]), sb("esum", [P, GT]), sb("rsum", [P, GT])
        probs = sb("probs", [P, GT, E])
        top8, top8i = sb("top8", [P, GT, 8]), sb("top8i", [P, GT, 8], U32)
        chosen = sb("chosen", [P, GT * 2])
        hot, hit = sb("hot", [P, GT * 2, E]), sb("hit", [P, GT * 2, E])
        picks = sb("picks", [P, GT, E], BF16)
        counts = sb("counts", [P, GT + 1, E], BF16)
        pos, slot, over = sb("pos", [P, GT * 2]), sb("slot", [P, GT * 2]), sb("over", [P, GT * 2])
        sidx = sb("sidx", [P, GT * 2], U32)
        pick = sb("pick", [P, GT, 4], U32)
        gs, us = (sb(n, [P, 2, DC, IS], BF16) for n in ("gs", "us"))
        ds_ = sb("ds_", [P, 2, 6, D], BF16)
        sg = [sb(f"sg{k}", [P, 3 * P]) for k in range(2)]
        hs = [sb(f"hs{k}", [P, 3 * P]) for k in range(2)]
        hT = sb("hsT", [P, 2, 6, GT * P], BF16)
        raw = hT[:, :, :, :].rearrange("p h m s -> p (h m s)").bitcast(F32)
        raw_in, raw_hi, raw_lo = sem("raw_in"), sem("raw_hi"), sem("raw_lo")
        x_in, gb_in = sem("x_in"), sem("gb_in")
        made, pool_c, pool_f, dve_c = sem("made"), sem("pool_c"), sem("pool_f"), sem("dve_c")
        gw_in, gw_ps, gw_hi, gw_lo = (sem(n) for n in ("gw_in", "gw_ps", "gw_hi", "gw_lo"))
        stat_done, rstd_done, y_done, xb_done = sem("stat_done"), sem("rstd_done"), sem("y_done"), sem("xb_done")
        own_ps, own_added, x1_done, xn_done = sem("own_ps"), sem("own_added"), sem("x1_done"), sem("xn_done")
        rows_hi, rows_lo, scattered = sem("rows_hi"), sem("rows_lo"), sem("scattered")
        xT_ps, xT_hi, xT_lo = sem("xT_ps"), sem("xT_hi"), sem("xT_lo")
        x1_out, xr_in, xr_out, pick_out = sem("x1_out"), sem("xr_in"), sem("xr_out"), sem("pick_out")
        logit_ps, nmax_done, exp_done = sem("logit_ps"), sem("nmax_done"), sem("exp_done")
        picks_done, rank_ps, sidx_done = sem("picks_done"), sem("rank_ps"), sem("sidx_done")
        gu_ps, silu_done, h_done, hT_hi, hT_lo = (sem(n) for n in (
            "gu_ps", "silu_done", "h_done", "hT_hi", "hT_lo"))
        down_ps, xr_done = sem("down_ps"), sem("xr_done")
        rowsof = x_f.rearrange("(t p) d -> p t d", p=P)
        x1of = x1_d.rearrange("(t p) d -> p t d", p=P)
        xsof = xs_d.rearrange("(t p) d -> p t d", p=P)
        pickof = pick_d.rearrange("(t p) k -> p t k", p=P)

        def routes(t):
            return not last_of(t, NG + 1)

        def shares(t):
            return later(t, 1)

        def chunk(q):
            return SUBS[q // 6], q % 6, SC[q % 6]

        def raw_parts(n):
            if n < 2:
                return [(raw[:, 0:DC * IS].rearrange("p (c i) -> p c i", c=DC),
                         [(gs, us)[n][:, h, :, :] for h in (HI, LO)])]
            tail = IS - 5 * P
            return [(raw[:, 0:5 * D].rearrange("p (c d) -> p c d", c=5), [ds_[:, h, 0:5, :] for h in (HI, LO)]),
                    (raw[0:tail, 5 * D:6 * D], [ds_[0:tail, h, 5, :] for h in (HI, LO)])]

        with nc.Block() as block:
            @block.sync
            def _(sp):
                sp.dma_start(gw[:, :], gate_w).then_inc(gw_in, 16)
                sp.dma_start(x[:, :, :], rowsof[:, 0:GT, :]).then_inc(x_in, 16)
                for dst, src in ((gamma_b, gamma), (beta_b, beta)):
                    sp.dma_start(dst[:, :], src.rearrange("(a n) -> a n", a=1).to_broadcast([P, D])
                                 ).then_inc(gb_in, 16)
                for n, w in enumerate((ws_gate, ws_up)):
                    if n:
                        sp.wait_ge(raw_lo, n)
                    sp.dma_start(raw_parts(n)[0][0], w.rearrange("(c p) i -> p c i", p=P)).then_inc(raw_in, 32)
                sp.wait_ge(raw_lo, 2)
                whole, rest = raw_parts(2)
                sp.dma_start(whole[0], ws_down[0:5 * P, :].rearrange("(c p) d -> p c d", p=P)).then_inc(raw_in, 16)
                sp.dma_start(rest[0], ws_down[5 * P:IS, :]).then_inc(raw_in, 16)

                def part(t, _):
                    if shares(t):
                        if later(t, 2):
                            sp.wait_ge(xr_out, t * 16 - 16)
                        sp.dma_start(xr[:, :, :], x1of[:, bass.ds(t * GT - GT, GT), :]).then_inc(xr_in, 16)
                    if routes(t):
                        sp.wait_ge(x1_done, t + 1)
                        sp.dma_start(x1of[:, bass.ds(t * GT, GT), :], x[:, :, :]).then_inc(x1_out, 16)
                        sp.wait_ge(x1_out, t * 16 + 16)
                        if not last_of(t, NG):
                            sp.wait_ge(xn_done, t + 1)
                            sp.dma_start(x[:, :, :], rowsof[:, bass.ds(t * GT + GT, GT), :]).then_inc(x_in, 16)
                        sp.wait_ge(sidx_done, t + 1)
                        sp.dma_start(pickof[:, bass.ds(t * GT, GT), :], pick[:, :, :]).then_inc(pick_out, 16)
                    if shares(t):
                        sp.wait_ge(xr_done, t * GT)
                        sp.dma_start(xsof[:, bass.ds(t * GT - GT, GT), :], xr[:, :, :]).then_inc(xr_out, 16)
                repeat(sp, Steps(sp, None), NG + 1, part, head=2, tail=2)
                sp.wait_ge(pick_out, NG * 16)
                sp.wait_ge(xr_out, NG * 16)

            @block.gpsimd
            def _(pool):
                st = Steps(pool, pool_c)
                st.did(pool.memset(power[:, :], -0.5))
                st.did(pool.memset(own[:, :], 1.0))
                st.settle()
                st.did(pool.affine_select(out=own[:, :], in_=own[:, :], compare_op=ALU.is_ge, fill=0.0,
                                          base=0, pattern=[[1, TOK]], channel_multiplier=-S))
                st.settle()
                pool.affine_select(out=own[:, :], in_=own[:, :], compare_op=ALU.is_ge, fill=0.0,
                                   base=S - 1, pattern=[[-1, TOK]], channel_multiplier=S).then_inc(made, 1)

                fixed = Steps(pool, pool_f)

                def constants():
                    fixed.did(pool.memset(before[:, :], 1.0))
                    fixed.did(pool.memset(ones[:, :], 1.0))
                    fixed.did(pool.memset(counts[:, :, :], 0.0))
                    fixed.did(pool.iota(iota_i[:, :], pattern=[[1, E]], base=0, channel_multiplier=0))
                    fixed.settle()
                    fixed.did(pool.tensor_copy(iota_f[:, :], iota_i[:, :]))
                    fixed.did(pool.affine_select(out=before[:, :], in_=before[:, :], compare_op=ALU.is_ge, fill=0.0,
                                              base=-1, pattern=[[1, P]], channel_multiplier=-1))
                    fixed.settle()
                    pool.wait_ge(gb_in, 32)
                    pool.tensor_scalar(beta_b[:, :], beta_b[:, :], gains[:, 0:1], None, ALU.mult).then_inc(made, 1)
                    pool.tensor_scalar(gamma_b[:, :], gamma_b[:, :], gains[:, 0:1], None, ALU.mult
                                       ).then_inc(made, 1)
                    pool.wait_ge(made, 3)

                def part(t, _):
                    for n in range(3):
                        pool.wait_ge(stat_done, t * 3 + n + 1)
                        apart(pool)
                        rsqrt(pool, st, rstd[:, :], mv[:, :, 1], power[:, :], rstd_done)
                        if n == 0 and not later(t, 1):
                            constants()
                        if n == 0:
                            pool.wait_ge(y_done, t + 1)
                            pool.tensor_tensor(x[:, :, :], x[:, :, :],
                                               beta_b[:, :].unsqueeze(1).to_broadcast([P, GT, D]),
                                               ALU.add).then_inc(xb_done, 1)
                    pool.wait_ge(rows_hi, t + 1)
                    pool.tensor_tensor(rows[:, :, LO, :], y[:, :, :], rows[:, :, HI, :],
                                       ALU.subtract).then_inc(rows_lo, 1)
                    pool.wait_ge(rows_lo, t + 1)
                    pool.wait_ge(sidx_done, t + 1)
                    apart(pool)
                    for j in range(GT):
                        for k in range(2):
                            pool.indirect_dma_start(
                                slots_d, bass.IndirectOffsetOnAxis(ap=sidx[:, 2 * j + k:2 * j + k + 1], axis=0),
                                rows[:, j, :, :].rearrange("p h d -> p (h d)"), None,
                                bounds_check=E * CAP - 1, oob_is_err=False).then_inc(scattered, 16)
                repeat(pool, st, NG, part)
                pool.wait_ge(scattered, NG * GT * 32)

            @block.scalar
            def _(act):
                act.wait_ge(gw_ps, 1)
                act.activation(gwT[:, HI, :, :], bank[7][:, 0:DC * E].rearrange("p (c e) -> p c e", c=DC),
                               ACT.Copy).then_inc(gw_hi, 1)
                for n in range(3):
                    act.wait_ge(raw_in, n * 32 + 32)
                    for src, (high, _) in raw_parts(n):
                        ins = act.activation(high, src, ACT.Copy)
                    ins.then_inc(raw_hi, 1)

                def silu(t, q):
                    (_, tn), _, (_, n) = chunk(q)
                    act.wait_ge(gu_ps, t * NQ - NQ + q + 1)
                    if later(t, 2) or q >= 2:
                        act.wait_ge(h_done, t * NQ - NQ + q - 1)
                    act.activation(sg[q % 2][0:n, 0:tn * P], bank[2 * (q % 2)][0:n, 0:tn * P], ACT.Silu
                                   ).then_inc(silu_done, 1)

                def hidden_hi(t, q):
                    (t0, tn), m, (_, n) = chunk(q)
                    act.wait_ge(h_done, t * NQ - NQ + q + 1)
                    if later(t, 2):
                        act.wait_ge(down_ps, t * GT - GT)
                    elif q == 0:
                        act.wait_ge(raw_lo, 3)
                    act.activation(hT[0:n, HI, m, t0 * P:(t0 + tn) * P], hs[q % 2][0:n, 0:tn * P], ACT.Copy
                                   ).then_inc(hT_hi, 1)

                def part(t, _):
                    if shares(t):
                        silu(t, 0)
                        for q in range(NQ):
                            if q < NQ - 1:
                                silu(t, q + 1)
                            hidden_hi(t, q)
                    if routes(t):
                        for j in range(GT):
                            act.wait_ge(xT_ps, t * GT + j + 1)
                            act.activation(xT[:, j, HI, :, :].rearrange("p c q -> p (c q)"), bank[TURN[j]][:, :],
                                           ACT.Copy).then_inc(xT_hi, 1)
                        if later(t, 1):
                            act.wait_ge(scattered, t * (GT * 32))
                        act.activation(rows[:, :, HI, :], y[:, :, :], ACT.Copy).then_inc(rows_hi, 1)
                        act.wait_ge(nmax_done, t + 1)
                        for j in range(GT):
                            ins = act.activation(probs[:, j, :], bank[7][:, j * E:(j + 1) * E], ACT.Exp,
                                                 bias=nmax[:, j:j + 1], accum_out=esum[:, j:j + 1])
                        ins.then_inc(exp_done, 1)
                repeat(act, Steps(act, None), NG + 1, part, head=2, tail=1)

            @block.vector
            def _(dve):
                st = Steps(dve, dve_c)
                dve.wait_ge(gw_hi, 1)
                dve.tensor_tensor(gwT[:, LO, :, :], bank[7][:, 0:DC * E].rearrange("p (c e) -> p c e", c=DC),
                                  gwT[:, HI, :, :], ALU.subtract).then_inc(gw_lo, 1)

                def hidden_lo(t, q):
                    (t0, tn), m, (_, n) = chunk(q)
                    dve.wait_ge(hT_hi, t * NQ - NQ + q + 1)
                    dve.tensor_tensor(hT[0:n, LO, m, t0 * P:(t0 + tn) * P], hs[q % 2][0:n, 0:tn * P],
                                      hT[0:n, HI, m, t0 * P:(t0 + tn) * P], ALU.subtract).then_inc(hT_lo, 1)

                def beside(t, q):
                    if not shares(t):
                        if q % 4 == 2:
                            n = q // 4
                            dve.wait_ge(raw_hi, n + 1)
                            for src, (high, low) in raw_parts(n):
                                ins = dve.tensor_tensor(low, src, high, ALU.subtract)
                            ins.then_inc(raw_lo, 1)
                        return
                    (_, tn), _, (_, n) = chunk(q)
                    if q == 0 and not later(t, 2):
                        dve.wait_ge(raw_lo, 3)
                    if q >= 1:
                        hidden_lo(t, q - 1)
                    dve.wait_ge(silu_done, t * NQ - NQ + q + 1)
                    if later(t, 2) or q >= 2:
                        dve.wait_ge(hT_hi, t * NQ - NQ + q - 1)
                        dve.wait_ge(hT_lo, t * NQ - NQ + q - 1)
                    dve.tensor_tensor(hs[q % 2][0:n, 0:tn * P], sg[q % 2][0:n, 0:tn * P],
                                      bank[2 * (q % 2) + 1][0:n, 0:tn * P], ALU.mult).then_inc(h_done, 1)

                def normed(t, n, src, dst, done=None):
                    dve.wait_ge(rstd_done, 3 * t + n + 1)
                    for j in range(GT):
                        ins = dve.tensor_scalar(dst[:, j, :], src[:, j, :], mv[:, j, 0:1], rstd[:, j:j + 1],
                                                ALU.subtract, ALU.mult)
                        if done is None or j < GT - 1:
                            st.did(ins)
                        else:
                            ins.then_inc(done, 1)

                def add_own(t, tiles):
                    for j in tiles:
                        dve.wait_ge(own_ps, t * GT + j + 1)
                        dve.tensor_tensor(y[:, j, :], y[:, j, :], bank[4 + j % 3][:, :], ALU.add
                                          ).then_inc(own_added, 1)

                def add_shared(t, j):
                    if shares(t):
                        dve.wait_ge(down_ps, t * GT - GT + j + 1)
                        dve.wait_ge(xr_in, t * 16)
                        dve.scalar_tensor_tensor(out=xr[:, j, :], in0=bank[4 + j % 3][:, :], scalar=gains[:, 2:3],
                                                 in1=xr[:, j, :], op0=ALU.mult, op1=ALU.add).then_inc(xr_done, 1)

                def part(t, _):
                    if not routes(t):
                        for q in range(NQ):
                            beside(t, q)
                        hidden_lo(t, NQ - 1)
                        for j in range(GT):
                            add_shared(t, j)
                        return
                    dve.wait_ge(x_in, t * 16 + 16)
                    row_stats(dve, st, lambda j: x[:, j, :], stats, mv, GT, stat_done)
                    beside(t, 0)
                    if later(t, 1):
                        dve.wait_ge(xT_ps, t * GT)
                        dve.wait_ge(rows_hi, t)
                        dve.wait_ge(rows_lo, t)
                    normed(t, 0, x, y, y_done)
                    beside(t, 1)
                    st.settle()
                    dve.wait_ge(y_done, t + 1)
                    add_own(t, range(0, 3))
                    beside(t, 2)
                    add_own(t, range(3, GT))
                    beside(t, 3)
                    dve.wait_ge(own_added, t * GT + GT)
                    row_stats(dve, st, lambda j: y[:, j, :], stats, mv, GT, stat_done)
                    beside(t, 4)
                    normed(t, 1, y, y)
                    beside(t, 5)
                    st.settle()
                    if not later(t, 1):
                        dve.wait_ge(made, 3)
                    st.did(dve.tensor_tensor(y[:, :, :], y[:, :, :],
                                             gamma_b[:, :].unsqueeze(1).to_broadcast([P, GT, D]), ALU.mult))
                    beside(t, 6)
                    st.settle()
                    dve.wait_ge(xb_done, t + 1)
                    dve.tensor_tensor(x[:, :, :], y[:, :, :], x[:, :, :], ALU.add).then_inc(x1_done, 1)
                    beside(t, 7)
                    dve.wait_ge(x1_done, t + 1)
                    row_stats(dve, st, lambda j: x[:, j, :], stats, mv, GT, stat_done)
                    beside(t, 8)
                    normed(t, 2, x, y, xn_done)
                    for q in range(9, NQ):
                        beside(t, q)
                    if shares(t):
                        hidden_lo(t, NQ - 1)
                    for j in range(GT):
                        dve.wait_ge(xT_hi, t * GT + j + 1)
                        dve.tensor_tensor(xT[:, j, LO, :, :].rearrange("p c q -> p (c q)"), bank[TURN[j]][:, :],
                                          xT[:, j, HI, :, :].rearrange("p c q -> p (c q)"),
                                          ALU.subtract).then_inc(xT_lo, 1)
                    dve.wait_ge(logit_ps, t + 1)
                    dve.tensor_reduce(nmax[:, :], bank[7][:, 0:GT * E].rearrange("p (j e) -> p j e", e=E),
                                      axis=AX.X, op=ALU.max, negate=True).then_inc(nmax_done, 1)
                    dve.wait_ge(exp_done, t + 1)
                    st.did(dve.reciprocal(rsum[:, :], esum[:, :]))
                    st.settle()
                    st.did(dve.tensor_tensor(probs[:, :, :], probs[:, :, :], wide(rsum[:, :], E), ALU.mult))
                    st.settle(alone=True)
                    for j in range(GT):
                        st.did(dve.max(top8[:, j, :], probs[:, j, :]))
                    st.settle(alone=True)
                    for j in range(GT):
                        st.did(dve.max_index(top8i[:, j, :], top8[:, j, :], probs[:, j, :]))
                    if later(t, 1):
                        dve.wait_ge(pick_out, t * 16)
                    st.did(dve.tensor_scalar(pick[:, :, 2:4].bitcast(F32), top8[:, :, 0:2], gains[:, 2:3], None,
                                             ALU.mult))
                    st.settle()
                    st.did(dve.tensor_copy(chosen[:, :].rearrange("p (j k) -> p j k", k=2), top8i[:, :, 0:2]))
                    st.settle()
                    st.did(dve.tensor_tensor(hot[:, :, :], iota_f[:, :].unsqueeze(1).to_broadcast([P, GT * 2, E]),
                                             wide(chosen[:, :], E), ALU.is_equal))
                    st.settle()
                    pair = hot[:, :, :].rearrange("p (j k) e -> p j k e", k=2)
                    st.did(dve.tensor_tensor(picks[:, :, :], pair[:, :, 0, :], pair[:, :, 1, :], ALU.add))
                    if later(t, 1):
                        st.did(dve.tensor_copy(counts[:, 0, :], counts[:, GT, :]))
                    else:
                        st.did(dve.tensor_copy(counts[:, GT, :], counts[:, 0, :]))
                    st.settle()
                    for j in range(GT):
                        ins = dve.tensor_tensor(counts[:, j + 1, :], counts[:, j, :], picks[:, j, :], ALU.add)
                        if j < GT - 1:
                            st.did(ins)
                            st.settle()
                    ins.then_inc(picks_done, 1)
                    add_shared(t, 0)
                    add_shared(t, 1)
                    dve.wait_ge(rank_ps, t + 1)
                    rank = bank[7][:, RANK:RANK + GT * E].rearrange("p (j e) -> p j e", e=E)
                    hits = hit[:, :, :].rearrange("p (j k) e -> p j k e", k=2)
                    for k in range(2):
                        st.did(dve.tensor_tensor(hits[:, :, k, :], pair[:, :, k, :], rank, ALU.mult))
                    st.settle()
                    st.did(dve.tensor_reduce(pos[:, :], hit[:, :, :], axis=AX.X, op=ALU.add))
                    st.settle()
                    st.did(dve.tensor_scalar(slot[:, :], pos[:, :], float(CAP - 1), None, ALU.min))
                    st.did(dve.tensor_scalar(over[:, :], pos[:, :], float(CAP), float(E * CAP),
                                             ALU.is_ge, ALU.mult))
                    st.settle()
                    st.did(dve.scalar_tensor_tensor(out=slot[:, :], in0=chosen[:, :], scalar=float(CAP),
                                                    in1=slot[:, :], op0=ALU.mult, op1=ALU.add))
                    st.settle()
                    st.did(dve.tensor_copy(pick[:, :, 0:2], slot[:, :].rearrange("p (j k) -> p j k", k=2)))
                    st.settle()
                    if later(t, 1):
                        dve.wait_ge(scattered, t * (GT * 32))
                    dve.tensor_tensor(sidx[:, :], slot[:, :], over[:, :], ALU.add).then_inc(sidx_done, 1)
                    for j in range(2, GT):
                        add_shared(t, j)
                repeat(dve, st, NG + 1, part, head=2, tail=1)

            @block.tensor
            def _(pe):
                pe.wait_ge(gw_in, 16)
                for c in range(DC):
                    ins = pe.transpose(bank[7][:, c * E:(c + 1) * E], gw[:, c * P:(c + 1) * P], ident[0:E, 0:E])
                ins.then_inc(gw_ps, 1)
                pe.wait_ge(made, 1)

                def give_own(t, tiles):
                    for j in tiles:
                        if j >= 3:
                            pe.wait_ge(own_added, t * GT + j - 2)
                        for n in range(3):
                            ins = pe.matmul(bank[4 + j % 3][:, :], own[:, bass.ds(t * (GT * P) + j * P, P)],
                                            summary[:, n, :], start=n == 0, stop=n == 2)
                        ins.then_inc(own_ps, 1)

                def gate_up(t, q):
                    (t0, tn), _, (i0, rows_) = chunk(q)
                    if later(t, 2) or q >= 2:
                        pe.wait_ge(h_done, t * NQ - NQ + q - 1)
                    for v, w_ in enumerate((gs, us)):
                        n = 0
                        for c in range(DC):
                            for a, w in PAIRS:
                                ins = pe.matmul(
                                    bank[2 * (q % 2) + v][0:rows_, 0:tn * P].rearrange("r (t q) -> r t q", q=P),
                                    w_[:, w, c, i0:i0 + rows_], xT[:, t0:t0 + tn, a, c, :],
                                    start=n == 0, stop=n == 11)
                                n += 1
                    ins.then_inc(gu_ps, 1)

                def down(t, j):
                    u = 0 if j < 3 else 1
                    pe.wait_ge(hT_hi, t * NQ - NQ + 6 * u + 6)
                    pe.wait_ge(hT_lo, t * NQ - NQ + 6 * u + 6)
                    if j >= 3:
                        pe.wait_ge(xr_done, t * GT - GT + j - 2)
                    n = 0
                    for c, (_, rows_) in enumerate(SC):
                        for a, w in PAIRS:
                            ins = pe.matmul(bank[4 + j % 3][:, :], hT[0:rows_, a, c, j * P:(j + 1) * P],
                                            ds_[0:rows_, w, c, :], start=n == 0, stop=n == 17)
                            n += 1
                    ins.then_inc(down_ps, 1)

                def part(t, _):
                    if later(t, 1):
                        pe.wait_ge(xT_hi, t * GT)
                        pe.wait_ge(xT_lo, t * GT)
                    if later(t, 2):
                        pe.wait_ge(xr_done, t * GT - GT)
                    if routes(t):
                        give_own(t, range(0, 3))
                    if shares(t):
                        if not later(t, 2):
                            pe.wait_ge(raw_lo, 3)
                        gate_up(t, 0)
                        gate_up(t, 1)
                    if routes(t):
                        give_own(t, range(3, GT))
                    if shares(t):
                        for q in range(2, NQ):
                            gate_up(t, q)
                    if routes(t):
                        if shares(t):
                            pe.wait_ge(h_done, t * NQ)
                        pe.wait_ge(xn_done, t + 1)
                        for j in range(GT):
                            for c in range(DC):
                                ins = pe.transpose(bank[TURN[j]][:, c * P:(c + 1) * P], y[:, j, c * P:(c + 1) * P],
                                                   ident[:, :])
                            ins.then_inc(xT_ps, 1)
                        for j in range(GT):
                            pe.wait_ge(xT_hi, t * GT + j + 1)
                            pe.wait_ge(xT_lo, t * GT + j + 1)
                            if j == 0:
                                if later(t, 1):
                                    pe.wait_ge(exp_done, t)
                                else:
                                    pe.wait_ge(gw_lo, 1)
                            n = 0
                            for c in range(DC):
                                for a, w in PAIRS:
                                    ins = pe.matmul(bank[7][:, j * E:(j + 1) * E], xT[:, j, a, c, :],
                                                    gwT[:, w, c, :], start=n == 0, stop=n == 11)
                                    n += 1
                        ins.then_inc(logit_ps, 1)
                    if shares(t):
                        for j in range(3):
                            down(t, j)
                    if routes(t):
                        pe.wait_ge(picks_done, t + 1)
                        at = slice(RANK, RANK + GT * E)
                        pe.matmul(bank[7][:, at], before[:, :], picks[:, :, :].rearrange("p j e -> p (j e)"),
                                  start=True, stop=False)
                        pe.matmul(bank[7][:, at], ones[:, :], counts[:, 0:GT, :].rearrange("p j e -> p (j e)"),
                                  start=False, stop=True).then_inc(rank_ps, 1)
                    if shares(t):
                        for j in range(3, GT):
                            down(t, j)
                repeat(pe, Steps(pe, None), NG + 1, part, head=2, tail=1)


def expert_phase(nc, g, w_gate, w_up, w_down, down2, slots_d, eout_d):
    ident, identb, bank, downT = g["ident"], g["identb"], g["bank"], g["downT"]
    with ExitStack() as es:
        def sb(name, shape, dt=F32):
            return es.enter_context(nc.sbuf_tensor(name, shape, dt))

        def sem(name):
            return nc.alloc_semaphore(f"expert_{name}")

        gu_raw = sb("gu_raw", [P, 2, DC, I])
        down_raw = sb("down_raw", [P, 3, D])
        gu = [sb(f"gu{k}", [P, 2, 2, DC, I], BF16) for k in range(2)]
        dn = [sb(f"dn{k}", [P, 2, 3, D], BF16) for k in range(2)]
        xs = [sb(f"xs{k}", [P, 2, 2, D], BF16) for k in range(2)]
        xsT = [sb(f"xsT{k}", [P, 2, DC, CAP], BF16) for k in range(2)]
        act_g = [sb(f"act_g{k}", [P, CAP]) for k in range(2)]
        h = [sb(f"h{k}", [P, CAP]) for k in range(2)]
        hT = sb("hT", [P, 2, 3, CAP], BF16)
        eo = [sb(f"eo{k}", [P, D]) for k in range(2)]
        wstage = [sb(f"estage{k}", [P, D]) for k in range(2)]
        wr = [sb(f"er{k}", [P, D]) for k in range(2)]
        wm, dq = sb("em", [P, D]), sb("edq", [P, D])
        wscale = [sb(f"escale{k}", [P, D // MXB]) for k in range(2)]
        wamax, winv = sb("eamax", [P, D // MXB]), sb("einv", [P, D // MXB])
        wst_in = [sem(f"wst_in{k}") for k in range(2)]
        dve_c, round_done, dq_done, wT_ps, wT_hi, wT_lo = (sem(n) for n in (
            "dve_c", "round_done", "dq_done", "wT_ps", "wT_hi", "wT_lo"))
        downv = down2.rearrange("(p r) (a n) -> p (r a) n", r=4, n=D)
        gu_in, down_in = sem("gu_in"), sem("down_in")
        xs_in = [sem(f"xs_in{k}") for k in range(2)]
        gu_hi, gu_lo, dn_hi, dn_lo = sem("gu_hi"), sem("gu_lo"), sem("dn_hi"), sem("dn_lo")
        xs_ps, xsT_done, xsT_done_v = sem("xs_ps"), sem("xsT_done"), sem("xsT_done_v")
        gu_ps, silu_done, h_done, hT_hi, hT_lo = (sem(n) for n in (
            "gu_ps", "silu_done", "h_done", "hT_hi", "hT_lo"))
        out_ps, eo_done = sem("out_ps"), sem("eo_done")
        eo_out = [sem(f"eo_out{k}") for k in range(2)]
        with nc.Block() as block:
            @block.sync
            def _(sp):
                def load_xs(t, k):
                    sp.dma_start(xs[k][:, :, :, :].rearrange("p s h d -> p s (h d)"),
                                 slots_d[bass.ds(t * CAP, CAP), :].rearrange("(s p) d -> p s d", p=P)
                                 ).then_inc(xs_in[k], 16)

                def load_w(t):
                    for n, w in enumerate((w_gate, w_up)):
                        sp.dma_start(gu_raw[:, n, :, :],
                                     w[bass.ds(t, 1), :, :].rearrange("a (c p) i -> p (a c) i", p=P)
                                     ).then_inc(gu_in, 16)

                def load_down(t):
                    rows = w_down[bass.ds(t, 1), :, :].rearrange("a i d -> (a i) d")
                    sp.dma_start(down_raw[:, 0:2, :], rows[0:256, :].rearrange("(c p) d -> p c d", p=P)
                                 ).then_inc(down_in, 16)
                    sp.dma_start(down_raw[0:I - 256, 2, :], rows[256:I, :]).then_inc(down_in, 16)

                def load_mx(t, k):
                    sp.dma_start(wstage[k][:, :], downv[:, bass.ds(t, 1), :].rearrange("p a n -> p (a n)")
                                 ).then_inc(wst_in[k], 16)
                load_w(0)
                load_xs(0, 0)
                load_down(0)
                load_xs(1, 1)
                load_mx(0, 0)
                load_mx(1, 1)

                def part(t, k):
                    if not last_of(t, E):
                        sp.wait_ge(gu_hi, t + 1)
                        sp.wait_ge(gu_lo, t + 1)
                        load_w(t + 1)
                        sp.wait_ge(dn_hi, t + 1)
                        sp.wait_ge(dn_lo, t + 1)
                        load_down(t + 1)
                    if not isinstance(t, int) or t < E - 2:
                        sp.wait_ge(xs_ps, 2 * t + 2)
                        load_xs(t + 2, k)
                        sp.wait_ge(round_done, t + 1)
                        load_mx(t + 2, k)
                    for s in range(2):
                        sp.wait_ge(eo_done, 2 * t + s + 1)
                        sp.dma_start(eout_d[bass.ds(t * CAP + s * P, P), :], eo[s][:, :]).then_inc(eo_out[s], 16)
                repeat(sp, Steps(sp, None), E, part, unroll=2, tail=2)
                for s in range(2):
                    sp.wait_ge(eo_out[s], E * 16)

            @block.gpsimd
            def _(pool):
                def part(t, k):
                    pool.wait_ge(dn_hi, t + 1)
                    if later(t, 2):
                        pool.wait_ge(out_ps, 2 * t - 2)
                    pool.tensor_tensor(dn[k][:, LO, 0:2, :], down_raw[:, 0:2, :], dn[k][:, HI, 0:2, :], ALU.subtract)
                    pool.tensor_tensor(dn[k][0:I - 256, LO, 2, :], down_raw[0:I - 256, 2, :],
                                       dn[k][0:I - 256, HI, 2, :], ALU.subtract).then_inc(dn_lo, 1)
                    pool.wait_ge(round_done, t + 1)
                    if later(t, 1):
                        pool.wait_ge(wT_ps, t)
                    pool.tensor_tensor(blocks(dq[:, :]), blocks(wr[k][:, :]), wide(wscale[k][:, :], MXB),
                                       ALU.mult).then_inc(dq_done, 1)
                repeat(pool, Steps(pool, None), E, part, unroll=2)

            @block.scalar
            def _(act):
                def split(t, k):
                    act.wait_ge(gu_in, t * 32 + 32)
                    if later(t, 2):
                        act.wait_ge(gu_ps, 3 * t - 3)
                    act.activation(gu[k][:, HI, :, :, :], gu_raw[:, :, :, :], ACT.Copy).then_inc(gu_hi, 1)
                    act.wait_ge(down_in, t * 32 + 32)
                    if later(t, 2):
                        act.wait_ge(out_ps, 2 * t - 2)
                    act.activation(dn[k][:, HI, 0:2, :], down_raw[:, 0:2, :], ACT.Copy)
                    act.activation(dn[k][0:I - 256, HI, 2, :], down_raw[0:I - 256, 2, :], ACT.Copy
                                   ).then_inc(dn_hi, 1)

                def mx_hi(t):
                    act.wait_ge(wT_ps, t + 1)
                    act.activation(downT[:, HI, bass.ds(t, 1), :, :].rearrange("p a c i -> p (a c) i"),
                                   bank[6][:, :].rearrange("p (c i) -> p c i", c=DC), ACT.Copy).then_inc(wT_hi, 1)
                split(0, 0)

                def part(t, k):
                    act.wait_ge(xs_ps, 2 * t + 1)
                    if later(t, 2):
                        act.wait_ge(gu_ps, 3 * t - 3)
                    act.activation(xsT[k][:, :, :, 0:P].rearrange("p h c q -> p (h c) q"),
                                   bank[2][:, :].bitcast(BF16).rearrange("p (c q) -> p c q", q=P),
                                   ACT.Copy).then_inc(xsT_done, 1)
                    for m, (_, rows) in enumerate(IC):
                        act.wait_ge(gu_ps, 3 * t + m + 1)
                        if later(t, 1) or m >= 2:
                            act.wait_ge(h_done, 3 * t + m - 1)
                        act.activation(act_g[(k + m) % 2][0:rows, :], bank[(k + m) % 2][0:rows, 0:CAP], ACT.Silu
                                       ).then_inc(silu_done, 1)
                        act.wait_ge(h_done, 3 * t + m + 1)
                        if later(t, 1):
                            act.wait_ge(out_ps, 2 * t)
                        act.activation(hT[0:rows, HI, m, :], h[(k + m) % 2][0:rows, :], ACT.Copy).then_inc(hT_hi, 1)
                    if not last_of(t, E):
                        split(t + 1, 1 - k)
                    for s in range(2):
                        act.wait_ge(out_ps, 2 * t + s + 1)
                        if later(t, 1):
                            act.wait_ge(eo_out[s], t * 16)
                        act.activation(eo[s][:, :], bank[4 + s][:, :], ACT.Copy).then_inc(eo_done, 1)
                        if s == 0 and later(t, 1):
                            mx_hi(t - 1)
                repeat(act, Steps(act, None), E, part, unroll=2, tail=2)
                mx_hi(E - 1)

            @block.vector
            def _(dve):
                st = Steps(dve, dve_c)

                def mx_low(t):
                    dve.wait_ge(wT_hi, t + 1)
                    lo, hi = (downT[:, h, bass.ds(t, 1), :, :].rearrange("p a c i -> p (a c) i") for h in (LO, HI))
                    dve.tensor_tensor(lo, bank[6][:, :].rearrange("p (c i) -> p c i", c=DC), hi,
                                      ALU.subtract).then_inc(wT_lo, 1)

                def mx_piece(t, k, n):
                    if n == 0:
                        dve.wait_ge(wst_in[k], t * 8 + (16 if k == 0 else 8))
                        if later(t, 2):
                            dve.wait_ge(dq_done, t - 1)
                        mx_scales(dve, st, wstage[k][:, :], wamax[:, :], wscale[k][:, :], winv[:, :])
                    if n == 1:
                        mx_round(dve, st, wstage[k][:, :], winv[:, :], wr[k][:, :], wm[:, :])
                    if n == 2:
                        dve.tensor_tensor(wr[k][:, :], wr[k][:, :], wm[:, :], ALU.subtract).then_inc(round_done, 1)

                def split(t, k):
                    dve.wait_ge(gu_hi, t + 1)
                    dve.tensor_tensor(gu[k][:, LO, :, :, :].rearrange("p n c i -> p (n c i)"),
                                      gu_raw[:, :, :, :].rearrange("p n c i -> p (n c i)"),
                                      gu[k][:, HI, :, :, :].rearrange("p n c i -> p (n c i)"),
                                      ALU.subtract).then_inc(gu_lo, 1)
                split(0, 0)

                def part(t, k):
                    dve.wait_ge(xs_ps, 2 * t + 2)
                    if later(t, 2):
                        dve.wait_ge(gu_ps, 3 * t - 3)
                    dve.tensor_copy(xsT[k][:, :, :, P:CAP].rearrange("p h c q -> p (h c) q"),
                                    bank[3][:, :].bitcast(BF16).rearrange("p (c q) -> p c q", q=P)
                                    ).then_inc(xsT_done_v, 1)
                    for m, (_, rows) in enumerate(IC):
                        dve.wait_ge(silu_done, 3 * t + m + 1)
                        if later(t, 1) or m >= 2:
                            dve.wait_ge(hT_hi, 3 * t + m - 1)
                            dve.wait_ge(hT_lo, 3 * t + m - 1)
                        dve.tensor_tensor(h[(k + m) % 2][0:rows, :], act_g[(k + m) % 2][0:rows, :],
                                          bank[(k + m) % 2][0:rows, CAP:2 * CAP], ALU.mult).then_inc(h_done, 1)
                        mx_piece(t, k, m)
                        dve.wait_ge(hT_hi, 3 * t + m + 1)
                        if later(t, 1):
                            dve.wait_ge(out_ps, 2 * t)
                        dve.tensor_tensor(hT[0:rows, LO, m, :], h[(k + m) % 2][0:rows, :], hT[0:rows, HI, m, :],
                                          ALU.subtract).then_inc(hT_lo, 1)
                    if not last_of(t, E):
                        split(t + 1, 1 - k)
                    if later(t, 1):
                        mx_low(t - 1)
                    dve.wait_ge(round_done, t + 1)
                repeat(dve, st, E, part, unroll=2, tail=2)
                mx_low(E - 1)

            @block.tensor
            def _(pe):
                def turn(t, k):
                    pe.wait_ge(xs_in[k], t * 8 + 16 if k == 0 else t * 8 + 8)
                    for s in range(2):
                        if later(t, 1):
                            pe.wait_ge((xsT_done, xsT_done_v)[s], t)
                        for q in range(2 * DC):
                            ins = pe.transpose(bank[2 + s][:, q * 64:(q + 1) * 64].bitcast(BF16),
                                               xs[k][:, s, q // DC, (q % DC) * P:(q % DC + 1) * P], identb[:, :])
                        ins.then_inc(xs_ps, 1)

                def mx_turn(t):
                    pe.wait_ge(dq_done, t + 1)
                    if later(t, 1):
                        pe.wait_ge(wT_lo, t)
                    for c in range(DC):
                        ins = pe.transpose(bank[6][:, c * P:(c + 1) * P], dq[:, c * P:(c + 1) * P], ident[:, :])
                    ins.then_inc(wT_ps, 1)
                turn(0, 0)

                def part(t, k):
                    pe.wait_ge(xsT_done, t + 1)
                    pe.wait_ge(xsT_done_v, t + 1)
                    pe.wait_ge(gu_hi, t + 1)
                    pe.wait_ge(gu_lo, t + 1)
                    for m, (i0, rows) in enumerate(IC):
                        if later(t, 1) or m >= 2:
                            pe.wait_ge(h_done, 3 * t + m - 1)
                        for u in range(2):
                            n = 0
                            for c in range(DC):
                                for a, w in PAIRS:
                                    ins = pe.matmul(bank[(k + m) % 2][0:rows, u * CAP:(u + 1) * CAP],
                                                    gu[k][:, w, u, c, i0:i0 + rows], xsT[k][:, a, c, :],
                                                    start=n == 0, stop=n == 11)
                                    n += 1
                        ins.then_inc(gu_ps, 1)
                    if not last_of(t, E):
                        turn(t + 1, 1 - k)
                    if later(t, 1):
                        mx_turn(t - 1)
                    pe.wait_ge(hT_hi, 3 * t + 3)
                    pe.wait_ge(hT_lo, 3 * t + 3)
                    pe.wait_ge(dn_lo, t + 1)
                    for s in range(2):
                        if later(t, 1):
                            pe.wait_ge(eo_done, 2 * t + s - 1)
                        n = 0
                        for c, (_, rows) in enumerate(IC):
                            for a, w in PAIRS:
                                ins = pe.matmul(bank[4 + s][:, :], hT[0:rows, a, c, s * P:(s + 1) * P],
                                                dn[k][0:rows, w, c, :], start=n == 0, stop=n == 8)
                                n += 1
                        ins.then_inc(out_ps, 1)
                repeat(pe, Steps(pe, None), E, part, unroll=2, tail=2)
                mx_turn(E - 1)


def attention_phase(nc, g, ctx, wq, wk, wv, wo, xs_d, pick_d, eout_d, x2_d, x3_d):
    ident, gains, bank = g["ident"], g["gains"], g["bank"]
    NB = 4
    GR = B // NB
    SCALE = float(D) ** -0.5
    KEYS = CTX + S
    VC = CT + [(CTX, S)]
    with ExitStack() as es:
        def sb(name, shape, dt=F32):
            return es.enter_context(nc.sbuf_tensor(name, shape, dt))

        def sem(name):
            return nc.alloc_semaphore(f"attention_{name}")

        wT = [sb(f"{n}T", [P, 2, DC, D], BF16) for n in ("wq", "wk", "wv", "wo")]
        wqT, wkT, wvT, woT = wT
        with ExitStack() as es2:
            raw = es2.enter_context(nc.sbuf_tensor("wraw", [P, 4, DC, D], F32))
            raw_in = [nc.alloc_semaphore(f"wraw_in{n}") for n in range(4)]
            t_ps, t_hi, t_lo = (nc.alloc_semaphore(n) for n in ("t_ps", "t_hi", "t_lo"))
            with nc.Block() as block:
                @block.sync
                def _(sp):
                    for n, w in enumerate((wq, wk, wv, wo)):
                        sp.dma_start(raw[:, n, :, :], w.rearrange("(c p) d -> p c d", p=P)).then_inc(raw_in[n], 16)

                @block.tensor
                def _(pe):
                    for q in range(16):
                        n, c = q // 4, q % 4
                        if c == 0:
                            pe.wait_ge(raw_in[n], 16)
                        if q >= 4:
                            pe.wait_ge(t_lo, q - 3)
                        for r in range(DC):
                            ins = pe.transpose(bank[c][:, r * P:(r + 1) * P], raw[:, n, r, c * P:(c + 1) * P],
                                               ident[:, :])
                        ins.then_inc(t_ps, 1)

                @block.scalar
                def _(act):
                    for q in range(16):
                        act.wait_ge(t_ps, q + 1)
                        act.activation(wT[q // 4][:, HI, q % 4, :], bank[q % 4][:, :], ACT.Copy).then_inc(t_hi, 1)

                @block.vector
                def _(dve):
                    for q in range(16):
                        dve.wait_ge(t_hi, q + 1)
                        dve.tensor_tensor(wT[q // 4][:, LO, q % 4, :], bank[q % 4][:, :],
                                          wT[q // 4][:, HI, q % 4, :], ALU.subtract).then_inc(t_lo, 1)

        crow = [sb(f"arow{k}", [P, 3, D]) for k in range(2)]
        V = sb("V", [P, 2, 3, D], BF16)
        Vn = [sb(f"Vn{k}", [S, 2, D], BF16) for k in range(2)]
        KT = sb("KT", [P, 2, DC, CTX], BF16)
        xin = [sb(f"xin{k}", [S, D]) for k in range(NB)]
        pick = [sb(f"apick{k}", [S, 4], U32) for k in range(NB)]
        fetched = sb("fetched", [S, 2, D])
        xres = [sb(f"xres{k}", [S, D]) for k in range(2)]
        xn = sb("axn", [S, NB, D])
        xgT = sb("xgT", [P, 2, DC, NB * S], BF16)
        qT, nkT = sb("qT", [P, 2, DC, NB * S], BF16), sb("nkT", [P, 2, DC, NB * S], BF16)
        prob = sb("prob", [S, KEYS + LAST - S])
        pT = sb("pT", [P, 2, 4, S], BF16)
        o = sb("o", [S, D])
        oT = sb("oT", [P, 2, DC, S], BF16)
        nmax, esum, rinv = (sb(n, [S, 2]) for n in ("anmax", "aesum", "arinv"))
        stats, mv, rstd, power = sb("astats", [S, 6]), sb("amv", [S, 2]), sb("arstd", [S, 1]), sb("apower", [S, 1])
        crow_in, xres_in, x3_out = ([sem(f"{n}{k}") for k in range(2)] for n in (
            "crow_in", "xres_in", "x3_out"))
        got = sem("got")
        xin_in, x2_out = ([sem(f"{n}{k}") for k in range(NB)] for n in ("xin_in", "x2_out"))
        first_done, x2_done = sem("first_done"), sem("x2_done")
        dve_c, pool_c, const_set = sem("dve_c5"), sem("pool_c5"), sem("const_set")
        stat_done, rstd_done, xn_done = sem("astat_done"), sem("arstd_done"), sem("axn_done")
        x_ps, xg_hi, xg_lo = sem("x_ps"), sem("xg_hi"), sem("xg_lo")
        qk_ps, qk_hi, qk_lo = sem("qk_ps"), sem("qk_hi"), sem("qk_lo")
        kT_ps, kT_hi, kT_lo = sem("kT_ps"), sem("kT_hi"), sem("kT_lo")
        vn_ps, vn_hi, vn_lo = sem("vn_ps"), sem("vn_hi"), sem("vn_lo")
        v_hi, v_lo = sem("v_hi"), sem("v_lo")
        s_ps, nmax_done, exp_done, rinv_done = sem("s_ps"), sem("anmax_done"), sem("aexp_done"), sem("rinv_done")
        pT_ps, pT_hi, pT_lo = sem("pT_ps"), sem("pT_hi"), sem("pT_lo")
        pv_ps, o_done = sem("pv_ps"), sem("o_done")
        oT_ps, oT_hi, oT_lo = sem("oT_ps"), sem("oT_hi"), sem("oT_lo")
        wo_ps, x3_done = sem("wo_ps"), sem("x3_done")

        def normed_at(t, i, more=0):
            ahead, place = divmod(i + NB + 1 + more, NB)
            return None if isinstance(t, int) and t + ahead >= GR else (t + ahead, place)

        def beyond(b, n):
            return not isinstance(b, int) or b >= n

        def dma_count(b, k, each=16):
            return b * (each // 2) + (each if k == 0 else each // 2)

        with nc.Block() as block:
            @block.sync
            def _(sp):
                def load_ctx(b, k):
                    row = ctx[bass.ds(b, 1), :, :].rearrange("a t d -> (a t) d")
                    sp.dma_start(crow[k][:, 0:2, :], row[0:256, :].rearrange("(c p) d -> p c d", p=P)
                                 ).then_inc(crow_in[k], 16)
                    sp.dma_start(crow[k][0:LAST, 2, :], row[256:CTX, :]).then_inc(crow_in[k], 16)

                def load_xin(t, i):
                    b = t * NB + i
                    sp.dma_start(xin[i][:, :], xs_d[bass.ds(b * S, S), :]).then_inc(xin_in[i], 16)
                    sp.dma_start(pick[i][:, :], pick_d[bass.ds(b * S, S), :]).then_inc(xin_in[i], 16)

                def load_xres(b, k):
                    sp.dma_start(xres[k][:, :], x2_d[bass.ds(b * S, S), :]).then_inc(xres_in[k], 16)

                def send_x2(t, i):
                    b = t * NB + i
                    sp.wait_ge(xn_done, b + 1)
                    sp.dma_start(x2_d[bass.ds(b * S, S), :], xin[i][:, :]).then_inc(x2_out[i], 16)
                    sp.wait_ge(x2_out[i], t * 16 + 16)
                    if not last_of(t, GR):
                        load_xin(t + 1, i)

                for i in range(NB):
                    load_xin(0, i)
                for b in range(2):
                    load_ctx(b, b)
                for i in range(NB):
                    send_x2(0, i)
                for b in range(2):
                    load_xres(b, b)
                send_x2(1, 0)

                def part(t, _):
                    for i in range(NB):
                        b, k = t * NB + i, i % 2
                        if not (last_of(t, GR) and i >= 2):
                            sp.wait_ge(v_hi, b + 1)
                            sp.wait_ge(v_lo, b + 1)
                            sp.wait_ge(kT_ps, b * DC + DC)
                            load_ctx(b + 2, k)
                        if normed_at(t, i):
                            send_x2(*normed_at(t, i))
                        sp.wait_ge(x3_done, b + 1)
                        sp.dma_start(x3_d[bass.ds(b * S, S), :], xres[k][:, :]).then_inc(x3_out[k], 16)
                        if not (last_of(t, GR) and i >= 2):
                            sp.wait_ge(x3_out[k], dma_count(b, k))
                            load_xres(b + 2, k)
                repeat(sp, Steps(sp, None), GR, part, tail=3)
                for k in range(2):
                    sp.wait_ge(x3_out[k], B // 2 * 16)

            @block.gpsimd
            def _(pool):
                st = Steps(pool, pool_c)
                pool.memset(power[:, :], -0.5)
                pool.memset(prob[:, KEYS:], 0.0).then_inc(const_set, 1)
                pool.wait_ge(const_set, 1)

                def norm(n):
                    pool.wait_ge(stat_done, n + 1)
                    apart(pool)
                    rsqrt(pool, st, rstd[:, :], mv[:, 1:2], power[:, :], rstd_done)

                def values(b, k):
                    pool.wait_ge(v_hi, b + 1)
                    pool.tensor_tensor(V[:, LO, 0:2, :], crow[k][:, 0:2, :], V[:, HI, 0:2, :], ALU.subtract)
                    pool.tensor_tensor(V[0:LAST, LO, 2, :], crow[k][0:LAST, 2, :], V[0:LAST, HI, 2, :],
                                       ALU.subtract).then_inc(v_lo, 1)

                def fetch(t, i):
                    b = t * NB + i
                    pool.wait_ge(xin_in[i], t * 32 + 32)
                    if beyond(b, 1):
                        pool.wait_ge(x2_done, b)
                    apart(pool)
                    for n in range(2):
                        pool.indirect_dma_start(fetched[:, n, :], None, eout_d,
                                                bass.IndirectOffsetOnAxis(ap=pick[i][:, n:n + 1], axis=0),
                                                bounds_check=E * CAP - 1, oob_is_err=False
                                                ).then_inc(got, 16)
                fetch(0, 0)
                for n in range(NB):
                    norm(n)
                    fetch(*divmod(n + 1, NB))
                values(0, 0)
                norm(NB)
                fetch(1, 1)

                def part(t, _):
                    for i in range(NB):
                        if normed_at(t, i):
                            norm(t * NB + i + NB + 1)
                            if normed_at(t, i, 1):
                                fetch(*normed_at(t, i, 1))
                        if not (last_of(t, GR) and i == NB - 1):
                            values(t * NB + i + 1, (i + 1) % 2)
                repeat(pool, st, GR, part, tail=2)

            @block.scalar
            def _(act):
                def keys_hi(b):
                    for c in range(DC):
                        act.wait_ge(kT_ps, b * DC + c + 1)
                        if c == 0 and beyond(b, 1):
                            act.wait_ge(s_ps, b)
                        act.activation(KT[:, HI, c, :], bank[1 + c % 2][:, 0:CTX], ACT.Copy).then_inc(kT_hi, 1)

                def rows_hi(t):
                    for i in range(NB):
                        act.wait_ge(x_ps, t * NB + i + 1)
                        act.activation(xgT[:, HI, :, i * S:(i + 1) * S],
                                       bank[1 + i % 2][:, 0:DC * S].rearrange("p (c s) -> p c s", c=DC),
                                       ACT.Copy).then_inc(xg_hi, 1)

                def project_hi(t):
                    for q in range(8):
                        act.wait_ge(qk_ps, t * 8 + q + 1)
                        act.activation((qT, nkT)[q // DC][:, HI, q % DC, :], bank[(3, 5)[q % 2]][:, 0:NB * S],
                                       ACT.Copy).then_inc(qk_hi, 1)

                def new_values_hi(b, k):
                    act.wait_ge(vn_ps, b + 1)
                    act.activation(Vn[k][:, HI, :], bank[3][0:S, :], ACT.Copy).then_inc(vn_hi, 1)

                def values_hi(b, k):
                    act.wait_ge(crow_in[k], dma_count(b, k, 32))
                    if beyond(b, 1):
                        act.wait_ge(pv_ps, b)
                    act.activation(V[:, HI, 0:2, :], crow[k][:, 0:2, :], ACT.Copy)
                    act.activation(V[0:LAST, HI, 2, :], crow[k][0:LAST, 2, :], ACT.Copy).then_inc(v_hi, 1)

                def attended_hi(b):
                    act.wait_ge(oT_ps, b + 1)
                    if beyond(b, 1):
                        act.wait_ge(wo_ps, b)
                    act.activation(oT[:, HI, :, :].rearrange("p c s -> p (c s)"), bank[6][:, 0:DC * S],
                                   ACT.Copy).then_inc(oT_hi, 1)
                rows_hi(0)
                project_hi(0)
                keys_hi(0)
                new_values_hi(0, 0)
                values_hi(0, 0)
                act.wait_ge(const_set, 1)

                def part(t, _):
                    for i in range(NB):
                        b, k = t * NB + i, i % 2
                        act.wait_ge(nmax_done, b + 1)
                        if beyond(b, 1):
                            act.wait_ge(pT_ps, b)
                        act.activation(prob[:, 0:KEYS], bank[0][0:S, 0:KEYS], ACT.Exp, scale=SCALE,
                                       bias=nmax[:, k:k + 1], accum_out=esum[:, k:k + 1]).then_inc(exp_done, 1)
                        if i == NB - 1 and not last_of(t, GR):
                            rows_hi(t + 1)
                        if beyond(b, 1):
                            attended_hi(b - 1)
                        if not (last_of(t, GR) and i == NB - 1):
                            keys_hi(b + 1)
                        if i == NB - 1 and not last_of(t, GR):
                            project_hi(t + 1)
                        act.wait_ge(pT_ps, b + 1)
                        if beyond(b, 1):
                            act.wait_ge(pv_ps, b)
                        act.activation(pT[:, HI, 0:2, :].rearrange("p c s -> p (c s)"), bank[4][:, 0:2 * S], ACT.Copy)
                        act.activation(pT[0:LAST, HI, 2:4, :].rearrange("p c s -> p (c s)"),
                                       bank[4][0:LAST, 2 * S:4 * S], ACT.Copy).then_inc(pT_hi, 1)
                        if not (last_of(t, GR) and i == NB - 1):
                            new_values_hi(b + 1, (i + 1) % 2)
                        act.wait_ge(pv_ps, b + 1)
                        act.wait_ge(rinv_done, b + 1)
                        act.activation(o[:, :], bank[5][0:S, :], ACT.Copy, scale=rinv[:, k:k + 1]).then_inc(o_done, 1)
                        if not (last_of(t, GR) and i == NB - 1):
                            values_hi(b + 1, (i + 1) % 2)
                repeat(act, Steps(act, None), GR, part, tail=1)
                attended_hi(B - 1)

            @block.vector
            def _(dve):
                st = Steps(dve, dve_c)

                def norm(t, k):
                    n, slot = t * NB + k, k
                    dve.wait_ge(xin_in[k], t * 32 + 32)
                    dve.wait_ge(got, n * 32 + 32)
                    if beyond(n, 1):
                        dve.wait_ge(stat_done, n)
                    weights = pick[k][:, 2:4].bitcast(F32)
                    for e, (done, count) in enumerate(((first_done, n + 1), (x2_done, n + 1))):
                        dve.scalar_tensor_tensor(out=xin[k][:, :], in0=fetched[:, e, :],
                                                 scalar=weights[:, e:e + 1], in1=xin[k][:, :],
                                                 op0=ALU.mult, op1=ALU.add).then_inc(done, 1)
                        dve.wait_ge(done, count)
                    st.did(dve.bn_stats(stats[:, :], xin[k][:, :]))
                    st.settle(alone=True)
                    dve.bn_aggr(mv[:, :], stats[:, :]).then_inc(stat_done, 1)
                    dve.wait_ge(rstd_done, n + 1)
                    dve.wait_ge(stat_done, n + 1)
                    if beyond(n, NB):
                        dve.wait_ge(x_ps, n - NB + 1)
                    dve.tensor_scalar(xn[:, slot, :], xin[k][:, :], mv[:, 0:1], rstd[:, 0:1],
                                      ALU.subtract, ALU.mult).then_inc(xn_done, 1)

                def keys_lo(b):
                    for c in range(DC):
                        dve.wait_ge(kT_hi, b * DC + c + 1)
                        dve.tensor_tensor(KT[:, LO, c, :], bank[1 + c % 2][:, 0:CTX], KT[:, HI, c, :],
                                          ALU.subtract).then_inc(kT_lo, 1)

                def rows_lo(t):
                    for i in range(NB):
                        dve.wait_ge(xg_hi, t * NB + i + 1)
                        dve.tensor_tensor(xgT[:, LO, :, i * S:(i + 1) * S],
                                          bank[1 + i % 2][:, 0:DC * S].rearrange("p (c s) -> p c s", c=DC),
                                          xgT[:, HI, :, i * S:(i + 1) * S], ALU.subtract).then_inc(xg_lo, 1)

                def project_lo(t):
                    for q in range(8):
                        dve.wait_ge(qk_hi, t * 8 + q + 1)
                        w = (qT, nkT)[q // DC]
                        dve.tensor_tensor(w[:, LO, q % DC, :], bank[(3, 5)[q % 2]][:, 0:NB * S],
                                          w[:, HI, q % DC, :], ALU.subtract).then_inc(qk_lo, 1)

                def new_values_lo(b, k):
                    dve.wait_ge(vn_hi, b + 1)
                    dve.tensor_tensor(Vn[k][:, LO, :], bank[3][0:S, :], Vn[k][:, HI, :],
                                      ALU.subtract).then_inc(vn_lo, 1)

                def attended_lo(b):
                    dve.wait_ge(oT_hi, b + 1)
                    dve.tensor_tensor(oT[:, LO, :, :].rearrange("p c s -> p (c s)"), bank[6][:, 0:DC * S],
                                      oT[:, HI, :, :].rearrange("p c s -> p (c s)"), ALU.subtract).then_inc(oT_lo, 1)

                def add(b, k):
                    dve.wait_ge(wo_ps, b + 1)
                    dve.wait_ge(xres_in[k], dma_count(b, k))
                    dve.scalar_tensor_tensor(out=xres[k][:, :], in0=bank[7][0:S, :], scalar=gains[0:S, 1:2],
                                             in1=xres[k][:, :], op0=ALU.mult, op1=ALU.add).then_inc(x3_done, 1)
                for n in range(NB):
                    norm(0, n)
                rows_lo(0)
                project_lo(0)
                keys_lo(0)
                new_values_lo(0, 0)
                norm(1, 0)

                def part(t, _):
                    for i in range(NB):
                        b, k = t * NB + i, i % 2
                        dve.wait_ge(s_ps, b + 1)
                        if beyond(b, 2):
                            dve.wait_ge(exp_done, b - 1)
                        st.did(dve.tensor_reduce(nmax[:, k:k + 1], bank[0][0:S, 0:KEYS], axis=AX.X, op=ALU.max,
                                                 negate=True))
                        st.settle()
                        dve.tensor_scalar(nmax[:, k:k + 1], nmax[:, k:k + 1], SCALE, None, ALU.mult
                                          ).then_inc(nmax_done, 1)
                        if i == NB - 1 and not last_of(t, GR):
                            rows_lo(t + 1)
                        if beyond(b, 1):
                            attended_lo(b - 1)
                        if not (last_of(t, GR) and i == NB - 1):
                            keys_lo(b + 1)
                        if beyond(b, 1):
                            add(b - 1, 1 - k)
                        if i == NB - 1 and not last_of(t, GR):
                            project_lo(t + 1)
                        dve.wait_ge(exp_done, b + 1)
                        if beyond(b, 2):
                            dve.wait_ge(o_done, b - 1)
                        dve.reciprocal(rinv[:, k:k + 1], esum[:, k:k + 1]).then_inc(rinv_done, 1)
                        dve.wait_ge(pT_hi, b + 1)
                        dve.tensor_tensor(pT[:, LO, 0:2, :].rearrange("p c s -> p (c s)"), bank[4][:, 0:2 * S],
                                          pT[:, HI, 0:2, :].rearrange("p c s -> p (c s)"), ALU.subtract)
                        dve.tensor_tensor(pT[0:LAST, LO, 2:4, :].rearrange("p c s -> p (c s)"),
                                          bank[4][0:LAST, 2 * S:4 * S],
                                          pT[0:LAST, HI, 2:4, :].rearrange("p c s -> p (c s)"),
                                          ALU.subtract).then_inc(pT_lo, 1)
                        if not (last_of(t, GR) and i == NB - 1):
                            new_values_lo(b + 1, (i + 1) % 2)
                        if normed_at(t, i):
                            norm(*normed_at(t, i))
                repeat(dve, st, GR, part, tail=2)
                attended_lo(B - 1)
                add(B - 1, 1)

            @block.tensor
            def _(pe):
                def turn_rows(t):
                    for i in range(NB):
                        pe.wait_ge(xn_done, t * NB + i + 1)
                        if i >= 2:
                            pe.wait_ge(xg_lo, t * NB + i - 1)
                        for c in range(DC):
                            ins = pe.transpose(bank[1 + i % 2][:, c * S:(c + 1) * S], xn[:, i, c * P:(c + 1) * P],
                                               ident[0:S, 0:S])
                        ins.then_inc(x_ps, 1)

                def turn_keys(b, k):
                    pe.wait_ge(crow_in[k], dma_count(b, k, 32))
                    for c in range(DC):
                        if c >= 2:
                            pe.wait_ge(kT_lo, b * DC + c - 1)
                        for r, (t0, rows) in enumerate(CT):
                            ins = pe.transpose(bank[1 + c % 2][:, t0:t0 + rows],
                                               crow[k][0:rows, r, c * P:(c + 1) * P], ident[0:rows, 0:rows])
                        ins.then_inc(kT_ps, 1)

                def project(t):
                    pe.wait_ge(xg_hi, t * NB + NB)
                    pe.wait_ge(xg_lo, t * NB + NB)
                    for q in range(8):
                        if q >= 2:
                            pe.wait_ge(qk_lo, t * 8 + q - 1)
                        w = (wqT, wkT)[q // DC]
                        n = 0
                        for c in range(DC):
                            for a, h in PAIRS:
                                ins = pe.matmul(bank[(3, 5)[q % 2]][:, 0:NB * S],
                                                w[:, h, c, (q % DC) * P:(q % DC + 1) * P], xgT[:, a, c, :],
                                                start=n == 0, stop=n == 11)
                                n += 1
                        ins.then_inc(qk_ps, 1)

                def new_values(b, i):
                    n = 0
                    for c in range(DC):
                        for a, h in PAIRS:
                            ins = pe.matmul(bank[3][0:S, :], xgT[:, a, c, i * S:(i + 1) * S], wvT[:, h, c, :],
                                            start=n == 0, stop=n == 11)
                            n += 1
                    ins.then_inc(vn_ps, 1)

                def turn_attended(b):
                    pe.wait_ge(o_done, b + 1)
                    if beyond(b, 1):
                        pe.wait_ge(oT_lo, b)
                    for c in range(DC):
                        ins = pe.transpose(bank[6][:, c * S:(c + 1) * S], o[:, c * P:(c + 1) * P], ident[0:S, 0:S])
                    ins.then_inc(oT_ps, 1)

                def output(b):
                    pe.wait_ge(oT_hi, b + 1)
                    pe.wait_ge(oT_lo, b + 1)
                    if beyond(b, 1):
                        pe.wait_ge(x3_done, b)
                    n = 0
                    for c in range(DC):
                        for a, h in PAIRS:
                            ins = pe.matmul(bank[7][0:S, :], oT[:, a, c, :], woT[:, h, c, :],
                                            start=n == 0, stop=n == 11)
                            n += 1
                    ins.then_inc(wo_ps, 1)
                turn_rows(0)
                project(0)
                pe.wait_ge(xg_lo, NB)
                turn_keys(0, 0)
                pe.wait_ge(qk_lo, 8)
                new_values(0, 0)

                def part(t, _):
                    for i in range(NB):
                        b, k = t * NB + i, i % 2
                        if i == 0:
                            pe.wait_ge(qk_hi, t * 8 + 8)
                            pe.wait_ge(qk_lo, t * 8 + 8)
                        pe.wait_ge(kT_hi, b * DC + DC)
                        pe.wait_ge(kT_lo, b * DC + DC)
                        if beyond(b, 1):
                            pe.wait_ge(exp_done, b)
                        for at, n_, keys in ((0, CTX, KT), (CTX, S, nkT)):
                            n = 0
                            for c in range(DC):
                                for a, h in PAIRS:
                                    rhs = keys[:, h, c, :] if n_ == CTX else keys[:, h, c, i * S:(i + 1) * S]
                                    ins = pe.matmul(bank[0][0:S, at:at + n_], qT[:, a, c, i * S:(i + 1) * S], rhs,
                                                    start=n == 0, stop=n == 11)
                                    n += 1
                        ins.then_inc(s_ps, 1)
                        if i == NB - 1 and not last_of(t, GR):
                            turn_rows(t + 1)
                            pe.wait_ge(xg_lo, t * NB + 2 * NB)
                        if beyond(b, 1):
                            turn_attended(b - 1)
                        if not (last_of(t, GR) and i == NB - 1):
                            turn_keys(b + 1, (i + 1) % 2)
                        if beyond(b, 1):
                            output(b - 1)
                        if i == NB - 1 and not last_of(t, GR):
                            pe.wait_ge(vn_lo, b + 1)
                            project(t + 1)
                        pe.wait_ge(exp_done, b + 1)
                        if beyond(b, 1):
                            pe.wait_ge(pT_lo, b)
                        for r, (t0, rows) in enumerate(VC):
                            rows = LAST if r == 3 else rows
                            ins = pe.transpose(bank[4][0:rows, r * S:(r + 1) * S], prob[:, t0:t0 + rows],
                                               ident[0:S, 0:S])
                        ins.then_inc(pT_ps, 1)
                        if not (last_of(t, GR) and i == NB - 1):
                            if i == NB - 1:
                                pe.wait_ge(qk_lo, t * 8 + 16)
                            else:
                                pe.wait_ge(vn_lo, b + 1)
                            new_values(b + 1, (i + 1) % NB)
                        pe.wait_ge(pT_hi, b + 1)
                        pe.wait_ge(pT_lo, b + 1)
                        pe.wait_ge(v_lo, b + 1)
                        pe.wait_ge(vn_lo, b + 1)
                        if beyond(b, 1):
                            pe.wait_ge(o_done, b)
                        n = 0
                        for r, (_, rows) in enumerate(VC):
                            for a, h in PAIRS:
                                rhs = Vn[k][:, h, :] if r == 3 else V[0:rows, h, r, :]
                                ins = pe.matmul(bank[5][0:S, :], pT[0:rows, a, r, :], rhs,
                                                start=n == 0, stop=n == 11)
                                n += 1
                        ins.then_inc(pv_ps, 1)
                repeat(pe, Steps(pe, None), GR, part, tail=1)
                turn_attended(B - 1)
                output(B - 1)


def mx_phase(nc, g, x3_d, out_f):
    ident, gains, bank = g["ident"], g["gains"], g["bank"]
    gateT, upT, downT = g["gateT"], g["upT"], g["downT"]
    HF = F // 2
    with ExitStack() as es:
        def sb(name, shape, dt=F32):
            return es.enter_context(nc.sbuf_tensor(name, shape, dt))

        def sem(name):
            return nc.alloc_semaphore(f"mx_{name}")

        xin = [sb(f"mxin{k}", [P, D]) for k in range(2)]
        xres = [sb(f"mxres{k}", [P, D]) for k in range(2)]
        xn, xr, xm, xq = (sb(n, [P, D]) for n in ("mxn", "mxr", "mxm", "mxq"))
        xqT = [sb(f"xqT{k}", [P, 2, DC, P], BF16) for k in range(2)]
        xamax, xscale, xinv = (sb(n, [P, D // MXB]) for n in ("xamax", "xscale", "xinv"))
        stats, mv, rstd, power = sb("mstats", [P, 6]), sb("mmv", [P, 2]), sb("mrstd", [P, 1]), sb("mpower", [P, 1])
        act_g = [sb(f"mact{k}", [P, D]) for k in range(2)]
        hraw, hr, hm, hq = (sb(n, [P, HF]) for n in ("hraw", "hr", "hm", "hq"))
        hamax, hscale, hinv = (sb(n, [P, HF // MXB]) for n in ("hamax", "hscale", "hinv"))
        hT = sb("mhT", [P, 2, 8, P], BF16)
        xin_in, xres_in, out_sent = ([sem(f"{n}{k}") for k in range(2)] for n in (
            "mxin_in", "mxres_in", "out_sent"))
        dve_c, pool_c, power_set = sem("dve_c6"), sem("pool_c6"), sem("power_set")
        stat_done, rstd_done, xn_done = sem("mstat"), sem("mrstd_done"), sem("mxn_done")
        xround_done, xdq_done, x_ps, xq_hi, xq_lo = (sem(n) for n in (
            "xround_done", "xdq_done", "mx_ps", "xq_hi", "xq_lo"))
        gu_ps, silu_done, h_done = sem("mgu_ps"), sem("msilu"), sem("mh_done")
        hround_done, hdq_done, hT_ps, hT_hi, hT_lo = (sem(n) for n in (
            "hround_done", "hdq_done", "mhT_ps", "mhT_hi", "mhT_lo"))
        y_ps, y_done = sem("y_ps"), sem("y_done")

        def dma_count(t, k):
            return t * 8 + (16 if k == 0 else 8)

        with nc.Block() as block:
            @block.sync
            def _(sp):
                def load(dst, t, k, signal):
                    sp.dma_start(dst[k][:, :], x3_d[bass.ds(t * P, P), :]).then_inc(signal[k], 16)
                for k in range(2):
                    load(xin, k, k, xin_in)
                    load(xres, k, k, xres_in)

                def part(t, k):
                    if not isinstance(t, int) or t < NT - 2:
                        sp.wait_ge(xn_done, t + 1)
                        load(xin, t + 2, k, xin_in)
                    sp.wait_ge(y_done, t + 1)
                    sp.dma_start(out_f[bass.ds(t * P, P), :], xres[k][:, :]).then_inc(out_sent[k], 16)
                    if not isinstance(t, int) or t < NT - 2:
                        sp.wait_ge(out_sent[k], dma_count(t, k))
                        load(xres, t + 2, k, xres_in)
                repeat(sp, Steps(sp, None), NT, part, unroll=2, tail=3)
                sp.wait_ge(out_sent[0], (NT + 1) // 2 * 16)
                sp.wait_ge(out_sent[1], NT // 2 * 16)

            @block.gpsimd
            def _(pool):
                st = Steps(pool, pool_c)
                pool.memset(power[:, :], -0.5).then_inc(power_set, 1)
                pool.wait_ge(power_set, 1)

                def rows(t):
                    pool.wait_ge(stat_done, t + 1)
                    apart(pool)
                    rsqrt(pool, st, rstd[:, :], mv[:, 1:2], power[:, :], rstd_done)
                    pool.wait_ge(xround_done, t + 1)
                    if later(t, 1):
                        pool.wait_ge(x_ps, t)
                    pool.tensor_tensor(blocks(xq[:, :]), blocks(xr[:, :]), wide(xscale[:, :], MXB),
                                       ALU.mult).then_inc(xdq_done, 1)
                rows(0)

                def part(t, _):
                    if not last_of(t, NT):
                        rows(t + 1)
                    for j in range(2):
                        q = 2 * t + j
                        pool.wait_ge(hround_done, q + 1)
                        if later(t, 1) or j:
                            pool.wait_ge(hT_ps, 2 * q)
                        pool.tensor_tensor(blocks(hq[:, :]), blocks(hr[:, :]), wide(hscale[:, :], MXB),
                                           ALU.mult).then_inc(hdq_done, 1)
                repeat(pool, st, NT, part, tail=1)

            @block.scalar
            def _(act):
                def rows_hi(t, k):
                    act.wait_ge(x_ps, t + 1)
                    act.activation(xqT[k][:, HI, :, :].rearrange("p c s -> p (c s)"), bank[7][:, :],
                                   ACT.Copy).then_inc(xq_hi, 1)

                def hidden_hi(q):
                    for v in range(2):
                        act.wait_ge(hT_ps, 2 * q + v + 1)
                        act.activation(hT[:, HI, 4 * v:4 * v + 4, :].rearrange("p c s -> p (c s)"),
                                       bank[4 + v][:, :], ACT.Copy).then_inc(hT_hi, 1)
                rows_hi(0, 0)

                def part(t, k):
                    for j in range(2):
                        q = 2 * t + j
                        for v in range(2):
                            act.wait_ge(gu_ps, 2 * q + v + 1)
                            act.activation(act_g[v][:, :], bank[v][:, :], ACT.Silu).then_inc(silu_done, 1)
                            if v == 0 and j == 1 and not last_of(t, NT):
                                rows_hi(t + 1, 1 - k)
                        if later(t, 1) or j:
                            hidden_hi(q - 1)
                repeat(act, Steps(act, None), NT, part, unroll=2, tail=1)
                hidden_hi(2 * NT - 1)

            @block.vector
            def _(dve):
                st = Steps(dve, dve_c)

                def rows(t, k):
                    dve.wait_ge(xin_in[k], dma_count(t, k))
                    st.did(dve.bn_stats(stats[:, :], xin[k][:, :]))
                    st.settle(alone=True)
                    dve.bn_aggr(mv[:, :], stats[:, :]).then_inc(stat_done, 1)
                    dve.wait_ge(rstd_done, t + 1)
                    dve.tensor_scalar(xn[:, :], xin[k][:, :], mv[:, 0:1], rstd[:, 0:1],
                                      ALU.subtract, ALU.mult).then_inc(xn_done, 1)
                    dve.wait_ge(xn_done, t + 1)
                    if later(t, 1):
                        dve.wait_ge(xdq_done, t)
                    mx_scales(dve, st, xn[:, :], xamax[:, :], xscale[:, :], xinv[:, :])
                    mx_round(dve, st, xn[:, :], xinv[:, :], xr[:, :], xm[:, :])
                    dve.tensor_tensor(xr[:, :], xr[:, :], xm[:, :], ALU.subtract).then_inc(xround_done, 1)

                def rows_lo(t, k):
                    dve.wait_ge(xq_hi, t + 1)
                    dve.tensor_tensor(xqT[k][:, LO, :, :].rearrange("p c s -> p (c s)"), bank[7][:, :],
                                      xqT[k][:, HI, :, :].rearrange("p c s -> p (c s)"),
                                      ALU.subtract).then_inc(xq_lo, 1)

                def hidden_lo(q):
                    for v in range(2):
                        dve.wait_ge(hT_hi, 2 * q + v + 1)
                        dve.tensor_tensor(hT[:, LO, 4 * v:4 * v + 4, :].rearrange("p c s -> p (c s)"),
                                          bank[4 + v][:, :],
                                          hT[:, HI, 4 * v:4 * v + 4, :].rearrange("p c s -> p (c s)"),
                                          ALU.subtract).then_inc(hT_lo, 1)

                def add(t, k):
                    dve.wait_ge(y_ps, t + 1)
                    dve.wait_ge(xres_in[k], dma_count(t, k))
                    row = xres[k][:, :].rearrange("p (q r) -> p r q", r=4)
                    dve.scalar_tensor_tensor(out=row, in0=bank[6][:, :].rearrange("p (r q) -> p r q", r=4),
                                             scalar=gains[:, 3:4], in1=row, op0=ALU.mult, op1=ALU.add
                                             ).then_inc(y_done, 1)
                rows(0, 0)
                rows_lo(0, 0)

                def part(t, k):
                    for j in range(2):
                        q = 2 * t + j
                        for v in range(2):
                            dve.wait_ge(silu_done, 2 * q + v + 1)
                            dve.tensor_tensor(hraw[:, v * D:(v + 1) * D], act_g[v][:, :], bank[2 + v][:, :],
                                              ALU.mult).then_inc(h_done, 1)
                            if v == 0 and j == 0 and not last_of(t, NT):
                                rows(t + 1, 1 - k)
                            if v == 0 and j == 1:
                                if not last_of(t, NT):
                                    rows_lo(t + 1, 1 - k)
                                if later(t, 1):
                                    add(t - 1, 1 - k)
                        if later(t, 1) or j:
                            hidden_lo(q - 1)
                            dve.wait_ge(hdq_done, q)
                        dve.wait_ge(h_done, 2 * q + 2)
                        mx_scales(dve, st, hraw[:, :], hamax[:, :], hscale[:, :], hinv[:, :])
                        mx_round(dve, st, hraw[:, :], hinv[:, :], hr[:, :], hm[:, :])
                        dve.tensor_tensor(hr[:, :], hr[:, :], hm[:, :], ALU.subtract).then_inc(hround_done, 1)
                repeat(dve, st, NT, part, unroll=2, tail=1)
                hidden_lo(2 * NT - 1)
                add(NT - 1, (NT - 1) % 2)

            @block.tensor
            def _(pe):
                def turn_rows(t):
                    pe.wait_ge(xdq_done, t + 1)
                    if later(t, 1):
                        pe.wait_ge(xq_lo, t)
                    for c in range(DC):
                        ins = pe.transpose(bank[7][:, c * P:(c + 1) * P], xq[:, c * P:(c + 1) * P], ident[:, :])
                    ins.then_inc(x_ps, 1)

                def gate_up(t, k, j, v):
                    q = 2 * t + j
                    if later(t, 1) or j:
                        pe.wait_ge(h_done, 2 * q + v - 1)
                    i0 = j * HF + v * D
                    for u, w in enumerate((gateT, upT)):
                        n = 0
                        for c in range(DC):
                            for a, h in PAIRS:
                                ins = pe.matmul(bank[2 * u + v][:, :], xqT[k][:, a, c, :], w[:, h, c, i0:i0 + D],
                                                start=n == 0, stop=n == 11)
                                n += 1
                    ins.then_inc(gu_ps, 1)

                def turn_hidden(q):
                    pe.wait_ge(hdq_done, q + 1)
                    for v in range(2):
                        if later(q, 1):
                            pe.wait_ge(hT_lo, 2 * q - 1 + v)
                        for c in range(4):
                            at = (4 * v + c) * P
                            ins = pe.transpose(bank[4 + v][:, c * P:(c + 1) * P], hq[:, at:at + P], ident[:, :])
                        ins.then_inc(hT_ps, 1)

                def down(t, j):
                    pe.wait_ge(hT_hi, 4 * t + 2 * j + 2)
                    pe.wait_ge(hT_lo, 4 * t + 2 * j + 2)
                    if j == 0 and later(t, 1):
                        pe.wait_ge(y_done, t)
                    n = 0
                    for c in range(8):
                        for a, h in PAIRS:
                            ins = pe.matmul(bank[6][:, :].rearrange("p (r q) -> p r q", r=4), hT[:, a, c, :],
                                            downT[:, h, 2 * j + c // 4:16:4, c % 4, :],
                                            start=n == 0 and j == 0, stop=n == 23 and j == 1)
                            n += 1
                    if j == 1:
                        ins.then_inc(y_ps, 1)
                turn_rows(0)

                def part(t, k):
                    pe.wait_ge(xq_hi, t + 1)
                    pe.wait_ge(xq_lo, t + 1)
                    for j in range(2):
                        gate_up(t, k, j, 0)
                        if later(t, 1):
                            down(t - 1, j)
                        if j == 1 and not last_of(t, NT):
                            turn_rows(t + 1)
                        gate_up(t, k, j, 1)
                        if later(t, 1) or j:
                            turn_hidden(2 * t + j - 1)
                repeat(pe, Steps(pe, None), NT, part, unroll=2, tail=1)
                down(NT - 1, 0)
                turn_hidden(2 * NT - 1)
                down(NT - 1, 1)


_INS = ["x", "ctx_2048", "g_xattn", "g_ffn", "L0_xattn_decay", "L0_xattn_W_in", "L0_xattn_b_in",
        "L0_xattn_W_out", "L0_xattn_b_out", "L0_xattn_gamma", "L0_xattn_beta", "L0_ffn_gate_w",
        "L0_ffn_w_gate", "L0_ffn_w_up", "L0_ffn_w_down", "L0_ffn_ws_gate", "L0_ffn_ws_up",
        "L0_ffn_ws_down", "L1_xattn_wq", "L1_xattn_wk", "L1_xattn_wv", "L1_xattn_wo",
        "L1_ffn_gate_w", "L1_ffn_up_w", "L1_ffn_down_w"]


def kernel(**inputs):
    import numpy as np
    import concourse.bacc as bacc
    from concourse.bass_utils import run_bass_kernel_spmd

    nc = bacc.Bacc("TRN2", target_bir_lowering=False, num_devices=1)
    arrays, args = {}, []
    for name in _INS:
        a = np.ascontiguousarray(inputs[name])
        if a.ndim == 0:
            a = a.reshape(1)
        arrays[f"in_{name}"] = a
        args.append(nc.dram_tensor(f"in_{name}", a.shape, mybir.dt.from_np(a.dtype), kind="ExternalInput").ap())
    out = nc.dram_tensor("out_0", (B, S, D), F32, kind="ExternalOutput").ap()
    program(nc, *args, out)
    r = run_bass_kernel_spmd(nc, [arrays], core_ids=[0])
    return r.results[0]["out_0"]
```

```python
from contextlib import ExitStack

import concourse.bass as bass
from concourse import mybir

F32 = mybir.dt.float32
BF16 = mybir.dt.bfloat16
U32 = mybir.dt.uint32
I32 = mybir.dt.int32
ALU = mybir.AluOpType
ACT = mybir.ActivationFunctionType
AX = mybir.AxisListType

P = 128
B, S, D = 32, 100, 512
TOK = B * S
NT = TOK // P
DC = D // P
CTX = 361
CT = [(0, 128), (128, 128), (256, CTX - 256)]
LAST = CTX - 256
E, I, CAP = 16, 352, 256
IC = [(0, 128), (128, 128), (256, I - 256)]
IS = 704
SC = [(128 * m, min(128, IS - 128 * m)) for m in range(6)]
F = 2048
GT = 5
NG = NT // GT
LN_EPS = 1e-5
FP8_MAX, MX_EPS, MXB = 448.0, 1e-30, 32
HI, LO = 0, 1
PAIRS = [(HI, HI), (HI, LO), (LO, HI)]


class Steps:

    def __init__(self, eng, sem):
        self.eng, self.sem, self.n, self.base = eng, sem, 0, 0

    def did(self, ins):
        ins.then_inc(self.sem, 1)
        self.n += 1

    def settle(self, alone=False):
        self.eng.wait_ge(self.sem, self.base + self.n)
        if alone:
            apart(self.eng)


def apart(eng):
    eng.nop(nofuse=True)


def repeat(eng, steps, count, body, unroll=1, head=0, tail=0):
    start = max(head, unroll)
    for t in range(start):
        n0 = steps.n
        body(t, t % unroll)
        per = steps.n - n0
    end = start + (count - start - tail) // unroll * unroll
    if end > start:
        n1 = steps.n
        with eng.Fori(start, end - unroll + 1, unroll) as t:
            steps.base = (t - start) * per
            for k in range(unroll):
                body(t + k if k else t, k)
        steps.base, steps.n = 0, n1 + (end - start) * per
    for t in range(end, count):
        body(t, t % unroll)


def later(t, n):
    return not isinstance(t, int) or t >= n


def wide(ap, n):
    return ap.unsqueeze(2).to_broadcast([ap.shape[0], ap.shape[1], n])


def blocks(ap, n=MXB):
    return ap.rearrange("p (b n) -> p b n", n=n)


def mx_scales(dve, st, src, amax, scale, inv):
    st.did(dve.tensor_reduce(amax, blocks(src), axis=AX.X, op=ALU.max, apply_absolute_value=True))
    st.settle()
    st.did(dve.tensor_scalar(scale, amax, 1.0 / FP8_MAX, MX_EPS, ALU.mult, ALU.max))
    st.settle()
    st.did(dve.reciprocal(inv, scale))
    st.settle()


def mx_round(dve, st, src, inv, r, m, done=None):
    st.did(dve.tensor_tensor(blocks(r), blocks(src), wide(inv, MXB), ALU.mult))
    st.settle()
    st.did(dve.tensor_scalar(m.bitcast(U32), r.bitcast(U32), 0x7F800000, 0xFFFFFFFF,
                             ALU.bitwise_and, ALU.bitwise_and))
    st.settle()
    st.did(dve.tensor_scalar(m, m, 2.0 ** -6, 1.5 * 2.0 ** 20, ALU.max, ALU.mult))
    st.settle()
    ins = dve.tensor_tensor(r, r, m, ALU.add)
    if done is None:
        st.did(ins)
        st.settle()
    else:
        ins.then_inc(done, 1)


def program(nc, x, ctx, g_xattn, g_ffn, decay, W_in, b_in, W_out, b_out, gamma, beta,
            gate_w, w_gate, w_up, w_down, ws_gate, ws_up, ws_down,
            wq, wk, wv, wo, gate2, up2, down2, out):
    x1_d = nc.dram_tensor("x1_d", (TOK, D), F32, kind="Internal").ap()
    x2_d = nc.dram_tensor("x2_d", (TOK, D), F32, kind="Internal").ap()
    x3_d = nc.dram_tensor("x3_d", (TOK, D), F32, kind="Internal").ap()
    xs_d = nc.dram_tensor("xs_d", (TOK, D), F32, kind="Internal").ap()
    pick_d = nc.dram_tensor("pick_d", (TOK, 4), U32, kind="Internal").ap()
    slots_d = nc.dram_tensor("slots_d", (E * CAP, 2 * D), BF16, kind="Internal").ap()
    eout_d = nc.dram_tensor("eout_d", (E * CAP, D), F32, kind="Internal").ap()
    x_f = x.rearrange("b s d -> (b s) d")
    out_f = out.rearrange("b s d -> (b s) d")
    with ExitStack() as keep:
        def sb(name, shape, dt=F32):
            return keep.enter_context(nc.sbuf_tensor(name, shape, dt))

        g = {}
        g["ident"] = sb("ident", [P, P])
        g["identb"] = sb("identb", [P, P], BF16)
        g["gains"] = sb("gains", [P, 4])
        g["gateT"] = sb("gateT", [P, 2, DC, F], BF16)
        g["upT"] = sb("upT", [P, 2, DC, F], BF16)
        g["bank"] = [keep.enter_context(nc.psum_tensor(f"bank{i}", [P, 512], F32)) for i in range(8)]
        with ExitStack() as l0:
            g["summary"] = l0.enter_context(nc.sbuf_tensor("summary", [B, 3, D], BF16))
            with nc.cleanup_on_exit():
                summary_phase(nc, g, ctx, g_xattn, g_ffn, decay, W_in, b_in, W_out, b_out,
                              gate2, up2)
            with nc.cleanup_on_exit():
                route_phase(nc, g, x_f, gamma, beta, gate_w, ws_gate, ws_up, ws_down,
                            x1_d, xs_d, pick_d, slots_d)
        g["downT"] = sb("downT", [P, 2, 16, DC, P], BF16)
        with ExitStack() as l1:
            g["wT"] = l1.enter_context(nc.sbuf_tensor("wT", [P, 2, DC, 4, D], BF16))
            with nc.cleanup_on_exit():
                expert_phase(nc, g, w_gate, w_up, w_down, down2, (wq, wk, wv, wo), slots_d, eout_d)
            with nc.cleanup_on_exit():
                attention_phase(nc, g, ctx, xs_d, pick_d, eout_d, x2_d, x3_d)
        with nc.cleanup_on_exit():
            mx_phase(nc, g, x3_d, out_f)


def summary_phase(nc, g, ctx, g_xattn, g_ffn, decay, W_in, b_in, W_out, b_out,
                  gate2, up2):
    ident, identb, gains, bank = g["ident"], g["identb"], g["gains"], g["bank"]
    summary = g["summary"]
    STEPS = F // P
    with ExitStack() as es:
        def sb(name, shape, dt=F32):
            return es.enter_context(nc.sbuf_tensor(name, shape, dt))

        def sem(name):
            return nc.alloc_semaphore(f"summary_{name}")

        crow = [sb(f"crow{k}", [P, 3, D]) for k in range(4)]
        wrow = sb("wrow", [P, CTX])
        kcol = sb("kcol", [P, 2])
        krow = sb("krow", [P, CTX])
        diag = sb("diag", [P, 3, CTX])
        picked = sb("picked", [P, CTX])
        wsum = sb("wsum", [P, 4])
        wcol = sb("wcol", [P, 3, 4, 4])
        four = sb("four", [4, D])
        wstage = [sb(f"wstage{k}", [P, 2, D]) for k in range(2)]
        wr = [sb(f"wr{k}", [P, 2, D]) for k in range(2)]
        wm = [sb(f"wm{k}", [P, 2, D]) for k in range(2)]
        dq = [sb(f"dq{k}", [P, 2, D]) for k in range(2)]
        scale = [sb(f"scale{k}", [P, 32]) for k in range(2)]
        amax, inv = sb("amax", [P, 32]), sb("inv", [P, 32])
        bias2 = sb("bias2", [B, 2, D])
        WT = [sb(f"WT{k}", [P, DC, D]) for k in range(2)]
        sumrow = sb("sumrow", [B, 2, D])
        sumT = [sb(f"sumT{n}", [P, DC, B]) for n in range(2)]
        left = sb("left", [B, D])
        gains_in, bias_in, sq_in = sem("gains_in"), sem("bias_in"), sem("sq_in")
        row_a = [sem(f"row_a{k}") for k in range(4)]
        wst_in = [sem(f"wst_in{k}") for k in range(2)]
        pool_c, dve_c, act_tanh = sem("pool_c"), sem("dve_c"), sem("act_tanh")
        masks_made = sem("masks_made")
        weights_ready = sem("weights_ready")
        row_mm, four_out, four_ps, four_kept = (sem(n) for n in ("row_mm", "four_out", "four_ps", "four_kept"))
        left_done = sem("left_done")
        round_done, dq_done, wT_ps, wT_hi, wT_lo = (sem(n) for n in (
            "round_done", "dq_done", "wT_ps", "wT_hi", "wT_lo"))
        sq_ps, sq_ev, fin_ps, fin_act, fin_dve = (sem(n) for n in (
            "sq_ps", "sq_ev", "fin_ps", "fin_act", "fin_dve"))
        sqs = [sb(f"square{n}", [P, DC, D]) for n in range(2)]
        with nc.Block() as block:
            @block.sync
            def _(sp):
                for n, src in enumerate((g_xattn, g_ffn)):
                    sp.dma_start(gains[:, 2 * n:2 * n + 2],
                                 src.rearrange("(a n) -> a n", a=1).to_broadcast([P, 2])).then_inc(gains_in, 16)
                sp.dma_start(kcol[:, 0:1],
                             decay.rearrange("(a n) -> a n", a=1).to_broadcast([P, 1])).then_inc(gains_in, 16)
                for n, src in enumerate((b_in, b_out)):
                    sp.dma_start(bias2[:, n, :],
                                 src.rearrange("(a n) -> a n", a=1).to_broadcast([B, D])).then_inc(bias_in, 16)

                def load(t, k):
                    if later(t, 2):
                        sp.wait_ge(round_done, t - 1)
                    sp.dma_start(wstage[k][:, 0, :], gate2[bass.ds(t * P, P), :]).then_inc(wst_in[k], 16)
                    sp.dma_start(wstage[k][:, 1, :], up2[bass.ds(t * P, P), :]).then_inc(wst_in[k], 16)
                    for i in range(2):
                        b = 2 * t + i
                        if later(t, 2):
                            sp.wait_ge(row_mm, 2 * t - 3 + i)
                        row = ctx[bass.ds(b, 1), :, :].rearrange("a t d -> (a t) d")
                        sp.dma_start(crow[2 * k + i][:, 0:2, :],
                                     row[0:256, :].rearrange("(c p) d -> p c d", p=P)).then_inc(row_a[2 * k + i], 16)
                        sp.dma_start(crow[2 * k + i][0:LAST, 2, :], row[256:CTX, :]).then_inc(row_a[2 * k + i], 16)
                    if isinstance(t, int) and t == 1:
                        for n, src in enumerate((W_in, W_out)):
                            sp.dma_start(sqs[n][:, :, :], src.rearrange("(c p) n -> p c n", p=P)).then_inc(sq_in, 16)
                repeat(sp, Steps(sp, None), STEPS, load, unroll=2)

            @block.gpsimd
            def _(pool):
                st = Steps(pool, pool_c)
                st.did(pool.memset(ident[:, :], 0.0))
                st.did(pool.memset(diag[:, :, :], 0.0))
                st.did(pool.memset(wcol[:, :, :, :], 0.0))
                st.settle()
                pool.affine_select(out=ident[:, :], in_=ident[:, :], compare_op=ALU.not_equal, fill=1.0,
                                   base=0, pattern=[[-1, P]], channel_multiplier=1).then_inc(masks_made, 1)
                pool.affine_select(out=diag[:, :, :], in_=diag[:, :, :], compare_op=ALU.not_equal, fill=1.0,
                                   base=1 - CTX, pattern=[[P, 3], [1, CTX]], channel_multiplier=1
                                   ).then_inc(masks_made, 1)
                pool.wait_ge(masks_made, 2)
                pool.tensor_copy(identb[:, :], ident[:, :]).then_inc(masks_made, 1)

                def part(t, k):
                    pool.wait_ge(round_done, t + 1)
                    if later(t, 2):
                        pool.wait_ge(wT_ps, 2 * t - 2)
                    r = wr[k][:, :, :].rearrange("p a n -> p (a n)")
                    pool.tensor_tensor(r, r, wm[k][:, :, :].rearrange("p a n -> p (a n)"), ALU.subtract
                                       ).then_inc(left_done, 1)
                    pool.wait_ge(left_done, t + 1)
                    pool.tensor_tensor(blocks(dq[k][:, :, :].rearrange("p a n -> p (a n)")),
                                       blocks(wr[k][:, :, :].rearrange("p a n -> p (a n)")),
                                       wide(scale[k][:, :], MXB), ALU.mult).then_inc(dq_done, 1)
                repeat(pool, Steps(pool, None), STEPS, part, unroll=2)

            @block.scalar
            def _(act):
                act.wait_ge(gains_in, 48)
                act.activation(gains[:, :], gains[:, :], ACT.Tanh).then_inc(act_tanh, 1)
                act.activation(kcol[:, 1:2], kcol[:, 0:1], ACT.Tanh, scale=0.5).then_inc(act_tanh, 1)

                def keep_four(t):
                    act.wait_ge(four_ps, t)
                    act.activation(sumT[0][:, :, bass.ds(2 * t - 4, 4)],
                                   bank[3][:, 0:DC * 4].rearrange("p (c b) -> p c b", c=DC), ACT.Copy
                                   ).then_inc(four_kept, 2)

                def part(t, k):
                    if k == 0 and later(t, 2):
                        keep_four(t)
                    if k == 1:
                        act.wait_ge(row_mm, 2 * t + 2)
                        if later(t, 2):
                            act.wait_ge(four_ps, t - 1)
                        act.activation(four[:, :], bank[0][0:4, :], ACT.Copy).then_inc(four_out, 2)
                    for n in range(2):
                        act.wait_ge(wT_ps, 2 * t + n + 1)
                        act.activation((g["gateT"], g["upT"])[n][:, HI, :, bass.ds(t * P, P)],
                                       bank[1 + n][:, :].rearrange("p (c i) -> p c i", c=DC),
                                       ACT.Copy).then_inc(wT_hi, 1)
                    if isinstance(t, int) and t == STEPS - 2:
                        for n in range(8):
                            act.wait_ge(sq_ps, n + 1)
                            act.activation(WT[n // 4][:, n % 4, :], bank[4 + n % 4][:, :], ACT.Copy
                                           ).then_inc(sq_ev, 1)
                repeat(act, Steps(act, None), STEPS, part, unroll=2, tail=2)
                keep_four(STEPS)
                act.wait_ge(fin_ps, 2)
                act.activation(sumT[1][:, :, :], bank[5][:, 0:DC * B].rearrange("p (c b) -> p c b", c=DC),
                               ACT.Copy).then_inc(fin_act, 1)

            @block.vector
            def _(dve):
                st = Steps(dve, dve_c)
                st.did(dve.memset(krow[:, :], 1.0))
                dve.wait_ge(act_tanh, 2)
                st.did(dve.tensor_scalar(kcol[:, 0:1], kcol[:, 1:2], 0.5, 0.5, ALU.mult, ALU.add))
                st.settle()
                st.did(dve.tensor_scalar(picked[:, :], krow[:, :], kcol[:, 0:1], None, ALU.mult))
                st.settle()
                st.did(dve.tensor_tensor_scan(wrow[:, :], picked[:, :], krow[:, :], 0.0, ALU.mult, ALU.add))
                st.settle()
                st.did(dve.tensor_scalar(wrow[:, :], wrow[:, :], 1.0 / CTX, None, ALU.mult))
                st.settle()
                dve.wait_ge(masks_made, 2)
                for c in range(3):
                    st.did(dve.tensor_tensor(picked[:, :], wrow[:, :], diag[:, c, :], ALU.mult))
                    st.settle()
                    st.did(dve.tensor_reduce(wsum[:, c:c + 1], picked[:, :], axis=AX.X, op=ALU.add))
                    st.settle()
                st.did(dve.tensor_reduce(wsum[:, 3:4], wrow[:, :], axis=AX.X, op=ALU.add))
                st.settle()
                for m in range(4):
                    dve.tensor_copy(wcol[:, :, m, m], wsum[:, 0:3]).then_inc(weights_ready, 1)

                def low(t):
                    for n in range(2):
                        dve.wait_ge(wT_hi, 2 * t + n + 1)
                        w = (g["gateT"], g["upT"])[n]
                        dve.tensor_tensor(w[:, LO, :, bass.ds(t * P, P)],
                                          bank[1 + n][:, :].rearrange("p (c i) -> p c i", c=DC),
                                          w[:, HI, :, bass.ds(t * P, P)], ALU.subtract).then_inc(wT_lo, 1)

                def part(t, k):
                    dve.wait_ge(wst_in[k], t * 16 + (32 if k == 0 else 16))
                    if later(t, 2):
                        dve.wait_ge(dq_done, t - 1)
                    flat, r, m = (v[:, :, :].rearrange("p a n -> p (a n)") for v in (wstage[k], wr[k], wm[k]))
                    mx_scales(dve, st, flat, amax[:, :], scale[k][:, :], inv[:, :])
                    mx_round(dve, st, flat, inv[:, :], r, m, round_done)
                    if later(t, 1):
                        low(t - 1)
                    dve.wait_ge(round_done, t + 1)
                repeat(dve, st, STEPS, part, unroll=2)
                low(STEPS - 1)
                dve.wait_ge(bias_in, 32)
                st.did(dve.tensor_scalar(bias2[:, 0, :], bias2[:, 0, :], wsum[0:B, 3:4], None, ALU.mult))
                st.settle()
                for n in range(2):
                    dve.wait_ge(fin_ps, 1 + 2 * n)
                    dve.tensor_tensor(sumrow[:, n, :], bank[6 + n][0:B, :], bias2[:, n, :],
                                      ALU.add).then_inc(fin_dve, 1)
                dve.wait_ge(fin_dve, 2)
                st.did(dve.tensor_copy(summary[:, 0, :], sumrow[:, 1, :]))
                st.settle()
                st.did(dve.tensor_tensor(left[:, :], sumrow[:, 1, :], summary[:, 0, :], ALU.subtract))
                st.settle()
                st.did(dve.tensor_copy(summary[:, 1, :], left[:, :]))
                st.settle()
                st.did(dve.tensor_tensor(summary[:, 2, :], left[:, :], summary[:, 1, :], ALU.subtract))

            @block.tensor
            def _(pe):
                pe.wait_ge(masks_made, 1)
                pe.wait_ge(weights_ready, 4)

                def turn_four(t):
                    pe.wait_ge(four_out, t)
                    if later(t, 3):
                        pe.wait_ge(four_kept, t - 2)
                    apart(pe)
                    for c in range(DC):
                        ins = pe.transpose(bank[3][:, c * 4:c * 4 + 4], four[:, c * P:(c + 1) * P],
                                           ident[0:4, 0:4])
                    ins.then_inc(four_ps, 2)

                def part(t, k):
                    if k == 0 and later(t, 2):
                        turn_four(t)
                    for i in range(2):
                        pe.wait_ge(row_a[2 * k + i], t * 16 + (32 if k == 0 else 16))
                        m = 2 * k + i
                        for r, (_, rows) in enumerate(CT):
                            ins = pe.matmul(bank[0][0:4, :], wcol[0:rows, r, m, :], crow[m][0:rows, r, :],
                                            start=m == 0 and r == 0, stop=m == 3 and r == 2)
                        ins.then_inc(row_mm, 1)
                    pe.wait_ge(dq_done, t + 1)
                    for n in range(2):
                        if later(t, 1):
                            pe.wait_ge(wT_lo, 2 * t - 1 + n)
                        for c in range(DC):
                            ins = pe.transpose(bank[1 + n][:, c * P:(c + 1) * P], dq[k][:, n, c * P:(c + 1) * P],
                                               ident[:, :])
                        ins.then_inc(wT_ps, 1)
                    if isinstance(t, int) and t == STEPS - 2:
                        squares()

                def squares():
                    pe.wait_ge(sq_in, 32)
                    for n in range(2):
                        for c in range(DC):
                            if n:
                                pe.wait_ge(sq_ev, c + 1)
                            for r in range(DC):
                                ins = pe.transpose(bank[4 + c][:, r * P:(r + 1) * P],
                                                   sqs[n][:, r, c * P:(c + 1) * P], ident[:, :])
                            ins.then_inc(sq_ps, 1)
                repeat(pe, Steps(pe, None), STEPS, part, unroll=2, tail=2)
                turn_four(STEPS)
                pe.wait_ge(sq_ev, 8)
                for n in range(2):
                    if n:
                        pe.wait_ge(fin_dve, 1)
                        for c in range(DC):
                            ins = pe.transpose(bank[5][:, c * B:(c + 1) * B], sumrow[:, 0, c * P:(c + 1) * P],
                                               ident[0:B, 0:B])
                        ins.then_inc(fin_ps, 1)
                    if n:
                        pe.wait_ge(fin_act, 1)
                    else:
                        pe.wait_ge(four_kept, STEPS)
                    for c in range(DC):
                        ins = pe.matmul(bank[6 + n][0:B, :], sumT[n][:, c, :], WT[n][:, c, :],
                                        start=c == 0, stop=c == DC - 1)
                    ins.then_inc(fin_ps, 1)


def row_stats(dve, st, src, stats, tiles):
    for j in tiles:
        st.did(dve.bn_stats(stats[:, j, :], src(j)))


def row_moments(dve, st, stats, mv, count, done):
    st.settle(alone=True)
    for j in range(count - 1):
        st.did(dve.bn_aggr(mv[:, j, :], stats[:, j, :]))
    dve.bn_aggr(mv[:, count - 1, :], stats[:, count - 1, :]).then_inc(done, 1)


def rsqrt(pool, st, rstd, mv, power, done):
    st.did(pool.tensor_scalar(rstd, mv, LN_EPS, None, ALU.add))
    st.settle()
    pool.tensor_tensor(rstd, rstd, power, ALU.pow).then_inc(done, 1)


def last_of(t, count):
    return isinstance(t, int) and t == count - 1


def route_phase(nc, g, x_f, gamma, beta, gate_w, ws_gate, ws_up, ws_down, x1_d, xs_d, pick_d, slots_d):
    ident, gains, bank, summary = g["ident"], g["gains"], g["bank"], g["summary"]
    SUBS = [(0, 3), (3, 2)]
    HALVES = (slice(0, 3), slice(3, GT))
    NQ = 12
    TURN = (0, 1, 2, 3, 6)
    RANK = P
    with ExitStack() as es:
        def sb(name, shape, dt=F32):
            return es.enter_context(nc.sbuf_tensor(name, shape, dt))

        def sem(name):
            return nc.alloc_semaphore(f"route_{name}")

        x, y, xr = sb("x", [P, GT, D]), sb("y", [P, GT, D]), sb("xr", [P, GT, D])
        rows = sb("rows", [P, GT, 2, D], BF16)
        xT = sb("xT", [P, GT, 2, DC, P], BF16)
        gamma_b, beta_b = sb("gamma_b", [P, D]), sb("beta_b", [P, D])
        own = sb("own", [B, TOK], BF16)
        before, ones = sb("before", [P, P], BF16), sb("ones", [P, P], BF16)
        iota_i, iota_f = sb("iota_i", [P, E], I32), sb("iota_f", [P, E])
        gw = sb("gw", [E, D])
        gwT = sb("gwT", [P, 2, DC, E], BF16)
        stats, mv = sb("stats", [P, GT, 6]), sb("mv", [P, GT, 2])
        rstd, power = sb("rstd", [P, GT]), sb("power", [P, GT])
        nmax, esum, rsum = sb("nmax", [P, GT]), sb("esum", [P, GT]), sb("rsum", [P, GT])
        probs = sb("probs", [P, GT, E])
        top8, top8i = sb("top8", [P, GT, 8]), sb("top8i", [P, GT, 8], U32)
        chosen = sb("chosen", [P, GT * 2])
        hot, hit = sb("hot", [P, GT * 2, E]), sb("hit", [P, GT * 2, E])
        picks = sb("picks", [P, GT, E], BF16)
        counts = sb("counts", [P, GT + 1, E], BF16)
        pos, slot, over = sb("pos", [P, GT * 2]), sb("slot", [P, GT * 2]), sb("over", [P, GT * 2])
        sidx = sb("sidx", [P, GT * 2], U32)
        pick = sb("pick", [P, GT, 4], U32)
        spare = sb("spare", [P, 1])
        zeros = sb("zeros", [P, D], BF16)
        zero_set, slots_zero = sem("zero_set"), sem("slots_zero")
        gs, us = (sb(n, [P, 2, DC, IS], BF16) for n in ("gs", "us"))
        ds_ = sb("ds_", [P, 2, 6, D], BF16)
        sg = [sb(f"sg{k}", [P, 3 * P]) for k in range(2)]
        hs = [sb(f"hs{k}", [P, 3 * P]) for k in range(2)]
        hT = sb("hsT", [P, 2, 6, GT * P], BF16)
        raw = hT[:, :, :, :].rearrange("p h m s -> p (h m s)").bitcast(F32)
        raw_in, raw_hi, raw_lo = sem("raw_in"), sem("raw_hi"), sem("raw_lo")
        x_in, gb_in = sem("x_in"), sem("gb_in")
        made, pool_c, pool_f, dve_c = sem("made"), sem("pool_c"), sem("pool_f"), sem("dve_c")
        gw_in, gw_ps, gw_hi, gw_lo = (sem(n) for n in ("gw_in", "gw_ps", "gw_hi", "gw_lo"))
        stat_done, rstd_done, y_done, xb_done = sem("stat_done"), sem("rstd_done"), sem("y_done"), sem("xb_done")
        own_ps, own_added, scaled, x1_done, xn_done = (sem(n) for n in (
            "own_ps", "own_added", "scaled", "x1_done", "xn_done"))
        rows_hi, rows_lo, scattered = sem("rows_hi"), sem("rows_lo"), sem("scattered")
        xT_ps, xT_hi, xT_lo = sem("xT_ps"), sem("xT_hi"), sem("xT_lo")
        x1_out, xr_in, xr_out, pick_out = sem("x1_out"), sem("xr_in"), sem("xr_out"), sem("pick_out")
        logit_ps, nmax_done, exp_done = sem("logit_ps"), sem("nmax_done"), sem("exp_done")
        picks_done, rank_ps, sidx_done = sem("picks_done"), sem("rank_ps"), sem("sidx_done")
        gu_ps, silu_done, h_done, hT_hi, hT_lo = (sem(n) for n in (
            "gu_ps", "silu_done", "h_done", "hT_hi", "hT_lo"))
        down_ps, xr_done = sem("down_ps"), sem("xr_done")
        rowsof = x_f.rearrange("(t p) d -> p t d", p=P)
        x1of = x1_d.rearrange("(t p) d -> p t d", p=P)
        xsof = xs_d.rearrange("(t p) d -> p t d", p=P)
        pickof = pick_d.rearrange("(t p) k -> p t k", p=P)

        def routes(t):
            return not last_of(t, NG + 1)

        def shares(t):
            return later(t, 1)

        def chunk(q):
            return SUBS[q // 6], q % 6, SC[q % 6]

        def raw_parts(n):
            if n < 2:
                return [(raw[:, 0:DC * IS].rearrange("p (c i) -> p c i", c=DC),
                         [(gs, us)[n][:, h, :, :] for h in (HI, LO)])]
            tail = IS - 5 * P
            return [(raw[:, 0:5 * D].rearrange("p (c d) -> p c d", c=5), [ds_[:, h, 0:5, :] for h in (HI, LO)]),
                    (raw[0:tail, 5 * D:6 * D], [ds_[0:tail, h, 5, :] for h in (HI, LO)])]

        with nc.Block() as block:
            @block.sync
            def _(sp):
                sp.dma_start(gw[:, :], gate_w).then_inc(gw_in, 16)
                sp.dma_start(x[:, :, :], rowsof[:, 0:GT, :]).then_inc(x_in, 16)
                for dst, src in ((gamma_b, gamma), (beta_b, beta)):
                    sp.dma_start(dst[:, :], src.rearrange("(a n) -> a n", a=1).to_broadcast([P, D])
                                 ).then_inc(gb_in, 16)

                def zero_slots(n):
                    sp.dma_start(slots_d.rearrange("r (h n) -> (r h) n", h=2)[n * 2048:(n + 1) * 2048, :]
                                 .rearrange("(a p) n -> p a n", p=P),
                                 zeros[:, :].unsqueeze(1).to_broadcast([P, 16, D])).then_inc(slots_zero, 16)
                for n, w in enumerate((ws_gate, ws_up)):
                    if n:
                        sp.wait_ge(raw_lo, n)
                    sp.dma_start(raw_parts(n)[0][0], w.rearrange("(c p) i -> p c i", p=P)).then_inc(raw_in, 32)
                    if n == 0:
                        sp.wait_ge(zero_set, 1)
                    zero_slots(n)
                sp.wait_ge(raw_lo, 2)
                whole, rest = raw_parts(2)
                sp.dma_start(whole[0], ws_down[0:5 * P, :].rearrange("(c p) d -> p c d", p=P)).then_inc(raw_in, 16)
                sp.dma_start(rest[0], ws_down[5 * P:IS, :]).then_inc(raw_in, 16)
                for n in range(2, 4):
                    zero_slots(n)

                def part(t, _):
                    if shares(t):
                        if later(t, 2):
                            sp.wait_ge(xr_out, t * 16 - 16)
                        sp.dma_start(xr[:, :, :], x1of[:, bass.ds(t * GT - GT, GT), :]).then_inc(xr_in, 16)
                    if routes(t):
                        sp.wait_ge(xn_done, t + 1)
                        sp.dma_start(x1of[:, bass.ds(t * GT, GT), :], x[:, :, :]).then_inc(x1_out, 16)
                        sp.wait_ge(x1_out, t * 16 + 16)
                        if not last_of(t, NG):
                            sp.dma_start(x[:, :, :], rowsof[:, bass.ds(t * GT + GT, GT), :]).then_inc(x_in, 16)
                        sp.wait_ge(sidx_done, t + 1)
                        sp.dma_start(pickof[:, bass.ds(t * GT, GT), :], pick[:, :, :]).then_inc(pick_out, 16)
                    if shares(t):
                        sp.wait_ge(xr_done, t * GT)
                        sp.dma_start(xsof[:, bass.ds(t * GT - GT, GT), :], xr[:, :, :]).then_inc(xr_out, 16)
                repeat(sp, Steps(sp, None), NG + 1, part, head=2, tail=2)
                sp.wait_ge(pick_out, NG * 16)
                sp.wait_ge(xr_out, NG * 16)

            @block.gpsimd
            def _(pool):
                st = Steps(pool, pool_c)
                pool.memset(zeros[:, :], 0.0).then_inc(zero_set, 1)
                st.did(pool.memset(power[:, :], -0.5))
                st.did(pool.memset(own[:, :], 1.0))
                st.settle()
                st.did(pool.affine_select(out=own[:, :], in_=own[:, :], compare_op=ALU.is_ge, fill=0.0,
                                          base=0, pattern=[[1, TOK]], channel_multiplier=-S))
                st.settle()
                pool.affine_select(out=own[:, :], in_=own[:, :], compare_op=ALU.is_ge, fill=0.0,
                                   base=S - 1, pattern=[[-1, TOK]], channel_multiplier=S).then_inc(made, 1)

                fixed = Steps(pool, pool_f)

                def constants():
                    fixed.did(pool.memset(before[:, :], 1.0))
                    fixed.did(pool.memset(ones[:, :], 1.0))
                    fixed.did(pool.memset(counts[:, :, :], 0.0))
                    fixed.did(pool.iota(iota_i[:, :], pattern=[[1, E]], base=0, channel_multiplier=0))
                    fixed.settle()
                    fixed.did(pool.tensor_copy(iota_f[:, :], iota_i[:, :]))
                    fixed.did(pool.affine_select(out=before[:, :], in_=before[:, :], compare_op=ALU.is_ge, fill=0.0,
                                              base=-1, pattern=[[1, P]], channel_multiplier=-1))
                    fixed.settle()
                    pool.wait_ge(gb_in, 32)
                    pool.tensor_scalar(beta_b[:, :], beta_b[:, :], gains[:, 0:1], None, ALU.mult).then_inc(made, 1)
                    pool.tensor_scalar(gamma_b[:, :], gamma_b[:, :], gains[:, 0:1], None, ALU.mult
                                       ).then_inc(made, 1)
                    pool.wait_ge(made, 3)

                def part(t, _):
                    for n in range(3):
                        pool.wait_ge(stat_done, t * 3 + n + 1)
                        apart(pool)
                        rsqrt(pool, st, rstd[:, :], mv[:, :, 1], power[:, :], rstd_done)
                        if n == 0 and not later(t, 1):
                            constants()
                        if n == 0:
                            pool.wait_ge(y_done, t + 1)
                            pool.tensor_tensor(x[:, :, :], x[:, :, :],
                                               beta_b[:, :].unsqueeze(1).to_broadcast([P, GT, D]),
                                               ALU.add).then_inc(xb_done, 1)
                            pool.wait_ge(xb_done, t + 1)
                        if n == 1:
                            for m, tiles in enumerate(HALVES):
                                pool.wait_ge(scaled, 2 * t + m + 1)
                                pool.tensor_tensor(x[:, tiles, :], y[:, tiles, :], x[:, tiles, :], ALU.add
                                                   ).then_inc(x1_done, 1)
                    pool.wait_ge(rows_hi, t + 1)
                    pool.tensor_tensor(rows[:, :, LO, :], y[:, :, :], rows[:, :, HI, :],
                                       ALU.subtract).then_inc(rows_lo, 1)
                    pool.wait_ge(rows_lo, t + 1)
                    pool.wait_ge(sidx_done, t + 1)
                    apart(pool)
                    if not later(t, 1):
                        pool.wait_ge(slots_zero, 64)
                    for j in range(GT):
                        for k in range(2):
                            pool.indirect_dma_start(
                                slots_d, bass.IndirectOffsetOnAxis(ap=sidx[:, 2 * j + k:2 * j + k + 1], axis=0),
                                rows[:, j, :, :].rearrange("p h d -> p (h d)"), None,
                                bounds_check=E * CAP - 1, oob_is_err=False).then_inc(scattered, 16)
                repeat(pool, st, NG, part)
                pool.wait_ge(scattered, NG * GT * 32)

            @block.scalar
            def _(act):
                act.wait_ge(gw_ps, 1)
                act.activation(gwT[:, HI, :, :], bank[7][:, 0:DC * E].rearrange("p (c e) -> p c e", c=DC),
                               ACT.Copy).then_inc(gw_hi, 1)
                for n in range(3):
                    act.wait_ge(raw_in, n * 32 + 32)
                    for src, (high, _) in raw_parts(n):
                        ins = act.activation(high, src, ACT.Copy)
                    ins.then_inc(raw_hi, 1)

                def prepare(function):
                    act.activation(spare[:, :], gains[:, 0:1], function)

                def silu(t, q):
                    (_, tn), _, (_, n) = chunk(q)
                    act.wait_ge(gu_ps, t * NQ - NQ + q + 1)
                    if later(t, 2) or q >= 2:
                        act.wait_ge(h_done, t * NQ - NQ + q - 1)
                    act.activation(sg[q % 2][0:n, 0:tn * P], bank[2 * (q % 2)][0:n, 0:tn * P], ACT.Silu
                                   ).then_inc(silu_done, 1)

                def hidden_hi(t, q):
                    (t0, tn), m, (_, n) = chunk(q)
                    act.wait_ge(h_done, t * NQ - NQ + q + 1)
                    if later(t, 2):
                        act.wait_ge(down_ps, t * GT - GT)
                    elif q == 0:
                        act.wait_ge(raw_lo, 3)
                    act.activation(hT[0:n, HI, m, t0 * P:(t0 + tn) * P], hs[q % 2][0:n, 0:tn * P], ACT.Copy
                                   ).then_inc(hT_hi, 1)

                def part(t, _):
                    if shares(t):
                        silu(t, 0)
                        for q in range(NQ):
                            if q < NQ - 1:
                                silu(t, q + 1)
                            hidden_hi(t, q)
                    if routes(t):
                        prepare(ACT.Exp)
                        for j in range(GT):
                            act.wait_ge(xT_ps, t * GT + j + 1)
                            act.activation(xT[:, j, HI, :, :].rearrange("p c q -> p (c q)"), bank[TURN[j]][:, :],
                                           ACT.Copy).then_inc(xT_hi, 1)
                        if later(t, 1):
                            act.wait_ge(scattered, t * (GT * 32))
                        act.activation(rows[:, :, HI, :], y[:, :, :], ACT.Copy).then_inc(rows_hi, 1)
                        act.wait_ge(nmax_done, t + 1)
                        for j in range(GT):
                            ins = act.activation(probs[:, j, :], bank[7][:, j * E:(j + 1) * E], ACT.Exp,
                                                 bias=nmax[:, j:j + 1], accum_out=esum[:, j:j + 1])
                        ins.then_inc(exp_done, 1)
                        prepare(ACT.Silu)
                repeat(act, Steps(act, None), NG + 1, part, head=2, tail=1)

            @block.vector
            def _(dve):
                st = Steps(dve, dve_c)
                dve.wait_ge(gw_hi, 1)
                dve.tensor_tensor(gwT[:, LO, :, :], bank[7][:, 0:DC * E].rearrange("p (c e) -> p c e", c=DC),
                                  gwT[:, HI, :, :], ALU.subtract).then_inc(gw_lo, 1)

                def hidden_lo(t, q):
                    (t0, tn), m, (_, n) = chunk(q)
                    dve.wait_ge(hT_hi, t * NQ - NQ + q + 1)
                    dve.tensor_tensor(hT[0:n, LO, m, t0 * P:(t0 + tn) * P], hs[q % 2][0:n, 0:tn * P],
                                      hT[0:n, HI, m, t0 * P:(t0 + tn) * P], ALU.subtract).then_inc(hT_lo, 1)

                def beside(t, q):
                    if not shares(t):
                        if q % 4 == 2:
                            n = q // 4
                            dve.wait_ge(raw_hi, n + 1)
                            for src, (high, low) in raw_parts(n):
                                ins = dve.tensor_tensor(low, src, high, ALU.subtract)
                            ins.then_inc(raw_lo, 1)
                        return
                    (_, tn), _, (_, n) = chunk(q)
                    if q == 0 and not later(t, 2):
                        dve.wait_ge(raw_lo, 3)
                    if q >= 1:
                        hidden_lo(t, q - 1)
                    dve.wait_ge(silu_done, t * NQ - NQ + q + 1)
                    if later(t, 2) or q >= 2:
                        dve.wait_ge(hT_hi, t * NQ - NQ + q - 1)
                        dve.wait_ge(hT_lo, t * NQ - NQ + q - 1)
                    dve.tensor_tensor(hs[q % 2][0:n, 0:tn * P], sg[q % 2][0:n, 0:tn * P],
                                      bank[2 * (q % 2) + 1][0:n, 0:tn * P], ALU.mult).then_inc(h_done, 1)

                def normed(t, n, src, dst, done=None):
                    dve.wait_ge(rstd_done, 3 * t + n + 1)
                    for j in range(GT):
                        ins = dve.tensor_scalar(dst[:, j, :], src[:, j, :], mv[:, j, 0:1], rstd[:, j:j + 1],
                                                ALU.subtract, ALU.mult)
                        if done is None or j < GT - 1:
                            st.did(ins)
                        else:
                            ins.then_inc(done, 1)

                def add_own(t, tiles):
                    for j in tiles:
                        dve.wait_ge(own_ps, t * GT + j + 1)
                        dve.tensor_tensor(y[:, j, :], y[:, j, :], bank[4 + j % 3][:, :], ALU.add
                                          ).then_inc(own_added, 1)

                def add_shared(t, j):
                    if shares(t):
                        dve.wait_ge(down_ps, t * GT - GT + j + 1)
                        dve.wait_ge(xr_in, t * 16)
                        dve.scalar_tensor_tensor(out=xr[:, j, :], in0=bank[4 + j % 3][:, :], scalar=gains[:, 2:3],
                                                 in1=xr[:, j, :], op0=ALU.mult, op1=ALU.add).then_inc(xr_done, 1)

                def part(t, _):
                    if not routes(t):
                        for q in range(NQ):
                            beside(t, q)
                        hidden_lo(t, NQ - 1)
                        for j in range(GT):
                            add_shared(t, j)
                        return
                    dve.wait_ge(x_in, t * 16 + 16)
                    row_stats(dve, st, lambda j: x[:, j, :], stats, range(GT))
                    row_moments(dve, st, stats, mv, GT, stat_done)
                    if later(t, 1):
                        dve.wait_ge(xT_ps, t * GT)
                        dve.wait_ge(rows_hi, t)
                        dve.wait_ge(rows_lo, t)
                    normed(t, 0, x, y, y_done)
                    beside(t, 0)
                    st.settle()
                    dve.wait_ge(y_done, t + 1)
                    add_own(t, range(0, 3))
                    beside(t, 1)
                    add_own(t, range(3, GT))
                    beside(t, 2)
                    dve.wait_ge(own_added, t * GT + GT)
                    row_stats(dve, st, lambda j: y[:, j, :], stats, range(GT))
                    row_moments(dve, st, stats, mv, GT, stat_done)
                    beside(t, 3)
                    normed(t, 1, y, y)
                    beside(t, 4)
                    st.settle()
                    if not later(t, 1):
                        dve.wait_ge(made, 3)
                    for m, tiles in enumerate(HALVES):
                        dve.tensor_tensor(y[:, tiles, :], y[:, tiles, :],
                                          gamma_b[:, :].unsqueeze(1).to_broadcast([P, tiles.stop - tiles.start, D]),
                                          ALU.mult).then_inc(scaled, 1)
                        beside(t, 5 + m)
                    for m, tiles in enumerate(HALVES):
                        dve.wait_ge(x1_done, 2 * t + m + 1)
                        row_stats(dve, st, lambda j: x[:, j, :], stats, range(tiles.start, tiles.stop))
                        beside(t, 7 + m)
                    row_moments(dve, st, stats, mv, GT, stat_done)
                    beside(t, 9)
                    normed(t, 2, x, y, xn_done)
                    for q in range(10, NQ):
                        beside(t, q)
                    if shares(t):
                        hidden_lo(t, NQ - 1)
                    for j in range(GT):
                        dve.wait_ge(xT_hi, t * GT + j + 1)
                        dve.tensor_tensor(xT[:, j, LO, :, :].rearrange("p c q -> p (c q)"), bank[TURN[j]][:, :],
                                          xT[:, j, HI, :, :].rearrange("p c q -> p (c q)"),
                                          ALU.subtract).then_inc(xT_lo, 1)
                    dve.wait_ge(logit_ps, t + 1)
                    dve.tensor_reduce(nmax[:, :], bank[7][:, 0:GT * E].rearrange("p (j e) -> p j e", e=E),
                                      axis=AX.X, op=ALU.max, negate=True).then_inc(nmax_done, 1)
                    dve.wait_ge(exp_done, t + 1)
                    st.did(dve.reciprocal(rsum[:, :], esum[:, :]))
                    st.settle()
                    st.did(dve.tensor_tensor(probs[:, :, :], probs[:, :, :], wide(rsum[:, :], E), ALU.mult))
                    st.settle(alone=True)
                    for j in range(GT):
                        st.did(dve.max(top8[:, j, :], probs[:, j, :]))
                    st.settle(alone=True)
                    for j in range(GT):
                        st.did(dve.max_index(top8i[:, j, :], top8[:, j, :], probs[:, j, :]))
                    if later(t, 1):
                        dve.wait_ge(pick_out, t * 16)
                    st.did(dve.tensor_scalar(pick[:, :, 2:4].bitcast(F32), top8[:, :, 0:2], gains[:, 2:3], None,
                                             ALU.mult))
                    st.settle()
                    st.did(dve.tensor_copy(chosen[:, :].rearrange("p (j k) -> p j k", k=2), top8i[:, :, 0:2]))
                    st.settle()
                    st.did(dve.tensor_tensor(hot[:, :, :], iota_f[:, :].unsqueeze(1).to_broadcast([P, GT * 2, E]),
                                             wide(chosen[:, :], E), ALU.is_equal))
                    st.settle()
                    pair = hot[:, :, :].rearrange("p (j k) e -> p j k e", k=2)
                    st.did(dve.tensor_tensor(picks[:, :, :], pair[:, :, 0, :], pair[:, :, 1, :], ALU.add))
                    if later(t, 1):
                        st.did(dve.tensor_copy(counts[:, 0, :], counts[:, GT, :]))
                    else:
                        st.did(dve.tensor_copy(counts[:, GT, :], counts[:, 0, :]))
                    st.settle()
                    for j in range(GT):
                        ins = dve.tensor_tensor(counts[:, j + 1, :], counts[:, j, :], picks[:, j, :], ALU.add)
                        if j < GT - 1:
                            st.did(ins)
                            st.settle()
                    ins.then_inc(picks_done, 1)
                    add_shared(t, 0)
                    add_shared(t, 1)
                    dve.wait_ge(rank_ps, t + 1)
                    rank = bank[7][:, RANK:RANK + GT * E].rearrange("p (j e) -> p j e", e=E)
                    hits = hit[:, :, :].rearrange("p (j k) e -> p j k e", k=2)
                    for k in range(2):
                        st.did(dve.tensor_tensor(hits[:, :, k, :], pair[:, :, k, :], rank, ALU.mult))
                    st.settle()
                    st.did(dve.tensor_reduce(pos[:, :], hit[:, :, :], axis=AX.X, op=ALU.add))
                    st.settle()
                    st.did(dve.tensor_scalar(slot[:, :], pos[:, :], float(CAP - 1), None, ALU.min))
                    st.did(dve.tensor_scalar(over[:, :], pos[:, :], float(CAP), float(E * CAP),
                                             ALU.is_ge, ALU.mult))
                    st.settle()
                    st.did(dve.scalar_tensor_tensor(out=slot[:, :], in0=chosen[:, :], scalar=float(CAP),
                                                    in1=slot[:, :], op0=ALU.mult, op1=ALU.add))
                    st.settle()
                    st.did(dve.tensor_copy(pick[:, :, 0:2], slot[:, :].rearrange("p (j k) -> p j k", k=2)))
                    st.settle()
                    if later(t, 1):
                        dve.wait_ge(scattered, t * (GT * 32))
                    dve.tensor_tensor(sidx[:, :], slot[:, :], over[:, :], ALU.add).then_inc(sidx_done, 1)
                    for j in range(2, GT):
                        add_shared(t, j)
                repeat(dve, st, NG + 1, part, head=2, tail=1)

            @block.tensor
            def _(pe):
                pe.wait_ge(gw_in, 16)
                for c in range(DC):
                    ins = pe.transpose(bank[7][:, c * E:(c + 1) * E], gw[:, c * P:(c + 1) * P], ident[0:E, 0:E])
                ins.then_inc(gw_ps, 1)
                pe.wait_ge(made, 1)

                def give_own(t, tiles):
                    for j in tiles:
                        if j >= 3:
                            pe.wait_ge(own_added, t * GT + j - 2)
                        for n in range(3):
                            ins = pe.matmul(bank[4 + j % 3][:, :], own[:, bass.ds(t * (GT * P) + j * P, P)],
                                            summary[:, n, :], start=n == 0, stop=n == 2)
                        ins.then_inc(own_ps, 1)

                def gate_up(t, q):
                    (t0, tn), _, (i0, rows_) = chunk(q)
                    if later(t, 2) or q >= 2:
                        pe.wait_ge(h_done, t * NQ - NQ + q - 1)
                    for v, w_ in enumerate((gs, us)):
                        n = 0
                        for c in range(DC):
                            for a, w in PAIRS:
                                ins = pe.matmul(
                                    bank[2 * (q % 2) + v][0:rows_, 0:tn * P].rearrange("r (t q) -> r t q", q=P),
                                    w_[:, w, c, i0:i0 + rows_], xT[:, t0:t0 + tn, a, c, :],
                                    start=n == 0, stop=n == 11)
                                n += 1
                    ins.then_inc(gu_ps, 1)

                def down(t, j):
                    u = 0 if j < 3 else 1
                    pe.wait_ge(hT_hi, t * NQ - NQ + 6 * u + 6)
                    pe.wait_ge(hT_lo, t * NQ - NQ + 6 * u + 6)
                    if j >= 3:
                        pe.wait_ge(xr_done, t * GT - GT + j - 2)
                    n = 0
                    for c, (_, rows_) in enumerate(SC):
                        for a, w in PAIRS:
                            ins = pe.matmul(bank[4 + j % 3][:, :], hT[0:rows_, a, c, j * P:(j + 1) * P],
                                            ds_[0:rows_, w, c, :], start=n == 0, stop=n == 17)
                            n += 1
                    ins.then_inc(down_ps, 1)

                def part(t, _):
                    if later(t, 1):
                        pe.wait_ge(xT_hi, t * GT)
                        pe.wait_ge(xT_lo, t * GT)
                    if later(t, 2):
                        pe.wait_ge(xr_done, t * GT - GT)
                    if routes(t):
                        give_own(t, range(0, 3))
                    if shares(t):
                        if not later(t, 2):
                            pe.wait_ge(raw_lo, 3)
                        gate_up(t, 0)
                        gate_up(t, 1)
                    if routes(t):
                        give_own(t, range(3, GT))
                    if shares(t):
                        for q in range(2, NQ):
                            gate_up(t, q)
                    if routes(t):
                        if shares(t):
                            pe.wait_ge(h_done, t * NQ)
                        pe.wait_ge(xn_done, t + 1)
                        for j in range(GT):
                            for c in range(DC):
                                ins = pe.transpose(bank[TURN[j]][:, c * P:(c + 1) * P], y[:, j, c * P:(c + 1) * P],
                                                   ident[:, :])
                            ins.then_inc(xT_ps, 1)
                        for j in range(GT):
                            pe.wait_ge(xT_hi, t * GT + j + 1)
                            pe.wait_ge(xT_lo, t * GT + j + 1)
                            if j == 0:
                                if later(t, 1):
                                    pe.wait_ge(exp_done, t)
                                else:
                                    pe.wait_ge(gw_lo, 1)
                            n = 0
                            for c in range(DC):
                                for a, w in PAIRS:
                                    ins = pe.matmul(bank[7][:, j * E:(j + 1) * E], xT[:, j, a, c, :],
                                                    gwT[:, w, c, :], start=n == 0, stop=n == 11)
                                    n += 1
                        ins.then_inc(logit_ps, 1)
                    if shares(t):
                        for j in range(3):
                            down(t, j)
                    if routes(t):
                        pe.wait_ge(picks_done, t + 1)
                        at = slice(RANK, RANK + GT * E)
                        pe.matmul(bank[7][:, at], before[:, :], picks[:, :, :].rearrange("p j e -> p (j e)"),
                                  start=True, stop=False)
                        pe.matmul(bank[7][:, at], ones[:, :], counts[:, 0:GT, :].rearrange("p j e -> p (j e)"),
                                  start=False, stop=True).then_inc(rank_ps, 1)
                    if shares(t):
                        for j in range(3, GT):
                            down(t, j)
                repeat(pe, Steps(pe, None), NG + 1, part, head=2, tail=1)


def expert_phase(nc, g, w_gate, w_up, w_down, down2, squares, slots_d, eout_d):
    ident, identb, bank, downT = g["ident"], g["identb"], g["bank"], g["downT"]
    wT = g["wT"]
    with ExitStack() as es:
        def sb(name, shape, dt=F32):
            return es.enter_context(nc.sbuf_tensor(name, shape, dt))

        def sem(name):
            return nc.alloc_semaphore(f"expert_{name}")

        gu_raw = sb("gu_raw", [P, 2, DC, I])
        down_raw = sb("down_raw", [P, 3, D])
        gu = [sb(f"gu{k}", [P, 2, 2, DC, I], BF16) for k in range(2)]
        dn = sb("dn", [P, 2, 3, D], BF16)
        xs = sb("xs", [P, 2, 2, D], BF16)
        xsT = [sb(f"xsT{k}", [P, 2, DC, CAP], BF16) for k in range(2)]
        act_g = [sb(f"act_g{k}", [P, CAP]) for k in range(2)]
        h = [sb(f"h{k}", [P, CAP]) for k in range(2)]
        hT = sb("hT", [P, 2, 3, CAP], BF16)
        eo = [sb(f"eo{k}", [P, D]) for k in range(2)]
        wstage = sb("estage", [P, D])
        wr = sb("er", [P, D])
        wm, dq = sb("em", [P, D]), sb("edq", [P, D])
        wscale = sb("escale", [P, D // MXB])
        wamax, winv = sb("eamax", [P, D // MXB]), sb("einv", [P, D // MXB])
        wst_in = sem("wst_in")
        square = sb("esquare", [P, D])
        sq_in = sem("sq_in")
        sq_ps, sq_hi, sq_lo = sem("sq_ps"), sem("sq_hi"), sem("sq_lo")
        dve_c, round_done, dq_done, wT_ps, wT_hi, wT_lo = (sem(n) for n in (
            "dve_c", "round_done", "dq_done", "wT_ps", "wT_hi", "wT_lo"))
        downv = down2.rearrange("(p r) (a n) -> p (r a) n", r=4, n=D)
        gu_in, down_in = [sem(f"gu_in{n}") for n in range(2)], sem("down_in")
        xs_in = sem("xs_in")
        gu_hi, gu_lo, dn_hi, dn_lo = sem("gu_hi"), sem("gu_lo"), sem("dn_hi"), sem("dn_lo")
        xs_ps, xsT_done, xsT_done_v = sem("xs_ps"), sem("xsT_done"), sem("xsT_done_v")
        gu_ps, silu_done, h_done, hT_hi, hT_lo = (sem(n) for n in (
            "gu_ps", "silu_done", "h_done", "hT_hi", "hT_lo"))
        out_ps, eo_done = sem("out_ps"), sem("eo_done")
        eo_out = [sem(f"eo_out{k}") for k in range(2)]
        with nc.Block() as block:
            @block.sync
            def _(sp):
                def load_xs(t):
                    sp.dma_start(xs[:, :, :, :].rearrange("p s h d -> p s (h d)"),
                                 slots_d[bass.ds(t * CAP, CAP), :].rearrange("(s p) d -> p s d", p=P)
                                 ).then_inc(xs_in, 16)

                def load_w(t):
                    for n, w in enumerate((w_gate, w_up)):
                        sp.dma_start(gu_raw[:, n, :, :],
                                     w[bass.ds(t, 1), :, :].rearrange("a (c p) i -> p (a c) i", p=P)
                                     ).then_inc(gu_in[n], 16)

                def load_down(t):
                    rows = w_down[bass.ds(t, 1), :, :].rearrange("a i d -> (a i) d")
                    sp.dma_start(down_raw[:, 0:2, :], rows[0:256, :].rearrange("(c p) d -> p c d", p=P)
                                 ).then_inc(down_in, 16)
                    sp.dma_start(down_raw[0:I - 256, 2, :], rows[256:I, :]).then_inc(down_in, 16)

                def load_mx(t):
                    sp.dma_start(wstage[:, :], downv[:, bass.ds(t, 1), :].rearrange("p a n -> p (a n)")
                                 ).then_inc(wst_in, 16)

                def load_squares(t):
                    for n, w in enumerate(squares):
                        sp.dma_start(square[n * 32:n * 32 + 32, :], w[bass.ds(t * 32, 32), :]
                                     ).then_inc(sq_in, 16)
                load_w(0)
                load_xs(0)
                load_down(0)
                load_mx(0)
                load_squares(0)
                sp.wait_ge(xs_ps, 2)
                load_xs(1)

                def part(t, k):
                    if not last_of(t, E):
                        sp.wait_ge(gu_hi, 2 * t + 2)
                        sp.wait_ge(gu_lo, 2 * t + 2)
                        load_w(t + 1)
                        sp.wait_ge(dn_hi, t + 1)
                        sp.wait_ge(dn_lo, t + 1)
                        load_down(t + 1)
                    if not isinstance(t, int) or t < E - 2:
                        sp.wait_ge(xs_ps, 2 * t + 4)
                        load_xs(t + 2)
                    if later(t, 1):
                        sp.wait_ge(sq_ps, t)
                        load_squares(t)
                    if not last_of(t, E):
                        sp.wait_ge(round_done, t + 1)
                        load_mx(t + 1)
                    for s in range(2):
                        sp.wait_ge(eo_done, 2 * t + s + 1)
                        sp.dma_start(eout_d[bass.ds(t * CAP + s * P, P), :], eo[s][:, :]).then_inc(eo_out[s], 16)
                repeat(sp, Steps(sp, None), E, part, unroll=2, tail=2)
                for s in range(2):
                    sp.wait_ge(eo_out[s], E * 16)

            @block.gpsimd
            def _(pool):
                def part(t, _):
                    pool.wait_ge(dn_hi, t + 1)
                    pool.tensor_tensor(dn[:, LO, 0:2, :], down_raw[:, 0:2, :], dn[:, HI, 0:2, :], ALU.subtract)
                    pool.tensor_tensor(dn[0:I - 256, LO, 2, :], down_raw[0:I - 256, 2, :],
                                       dn[0:I - 256, HI, 2, :], ALU.subtract).then_inc(dn_lo, 1)
                    pool.wait_ge(round_done, t + 1)
                    if later(t, 1):
                        pool.wait_ge(wT_ps, t)
                    pool.tensor_tensor(blocks(dq[:, :]), blocks(wr[:, :]), wide(wscale[:, :], MXB),
                                       ALU.mult).then_inc(dq_done, 1)
                repeat(pool, Steps(pool, None), E, part)

            @block.scalar
            def _(act):
                def split(t, k, n):
                    act.wait_ge(gu_in[n], t * 16 + 16)
                    if later(t, 2):
                        act.wait_ge(gu_ps, 3 * t - 3)
                    act.activation(gu[k][:, HI, n, :, :], gu_raw[:, n, :, :], ACT.Copy).then_inc(gu_hi, 1)

                def split_down(t):
                    act.wait_ge(down_in, t * 32 + 32)
                    if later(t, 1):
                        act.wait_ge(out_ps, 2 * t)
                    act.activation(dn[:, HI, 0:2, :], down_raw[:, 0:2, :], ACT.Copy)
                    act.activation(dn[0:I - 256, HI, 2, :], down_raw[0:I - 256, 2, :], ACT.Copy
                                   ).then_inc(dn_hi, 1)

                def mx_hi(t):
                    act.wait_ge(wT_ps, t + 1)
                    act.activation(downT[:, HI, bass.ds(t, 1), :, :].rearrange("p a c i -> p (a c) i"),
                                   bank[6][:, :].rearrange("p (c i) -> p c i", c=DC), ACT.Copy).then_inc(wT_hi, 1)

                def squares_hi(t):
                    act.wait_ge(sq_ps, t + 1)
                    act.activation(wT[:, HI, :, :, bass.ds(t * 32, 32)].rearrange("p c n i -> p (c n) i"),
                                   bank[7][:, :].rearrange("p (a i) -> p a i", i=32), ACT.Copy).then_inc(sq_hi, 1)

                def slots_of(t, k):
                    act.wait_ge(xs_ps, 2 * t + 1)
                    if later(t, 2):
                        act.wait_ge(gu_ps, 3 * t - 3)
                    act.activation(xsT[k][:, :, :, 0:P].rearrange("p h c q -> p (h c) q"),
                                   bank[2][:, :].bitcast(BF16).rearrange("p (c q) -> p c q", q=P),
                                   ACT.Copy).then_inc(xsT_done, 1)
                for n in range(2):
                    split(0, 0, n)
                slots_of(0, 0)
                split_down(0)

                def part(t, k):
                    for m, (_, rows) in enumerate(IC):
                        act.wait_ge(gu_ps, 3 * t + m + 1)
                        if later(t, 1) or m >= 2:
                            act.wait_ge(h_done, 3 * t + m - 1)
                        act.activation(act_g[(k + m) % 2][0:rows, :], bank[(k + m) % 2][0:rows, 0:CAP], ACT.Silu
                                       ).then_inc(silu_done, 1)
                        act.wait_ge(h_done, 3 * t + m + 1)
                        if later(t, 1):
                            act.wait_ge(out_ps, 2 * t)
                        act.activation(hT[0:rows, HI, m, :], h[(k + m) % 2][0:rows, :], ACT.Copy).then_inc(hT_hi, 1)
                        if m == 1 and not last_of(t, E):
                            split(t + 1, 1 - k, 0)
                    if not last_of(t, E):
                        slots_of(t + 1, 1 - k)
                        split(t + 1, 1 - k, 1)
                    for s in range(2):
                        act.wait_ge(out_ps, 2 * t + s + 1)
                        if later(t, 1):
                            act.wait_ge(eo_out[s], t * 16)
                        act.activation(eo[s][:, :], bank[4 + s][:, :], ACT.Copy).then_inc(eo_done, 1)
                        if s == 0 and later(t, 1):
                            mx_hi(t - 1)
                            squares_hi(t - 1)
                    if not last_of(t, E):
                        split_down(t + 1)
                repeat(act, Steps(act, None), E, part, unroll=2, tail=2)
                mx_hi(E - 1)
                squares_hi(E - 1)

            @block.vector
            def _(dve):
                st = Steps(dve, dve_c)

                def mx_low(t):
                    dve.wait_ge(wT_hi, t + 1)
                    lo, hi = (downT[:, h, bass.ds(t, 1), :, :].rearrange("p a c i -> p (a c) i") for h in (LO, HI))
                    dve.tensor_tensor(lo, bank[6][:, :].rearrange("p (c i) -> p c i", c=DC), hi,
                                      ALU.subtract).then_inc(wT_lo, 1)

                def squares_low(t):
                    dve.wait_ge(sq_hi, t + 1)
                    lo, hi = (wT[:, h, :, :, bass.ds(t * 32, 32)].rearrange("p c n i -> p (c n) i")
                              for h in (LO, HI))
                    dve.tensor_tensor(lo, bank[7][:, :].rearrange("p (a i) -> p a i", i=32), hi,
                                      ALU.subtract).then_inc(sq_lo, 1)

                def mx_piece(t, k, n):
                    if n == 0:
                        dve.wait_ge(wst_in, t * 16 + 16)
                        if later(t, 1):
                            dve.wait_ge(dq_done, t)
                        mx_scales(dve, st, wstage[:, :], wamax[:, :], wscale[:, :], winv[:, :])
                    if n == 1:
                        mx_round(dve, st, wstage[:, :], winv[:, :], wr[:, :], wm[:, :])
                    if n == 2:
                        dve.tensor_tensor(wr[:, :], wr[:, :], wm[:, :], ALU.subtract).then_inc(round_done, 1)

                def split(t, k, n):
                    dve.wait_ge(gu_hi, 2 * t + n + 1)
                    dve.tensor_tensor(gu[k][:, LO, n, :, :].rearrange("p c i -> p (c i)"),
                                      gu_raw[:, n, :, :].rearrange("p c i -> p (c i)"),
                                      gu[k][:, HI, n, :, :].rearrange("p c i -> p (c i)"),
                                      ALU.subtract).then_inc(gu_lo, 1)

                def slots_of(t, k):
                    dve.wait_ge(xs_ps, 2 * t + 2)
                    if later(t, 2):
                        dve.wait_ge(gu_ps, 3 * t - 3)
                    dve.tensor_copy(xsT[k][:, :, :, P:CAP].rearrange("p h c q -> p (h c) q"),
                                    bank[3][:, :].bitcast(BF16).rearrange("p (c q) -> p c q", q=P)
                                    ).then_inc(xsT_done_v, 1)
                for n in range(2):
                    split(0, 0, n)
                slots_of(0, 0)

                def part(t, k):
                    for m, (_, rows) in enumerate(IC):
                        dve.wait_ge(silu_done, 3 * t + m + 1)
                        if later(t, 1) or m >= 2:
                            dve.wait_ge(hT_hi, 3 * t + m - 1)
                            dve.wait_ge(hT_lo, 3 * t + m - 1)
                        dve.tensor_tensor(h[(k + m) % 2][0:rows, :], act_g[(k + m) % 2][0:rows, :],
                                          bank[(k + m) % 2][0:rows, CAP:2 * CAP], ALU.mult).then_inc(h_done, 1)
                        mx_piece(t, k, m)
                        dve.wait_ge(hT_hi, 3 * t + m + 1)
                        if later(t, 1):
                            dve.wait_ge(out_ps, 2 * t)
                        dve.tensor_tensor(hT[0:rows, LO, m, :], h[(k + m) % 2][0:rows, :], hT[0:rows, HI, m, :],
                                          ALU.subtract).then_inc(hT_lo, 1)
                    if not last_of(t, E):
                        slots_of(t + 1, 1 - k)
                        for n in range(2):
                            split(t + 1, 1 - k, n)
                    if later(t, 1):
                        mx_low(t - 1)
                        squares_low(t - 1)
                    dve.wait_ge(round_done, t + 1)
                repeat(dve, st, E, part, unroll=2, tail=2)
                mx_low(E - 1)
                squares_low(E - 1)

            @block.tensor
            def _(pe):
                def turn(t, k):
                    pe.wait_ge(xs_in, t * 16 + 16)
                    for s in range(2):
                        if later(t, 1):
                            pe.wait_ge((xsT_done, xsT_done_v)[s], t)
                        for q in range(2 * DC):
                            ins = pe.transpose(bank[2 + s][:, q * 64:(q + 1) * 64].bitcast(BF16),
                                               xs[:, s, q // DC, (q % DC) * P:(q % DC + 1) * P], identb[:, :])
                        ins.then_inc(xs_ps, 1)

                def mx_turn(t):
                    pe.wait_ge(dq_done, t + 1)
                    if later(t, 1):
                        pe.wait_ge(wT_lo, t)
                    for c in range(DC):
                        ins = pe.transpose(bank[6][:, c * P:(c + 1) * P], dq[:, c * P:(c + 1) * P], ident[:, :])
                    ins.then_inc(wT_ps, 1)

                def turn_squares(t, k):
                    pe.wait_ge(sq_in, t * 64 + 64)
                    if later(t, 1):
                        pe.wait_ge(sq_lo, t)
                    for c in range(DC):
                        ins = pe.transpose(bank[7][:, c * P:(c + 1) * P], square[:, c * P:(c + 1) * P],
                                           ident[:, :])
                    ins.then_inc(sq_ps, 1)
                turn(0, 0)

                def part(t, k):
                    pe.wait_ge(xsT_done, t + 1)
                    pe.wait_ge(xsT_done_v, t + 1)
                    pe.wait_ge(gu_hi, 2 * t + 2)
                    pe.wait_ge(gu_lo, 2 * t + 2)
                    for m, (i0, rows) in enumerate(IC):
                        if later(t, 1) or m >= 2:
                            pe.wait_ge(h_done, 3 * t + m - 1)
                        for u in range(2):
                            n = 0
                            for c in range(DC):
                                for a, w in PAIRS:
                                    ins = pe.matmul(bank[(k + m) % 2][0:rows, u * CAP:(u + 1) * CAP],
                                                    gu[k][:, w, u, c, i0:i0 + rows], xsT[k][:, a, c, :],
                                                    start=n == 0, stop=n == 11)
                                    n += 1
                        ins.then_inc(gu_ps, 1)
                    if not last_of(t, E):
                        turn(t + 1, 1 - k)
                    if later(t, 1):
                        mx_turn(t - 1)
                        turn_squares(t - 1, 1 - k)
                    pe.wait_ge(hT_hi, 3 * t + 3)
                    pe.wait_ge(hT_lo, 3 * t + 3)
                    pe.wait_ge(dn_lo, t + 1)
                    for s in range(2):
                        if later(t, 1):
                            pe.wait_ge(eo_done, 2 * t + s - 1)
                        n = 0
                        for c, (_, rows) in enumerate(IC):
                            for a, w in PAIRS:
                                ins = pe.matmul(bank[4 + s][:, :], hT[0:rows, a, c, s * P:(s + 1) * P],
                                                dn[0:rows, w, c, :], start=n == 0, stop=n == 8)
                                n += 1
                        ins.then_inc(out_ps, 1)
                repeat(pe, Steps(pe, None), E, part, unroll=2, tail=2)
                mx_turn(E - 1)
                turn_squares(E - 1, 1)


def attention_phase(nc, g, ctx, xs_d, pick_d, eout_d, x2_d, x3_d):
    ident, gains, bank, wT = g["ident"], g["gains"], g["bank"], g["wT"]
    WQ, WK, WV, WO = range(4)
    NB = 4
    GR = B // NB
    SCALE = float(D) ** -0.5
    KEYS = CTX + S
    VC = CT + [(CTX, S)]
    with ExitStack() as es:
        def sb(name, shape, dt=F32):
            return es.enter_context(nc.sbuf_tensor(name, shape, dt))

        def sem(name):
            return nc.alloc_semaphore(f"attention_{name}")

        crow = [sb(f"arow{k}", [P, 3, D]) for k in range(2)]
        V = sb("V", [P, 2, 3, D], BF16)
        Vn = [sb(f"Vn{k}", [S, 2, D], BF16) for k in range(2)]
        KT = sb("KT", [P, 2, DC, CTX], BF16)
        xin = [sb(f"xin{k}", [S, D]) for k in range(NB)]
        pick = [sb(f"apick{k}", [S, 4], U32) for k in range(NB)]
        fetched = sb("fetched", [S, 2, D])
        xres = [sb(f"xres{k}", [S, D]) for k in range(2)]
        xn = sb("axn", [S, NB, D])
        xgT = sb("xgT", [P, 2, DC, NB * S], BF16)
        qT, nkT = sb("qT", [P, 2, DC, NB * S], BF16), sb("nkT", [P, 2, DC, NB * S], BF16)
        first = [fetched[:, :, :], xn[:, 2:4, :]] + [
            part[0:S, :, :, :].rearrange("p h c i -> p (h c i)").bitcast(F32)[:, 0:2 * D].rearrange(
                "p (e d) -> p e d", e=2) for part in (qT, nkT)]
        prob = sb("prob", [S, KEYS + LAST - S])
        pT = sb("pT", [P, 2, 4, S], BF16)
        o = sb("o", [S, D])
        oT = sb("oT", [P, 2, DC, S], BF16)
        nmax, esum, rinv = (sb(n, [S, 2]) for n in ("anmax", "aesum", "arinv"))
        stats, mv, rstd, power = sb("astats", [S, 6]), sb("amv", [S, 2]), sb("arstd", [S, 1]), sb("apower", [S, 1])
        crow_in, xres_in, x3_out = ([sem(f"{n}{k}") for k in range(2)] for n in (
            "crow_in", "xres_in", "x3_out"))
        got, first_got = sem("got"), [sem(f"first_got{i}") for i in range(NB)]
        xin_in, x2_out = ([sem(f"{n}{k}") for k in range(NB)] for n in ("xin_in", "x2_out"))
        first_done, x2_done = sem("first_done"), sem("x2_done")
        dve_c, pool_c, const_set = sem("dve_c5"), sem("pool_c5"), sem("const_set")
        stat_done, rstd_done, xn_done = sem("astat_done"), sem("arstd_done"), sem("axn_done")
        x_ps, xg_hi, xg_lo = sem("x_ps"), sem("xg_hi"), sem("xg_lo")
        qk_ps, qk_hi, qk_lo = sem("qk_ps"), sem("qk_hi"), sem("qk_lo")
        kT_ps, kT_hi, kT_lo = sem("kT_ps"), sem("kT_hi"), sem("kT_lo")
        vn_ps, vn_hi, vn_lo = sem("vn_ps"), sem("vn_hi"), sem("vn_lo")
        v_hi, v_lo = sem("v_hi"), sem("v_lo")
        s_ps, nmax_done, exp_done, rinv_done = sem("s_ps"), sem("anmax_done"), sem("aexp_done"), sem("rinv_done")
        pT_ps, pT_hi, pT_lo = sem("pT_ps"), sem("pT_hi"), sem("pT_lo")
        pv_ps, o_done = sem("pv_ps"), sem("o_done")
        oT_ps, oT_hi, oT_lo = sem("oT_ps"), sem("oT_hi"), sem("oT_lo")
        wo_ps, x3_done = sem("wo_ps"), sem("x3_done")

        def normed_at(t, i, more=0):
            ahead, place = divmod(i + NB + 1 + more, NB)
            return None if isinstance(t, int) and t + ahead >= GR else (t + ahead, place)

        def beyond(b, n):
            return not isinstance(b, int) or b >= n

        def dma_count(b, k, each=16):
            return b * (each // 2) + (each if k == 0 else each // 2)

        with nc.Block() as block:
            @block.sync
            def _(sp):
                def load_xin(t, i):
                    b = t * NB + i
                    sp.dma_start(xin[i][:, :], xs_d[bass.ds(b * S, S), :]).then_inc(xin_in[i], 16)
                    sp.dma_start(pick[i][:, :], pick_d[bass.ds(b * S, S), :]).then_inc(xin_in[i], 16)

                def load_xres(b, k):
                    sp.dma_start(xres[k][:, :], x2_d[bass.ds(b * S, S), :]).then_inc(xres_in[k], 16)

                def send_x2(t, i):
                    b = t * NB + i
                    sp.wait_ge(xn_done, b + 1)
                    sp.dma_start(x2_d[bass.ds(b * S, S), :], xin[i][:, :]).then_inc(x2_out[i], 16)
                    sp.wait_ge(x2_out[i], t * 16 + 16)
                    if not last_of(t, GR):
                        load_xin(t + 1, i)

                for i in range(NB):
                    load_xin(0, i)
                for i in range(NB):
                    send_x2(0, i)
                for b in range(2):
                    load_xres(b, b)
                send_x2(1, 0)

                def part(t, _):
                    for i in range(NB):
                        b, k = t * NB + i, i % 2
                        if normed_at(t, i):
                            send_x2(*normed_at(t, i))
                        sp.wait_ge(x3_done, b + 1)
                        sp.dma_start(x3_d[bass.ds(b * S, S), :], xres[k][:, :]).then_inc(x3_out[k], 16)
                        if not (last_of(t, GR) and i >= 2):
                            sp.wait_ge(x3_out[k], dma_count(b, k))
                            load_xres(b + 2, k)
                repeat(sp, Steps(sp, None), GR, part, tail=3)
                for k in range(2):
                    sp.wait_ge(x3_out[k], B // 2 * 16)

            @block.gpsimd
            def _(pool):
                st = Steps(pool, pool_c)
                pool.memset(power[:, :], -0.5)
                pool.memset(prob[:, KEYS:], 0.0).then_inc(const_set, 1)
                pool.wait_ge(const_set, 1)

                def norm(n):
                    pool.wait_ge(stat_done, n + 1)
                    apart(pool)
                    rsqrt(pool, st, rstd[:, :], mv[:, 1:2], power[:, :], rstd_done)

                def values(b, k):
                    pool.wait_ge(v_hi, b + 1)
                    pool.tensor_tensor(V[:, LO, 0:2, :], crow[k][:, 0:2, :], V[:, HI, 0:2, :], ALU.subtract)
                    pool.tensor_tensor(V[0:LAST, LO, 2, :], crow[k][0:LAST, 2, :], V[0:LAST, HI, 2, :],
                                       ALU.subtract).then_inc(v_lo, 1)

                def fetch(t, i):
                    b = t * NB + i
                    pool.wait_ge(xin_in[i], t * 32 + 32)
                    if beyond(b, NB):
                        pool.wait_ge(x2_done, b)
                    apart(pool)
                    place, signal = (fetched, got) if beyond(b, NB) else (first[i], first_got[i])
                    for n in range(2):
                        pool.indirect_dma_start(place[:, n, :], None, eout_d,
                                                bass.IndirectOffsetOnAxis(ap=pick[i][:, n:n + 1], axis=0),
                                                bounds_check=E * CAP - 1, oob_is_err=False
                                                ).then_inc(signal, 16)
                for i in range(NB):
                    fetch(0, i)
                for n in range(NB):
                    norm(n)
                fetch(1, 0)
                values(0, 0)
                norm(NB)
                fetch(1, 1)

                def part(t, _):
                    for i in range(NB):
                        if normed_at(t, i):
                            norm(t * NB + i + NB + 1)
                            if normed_at(t, i, 1):
                                fetch(*normed_at(t, i, 1))
                        if not (last_of(t, GR) and i == NB - 1):
                            values(t * NB + i + 1, (i + 1) % 2)
                repeat(pool, st, GR, part, tail=2)

            @block.scalar
            def _(act):
                def load_ctx(b, k):
                    row = ctx[bass.ds(b, 1), :, :].rearrange("a t d -> (a t) d")
                    act.dma_start(crow[k][:, 0:2, :], row[0:256, :].rearrange("(c p) d -> p c d", p=P)
                                 ).then_inc(crow_in[k], 16)
                    act.dma_start(crow[k][0:LAST, 2, :], row[256:CTX, :]).then_inc(crow_in[k], 16)

                def keys_hi(b):
                    for c in range(DC):
                        act.wait_ge(kT_ps, b * DC + c + 1)
                        if c == 0 and beyond(b, 1):
                            act.wait_ge(s_ps, b)
                        act.activation(KT[:, HI, c, :], bank[1 + c % 2][:, 0:CTX], ACT.Copy).then_inc(kT_hi, 1)

                def rows_hi(t, batches):
                    for i in batches:
                        act.wait_ge(x_ps, t * NB + i + 1)
                        act.activation(xgT[:, HI, :, i * S:(i + 1) * S],
                                       bank[1 + i % 2][:, 0:DC * S].rearrange("p (c s) -> p c s", c=DC),
                                       ACT.Copy).then_inc(xg_hi, 1)

                def project_hi(t):
                    for q in range(8):
                        act.wait_ge(qk_ps, t * 8 + q + 1)
                        act.activation((qT, nkT)[q // DC][:, HI, q % DC, :], bank[(3, 5)[q % 2]][:, 0:NB * S],
                                       ACT.Copy).then_inc(qk_hi, 1)

                def new_values_hi(b, k):
                    act.wait_ge(vn_ps, b + 1)
                    act.activation(Vn[k][:, HI, :], bank[3][0:S, :], ACT.Copy).then_inc(vn_hi, 1)

                def values_hi(b, k):
                    act.wait_ge(crow_in[k], dma_count(b, k, 32))
                    if beyond(b, 1):
                        act.wait_ge(pv_ps, b)
                    act.activation(V[:, HI, 0:2, :], crow[k][:, 0:2, :], ACT.Copy)
                    act.activation(V[0:LAST, HI, 2, :], crow[k][0:LAST, 2, :], ACT.Copy).then_inc(v_hi, 1)

                def attended_hi(b):
                    act.wait_ge(oT_ps, b + 1)
                    if beyond(b, 1):
                        act.wait_ge(wo_ps, b)
                    act.activation(oT[:, HI, :, :].rearrange("p c s -> p (c s)"), bank[6][:, 0:DC * S],
                                   ACT.Copy).then_inc(oT_hi, 1)
                for b in range(2):
                    load_ctx(b, b)
                rows_hi(0, range(NB))
                project_hi(0)
                keys_hi(0)
                new_values_hi(0, 0)
                values_hi(0, 0)
                act.wait_ge(const_set, 1)

                def part(t, _):
                    for i in range(NB):
                        b, k = t * NB + i, i % 2
                        act.wait_ge(nmax_done, b + 1)
                        if beyond(b, 1):
                            act.wait_ge(pT_ps, b)
                        act.activation(prob[:, 0:KEYS], bank[0][0:S, 0:KEYS], ACT.Exp, scale=SCALE,
                                       bias=nmax[:, k:k + 1], accum_out=esum[:, k:k + 1]).then_inc(exp_done, 1)
                        if i >= 2 and not last_of(t, GR):
                            rows_hi(t + 1, range(2 * i - 4, 2 * i - 2))
                        if beyond(b, 1):
                            attended_hi(b - 1)
                        if not (last_of(t, GR) and i == NB - 1):
                            new_values_hi(b + 1, (i + 1) % 2)
                            keys_hi(b + 1)
                        if i == NB - 1 and not last_of(t, GR):
                            project_hi(t + 1)
                        act.wait_ge(pT_ps, b + 1)
                        if beyond(b, 1):
                            act.wait_ge(pv_ps, b)
                        act.activation(pT[:, HI, 0:2, :].rearrange("p c s -> p (c s)"), bank[4][:, 0:2 * S], ACT.Copy)
                        act.activation(pT[0:LAST, HI, 2:4, :].rearrange("p c s -> p (c s)"),
                                       bank[4][0:LAST, 2 * S:4 * S], ACT.Copy).then_inc(pT_hi, 1)
                        if not (last_of(t, GR) and i >= 2):
                            act.wait_ge(v_lo, b + 1)
                            act.wait_ge(kT_ps, b * DC + DC)
                            load_ctx(b + 2, k)
                        act.wait_ge(pv_ps, b + 1)
                        act.wait_ge(rinv_done, b + 1)
                        act.activation(o[:, :], bank[5][0:S, :], ACT.Copy, scale=rinv[:, k:k + 1]).then_inc(o_done, 1)
                        if not (last_of(t, GR) and i == NB - 1):
                            values_hi(b + 1, (i + 1) % 2)
                repeat(act, Steps(act, None), GR, part, tail=1)
                attended_hi(B - 1)

            @block.vector
            def _(dve):
                st = Steps(dve, dve_c)

                def norm(t, k):
                    n, slot = t * NB + k, k
                    dve.wait_ge(xin_in[k], t * 32 + 32)
                    if beyond(n, NB):
                        place = fetched
                        dve.wait_ge(got, n * 32 - (NB - 1) * 32)
                    else:
                        place = first[k]
                        dve.wait_ge(first_got[k], 32)
                    if beyond(n, 1):
                        dve.wait_ge(stat_done, n)
                    weights = pick[k][:, 2:4].bitcast(F32)
                    for e, (done, count) in enumerate(((first_done, n + 1), (x2_done, n + 1))):
                        dve.scalar_tensor_tensor(out=xin[k][:, :], in0=place[:, e, :],
                                                 scalar=weights[:, e:e + 1], in1=xin[k][:, :],
                                                 op0=ALU.mult, op1=ALU.add).then_inc(done, 1)
                        dve.wait_ge(done, count)
                    st.did(dve.bn_stats(stats[:, :], xin[k][:, :]))
                    st.settle(alone=True)
                    dve.bn_aggr(mv[:, :], stats[:, :]).then_inc(stat_done, 1)
                    dve.wait_ge(rstd_done, n + 1)
                    dve.wait_ge(stat_done, n + 1)
                    if beyond(n, NB):
                        dve.wait_ge(x_ps, n - NB + 1)
                    dve.tensor_scalar(xn[:, slot, :], xin[k][:, :], mv[:, 0:1], rstd[:, 0:1],
                                      ALU.subtract, ALU.mult).then_inc(xn_done, 1)

                def keys_lo(b):
                    for c in range(DC):
                        dve.wait_ge(kT_hi, b * DC + c + 1)
                        dve.tensor_tensor(KT[:, LO, c, :], bank[1 + c % 2][:, 0:CTX], KT[:, HI, c, :],
                                          ALU.subtract).then_inc(kT_lo, 1)

                def rows_lo(t, batches):
                    for i in batches:
                        dve.wait_ge(xg_hi, t * NB + i + 1)
                        dve.tensor_tensor(xgT[:, LO, :, i * S:(i + 1) * S],
                                          bank[1 + i % 2][:, 0:DC * S].rearrange("p (c s) -> p c s", c=DC),
                                          xgT[:, HI, :, i * S:(i + 1) * S], ALU.subtract).then_inc(xg_lo, 1)

                def project_lo(t):
                    for q in range(8):
                        dve.wait_ge(qk_hi, t * 8 + q + 1)
                        w = (qT, nkT)[q // DC]
                        dve.tensor_tensor(w[:, LO, q % DC, :], bank[(3, 5)[q % 2]][:, 0:NB * S],
                                          w[:, HI, q % DC, :], ALU.subtract).then_inc(qk_lo, 1)

                def new_values_lo(b, k):
                    dve.wait_ge(vn_hi, b + 1)
                    dve.tensor_tensor(Vn[k][:, LO, :], bank[3][0:S, :], Vn[k][:, HI, :],
                                      ALU.subtract).then_inc(vn_lo, 1)

                def attended_lo(b):
                    dve.wait_ge(oT_hi, b + 1)
                    dve.tensor_tensor(oT[:, LO, :, :].rearrange("p c s -> p (c s)"), bank[6][:, 0:DC * S],
                                      oT[:, HI, :, :].rearrange("p c s -> p (c s)"), ALU.subtract).then_inc(oT_lo, 1)

                def add(b, k):
                    dve.wait_ge(wo_ps, b + 1)
                    dve.wait_ge(xres_in[k], dma_count(b, k))
                    dve.scalar_tensor_tensor(out=xres[k][:, :], in0=bank[7][0:S, :], scalar=gains[0:S, 1:2],
                                             in1=xres[k][:, :], op0=ALU.mult, op1=ALU.add).then_inc(x3_done, 1)
                for n in range(NB):
                    norm(0, n)
                rows_lo(0, range(NB))
                project_lo(0)
                keys_lo(0)
                new_values_lo(0, 0)
                norm(1, 0)

                def part(t, _):
                    for i in range(NB):
                        b, k = t * NB + i, i % 2
                        dve.wait_ge(s_ps, b + 1)
                        if beyond(b, 2):
                            dve.wait_ge(exp_done, b - 1)
                        st.did(dve.tensor_reduce(nmax[:, k:k + 1], bank[0][0:S, 0:KEYS], axis=AX.X, op=ALU.max,
                                                 negate=True))
                        st.settle()
                        dve.tensor_scalar(nmax[:, k:k + 1], nmax[:, k:k + 1], SCALE, None, ALU.mult
                                          ).then_inc(nmax_done, 1)
                        if i >= 2 and not last_of(t, GR):
                            rows_lo(t + 1, range(2 * i - 4, 2 * i - 2))
                        if beyond(b, 1):
                            attended_lo(b - 1)
                        if not (last_of(t, GR) and i == NB - 1):
                            new_values_lo(b + 1, (i + 1) % 2)
                            keys_lo(b + 1)
                        if i == NB - 1 and not last_of(t, GR):
                            project_lo(t + 1)
                        dve.wait_ge(exp_done, b + 1)
                        if beyond(b, 2):
                            dve.wait_ge(o_done, b - 1)
                        dve.reciprocal(rinv[:, k:k + 1], esum[:, k:k + 1]).then_inc(rinv_done, 1)
                        dve.wait_ge(pT_hi, b + 1)
                        dve.tensor_tensor(pT[:, LO, 0:2, :].rearrange("p c s -> p (c s)"), bank[4][:, 0:2 * S],
                                          pT[:, HI, 0:2, :].rearrange("p c s -> p (c s)"), ALU.subtract)
                        dve.tensor_tensor(pT[0:LAST, LO, 2:4, :].rearrange("p c s -> p (c s)"),
                                          bank[4][0:LAST, 2 * S:4 * S],
                                          pT[0:LAST, HI, 2:4, :].rearrange("p c s -> p (c s)"),
                                          ALU.subtract).then_inc(pT_lo, 1)
                        if beyond(b, 1):
                            add(b - 1, 1 - k)
                        if normed_at(t, i):
                            norm(*normed_at(t, i))
                repeat(dve, st, GR, part, tail=2)
                attended_lo(B - 1)
                add(B - 1, 1)

            @block.tensor
            def _(pe):
                def turn_rows(t, batches):
                    for i in batches:
                        pe.wait_ge(xn_done, t * NB + i + 1)
                        if len(batches) == NB and i >= 2:
                            pe.wait_ge(xg_lo, t * NB + i - 1)
                        for c in range(DC):
                            ins = pe.transpose(bank[1 + i % 2][:, c * S:(c + 1) * S], xn[:, i, c * P:(c + 1) * P],
                                               ident[0:S, 0:S])
                        ins.then_inc(x_ps, 1)

                def turn_keys(b, k, chunks):
                    pe.wait_ge(crow_in[k], dma_count(b, k, 32))
                    for c in chunks:
                        if c >= 2:
                            pe.wait_ge(kT_lo, b * DC + c - 1)
                        for r, (t0, rows) in enumerate(CT):
                            ins = pe.transpose(bank[1 + c % 2][:, t0:t0 + rows],
                                               crow[k][0:rows, r, c * P:(c + 1) * P], ident[0:rows, 0:rows])
                        ins.then_inc(kT_ps, 1)

                def project(t):
                    pe.wait_ge(xg_hi, t * NB + NB)
                    pe.wait_ge(xg_lo, t * NB + NB)
                    for q in range(8):
                        if q >= 2:
                            pe.wait_ge(qk_lo, t * 8 + q - 1)
                        w = (WQ, WK)[q // DC]
                        n = 0
                        for c in range(DC):
                            for a, h in PAIRS:
                                ins = pe.matmul(bank[(3, 5)[q % 2]][:, 0:NB * S],
                                                wT[:, h, c, w, (q % DC) * P:(q % DC + 1) * P], xgT[:, a, c, :],
                                                start=n == 0, stop=n == 11)
                                n += 1
                        ins.then_inc(qk_ps, 1)

                def new_values(b, i):
                    n = 0
                    for c in range(DC):
                        for a, h in PAIRS:
                            ins = pe.matmul(bank[3][0:S, :], xgT[:, a, c, i * S:(i + 1) * S], wT[:, h, c, WV, :],
                                            start=n == 0, stop=n == 11)
                            n += 1
                    ins.then_inc(vn_ps, 1)

                def turn_attended(b):
                    pe.wait_ge(o_done, b + 1)
                    if beyond(b, 1):
                        pe.wait_ge(oT_lo, b)
                    for c in range(DC):
                        ins = pe.transpose(bank[6][:, c * S:(c + 1) * S], o[:, c * P:(c + 1) * P], ident[0:S, 0:S])
                    ins.then_inc(oT_ps, 1)

                def output(b, half):
                    if half == 0:
                        pe.wait_ge(oT_hi, b + 1)
                        pe.wait_ge(oT_lo, b + 1)
                        if beyond(b, 1):
                            pe.wait_ge(x3_done, b)
                    for c in (0, 1) if half == 0 else (2, 3):
                        for n, (a, h) in enumerate(PAIRS):
                            ins = pe.matmul(bank[7][0:S, :], oT[:, a, c, :], wT[:, h, c, WO, :],
                                            start=c == 0 and n == 0, stop=c == DC - 1 and n == 2,
                                            skip_group_check=True)
                    if half:
                        ins.then_inc(wo_ps, 1)
                turn_rows(0, range(NB))
                project(0)
                pe.wait_ge(xg_lo, NB)
                turn_keys(0, 0, range(DC))
                pe.wait_ge(qk_lo, 8)
                new_values(0, 0)

                def part(t, _):
                    for i in range(NB):
                        b, k = t * NB + i, i % 2
                        if i == 0:
                            pe.wait_ge(qk_hi, t * 8 + 8)
                            pe.wait_ge(qk_lo, t * 8 + 8)
                        pe.wait_ge(kT_hi, b * DC + DC)
                        pe.wait_ge(kT_lo, b * DC + DC)
                        if beyond(b, 1):
                            pe.wait_ge(exp_done, b)
                        for at, n_, keys in ((0, CTX, KT), (CTX, S, nkT)):
                            n = 0
                            for c in range(DC):
                                for a, h in PAIRS:
                                    rhs = keys[:, h, c, :] if n_ == CTX else keys[:, h, c, i * S:(i + 1) * S]
                                    ins = pe.matmul(bank[0][0:S, at:at + n_], qT[:, a, c, i * S:(i + 1) * S], rhs,
                                                    start=n == 0, stop=n == 11)
                                    n += 1
                        ins.then_inc(s_ps, 1)
                        if i >= 2 and not last_of(t, GR):
                            turn_rows(t + 1, range(2 * i - 4, 2 * i - 2))
                        if beyond(b, 1):
                            turn_attended(b - 1)
                        if not (last_of(t, GR) and i == NB - 1):
                            pe.wait_ge(vn_lo, b + 1)
                            new_values(b + 1, (i + 1) % NB)
                            if i >= 2 and not last_of(t, GR):
                                pe.wait_ge(xg_lo, t * NB + NB + 2 * i - 2)
                            turn_keys(b + 1, (i + 1) % 2, range(0, 2))
                        if beyond(b, 1):
                            output(b - 1, 0)
                        if not (last_of(t, GR) and i == NB - 1):
                            turn_keys(b + 1, (i + 1) % 2, range(2, DC))
                        if i == NB - 1 and not last_of(t, GR):
                            pe.wait_ge(vn_lo, b + 2)
                            project(t + 1)
                        pe.wait_ge(exp_done, b + 1)
                        if beyond(b, 1):
                            pe.wait_ge(pT_lo, b)
                        for r, (t0, rows) in enumerate(VC):
                            rows = LAST if r == 3 else rows
                            ins = pe.transpose(bank[4][0:rows, r * S:(r + 1) * S], prob[:, t0:t0 + rows],
                                               ident[0:S, 0:S])
                        ins.then_inc(pT_ps, 1)
                        if beyond(b, 1):
                            output(b - 1, 1)
                        if i == NB - 1 and not last_of(t, GR):
                            pe.wait_ge(qk_lo, t * 8 + 16)
                        pe.wait_ge(pT_hi, b + 1)
                        pe.wait_ge(pT_lo, b + 1)
                        pe.wait_ge(v_lo, b + 1)
                        pe.wait_ge(vn_lo, b + 1)
                        if beyond(b, 1):
                            pe.wait_ge(o_done, b)
                        n = 0
                        for r, (_, rows) in enumerate(VC):
                            for a, h in PAIRS:
                                rhs = Vn[k][:, h, :] if r == 3 else V[0:rows, h, r, :]
                                ins = pe.matmul(bank[5][0:S, :], pT[0:rows, a, r, :], rhs,
                                                start=n == 0, stop=n == 11)
                                n += 1
                        ins.then_inc(pv_ps, 1)
                repeat(pe, Steps(pe, None), GR, part, tail=1)
                turn_attended(B - 1)
                output(B - 1, 0)
                output(B - 1, 1)


def mx_phase(nc, g, x3_d, out_f):
    ident, gains, bank = g["ident"], g["gains"], g["bank"]
    gateT, upT, downT = g["gateT"], g["upT"], g["downT"]
    HF = F // 2
    with ExitStack() as es:
        def sb(name, shape, dt=F32):
            return es.enter_context(nc.sbuf_tensor(name, shape, dt))

        def sem(name):
            return nc.alloc_semaphore(f"mx_{name}")

        xin = [sb(f"mxin{k}", [P, D]) for k in range(2)]
        xres = [sb(f"mxres{k}", [P, D]) for k in range(2)]
        xn, xr, xm, xq = (sb(n, [P, D]) for n in ("mxn", "mxr", "mxm", "mxq"))
        xqT = [sb(f"xqT{k}", [P, 2, DC, P], BF16) for k in range(2)]
        xamax, xscale, xinv = (sb(n, [P, D // MXB]) for n in ("xamax", "xscale", "xinv"))
        stats, mv, rstd, power = sb("mstats", [P, 6]), sb("mmv", [P, 2]), sb("mrstd", [P, 1]), sb("mpower", [P, 1])
        act_g = [sb(f"mact{k}", [P, D]) for k in range(2)]
        hraw, hr, hm, hq = (sb(n, [P, HF]) for n in ("hraw", "hr", "hm", "hq"))
        hamax, hscale, hinv = (sb(n, [P, HF // MXB]) for n in ("hamax", "hscale", "hinv"))
        hT = sb("mhT", [P, 2, 8, P], BF16)
        xin_in, xres_in, out_sent = ([sem(f"{n}{k}") for k in range(2)] for n in (
            "mxin_in", "mxres_in", "out_sent"))
        dve_c, pool_c, power_set = sem("dve_c6"), sem("pool_c6"), sem("power_set")
        stat_done, rstd_done, xn_done = sem("mstat"), sem("mrstd_done"), sem("mxn_done")
        xround_done, xdq_done, x_ps, xq_hi, xq_lo = (sem(n) for n in (
            "xround_done", "xdq_done", "mx_ps", "xq_hi", "xq_lo"))
        gu_ps, silu_done, h_done = sem("mgu_ps"), sem("msilu"), sem("mh_done")
        hround_done, hdq_done, hT_ps, hT_hi, hT_lo = (sem(n) for n in (
            "hround_done", "hdq_done", "mhT_ps", "mhT_hi", "mhT_lo"))
        y_ps, y_done = sem("y_ps"), sem("y_done")

        def dma_count(t, k):
            return t * 8 + (16 if k == 0 else 8)

        with nc.Block() as block:
            @block.sync
            def _(sp):
                def load(dst, t, k, signal):
                    sp.dma_start(dst[k][:, :], x3_d[bass.ds(t * P, P), :]).then_inc(signal[k], 16)
                for k in range(2):
                    load(xin, k, k, xin_in)
                    load(xres, k, k, xres_in)

                def part(t, k):
                    if not isinstance(t, int) or t < NT - 2:
                        sp.wait_ge(xn_done, t + 1)
                        load(xin, t + 2, k, xin_in)
                    sp.wait_ge(y_done, t + 1)
                    sp.dma_start(out_f[bass.ds(t * P, P), :], xres[k][:, :]).then_inc(out_sent[k], 16)
                    if not isinstance(t, int) or t < NT - 2:
                        sp.wait_ge(out_sent[k], dma_count(t, k))
                        load(xres, t + 2, k, xres_in)
                repeat(sp, Steps(sp, None), NT, part, unroll=2, tail=3)
                sp.wait_ge(out_sent[0], (NT + 1) // 2 * 16)
                sp.wait_ge(out_sent[1], NT // 2 * 16)

            @block.gpsimd
            def _(pool):
                st = Steps(pool, pool_c)
                pool.memset(power[:, :], -0.5).then_inc(power_set, 1)
                pool.wait_ge(power_set, 1)

                def rows(t):
                    pool.wait_ge(stat_done, t + 1)
                    apart(pool)
                    rsqrt(pool, st, rstd[:, :], mv[:, 1:2], power[:, :], rstd_done)
                    pool.wait_ge(xround_done, t + 1)
                    if later(t, 1):
                        pool.wait_ge(x_ps, t)
                    pool.tensor_tensor(blocks(xq[:, :]), blocks(xr[:, :]), wide(xscale[:, :], MXB),
                                       ALU.mult).then_inc(xdq_done, 1)
                rows(0)

                def part(t, _):
                    if not last_of(t, NT):
                        rows(t + 1)
                    for j in range(2):
                        q = 2 * t + j
                        pool.wait_ge(hround_done, q + 1)
                        if later(t, 1) or j:
                            pool.wait_ge(hT_ps, 2 * q)
                        pool.tensor_tensor(blocks(hq[:, :]), blocks(hr[:, :]), wide(hscale[:, :], MXB),
                                           ALU.mult).then_inc(hdq_done, 1)
                repeat(pool, st, NT, part, tail=1)

            @block.scalar
            def _(act):
                def rows_hi(t, k):
                    act.wait_ge(x_ps, t + 1)
                    act.activation(xqT[k][:, HI, :, :].rearrange("p c s -> p (c s)"), bank[7][:, :],
                                   ACT.Copy).then_inc(xq_hi, 1)

                def hidden_hi(q):
                    for v in range(2):
                        act.wait_ge(hT_ps, 2 * q + v + 1)
                        act.activation(hT[:, HI, 4 * v:4 * v + 4, :].rearrange("p c s -> p (c s)"),
                                       bank[4 + v][:, :], ACT.Copy).then_inc(hT_hi, 1)
                rows_hi(0, 0)

                def part(t, k):
                    for j in range(2):
                        q = 2 * t + j
                        for v in range(2):
                            act.wait_ge(gu_ps, 2 * q + v + 1)
                            act.activation(act_g[v][:, :], bank[v][:, :], ACT.Silu).then_inc(silu_done, 1)
                            if v == 0 and j == 1 and not last_of(t, NT):
                                rows_hi(t + 1, 1 - k)
                        if later(t, 1) or j:
                            hidden_hi(q - 1)
                repeat(act, Steps(act, None), NT, part, unroll=2, tail=1)
                hidden_hi(2 * NT - 1)

            @block.vector
            def _(dve):
                st = Steps(dve, dve_c)

                def rows(t, k):
                    dve.wait_ge(xin_in[k], dma_count(t, k))
                    st.did(dve.bn_stats(stats[:, :], xin[k][:, :]))
                    st.settle(alone=True)
                    dve.bn_aggr(mv[:, :], stats[:, :]).then_inc(stat_done, 1)
                    dve.wait_ge(rstd_done, t + 1)
                    dve.tensor_scalar(xn[:, :], xin[k][:, :], mv[:, 0:1], rstd[:, 0:1],
                                      ALU.subtract, ALU.mult).then_inc(xn_done, 1)
                    dve.wait_ge(xn_done, t + 1)
                    if later(t, 1):
                        dve.wait_ge(xdq_done, t)
                    mx_scales(dve, st, xn[:, :], xamax[:, :], xscale[:, :], xinv[:, :])
                    mx_round(dve, st, xn[:, :], xinv[:, :], xr[:, :], xm[:, :])
                    dve.tensor_tensor(xr[:, :], xr[:, :], xm[:, :], ALU.subtract).then_inc(xround_done, 1)

                def rows_lo(t, k):
                    dve.wait_ge(xq_hi, t + 1)
                    dve.tensor_tensor(xqT[k][:, LO, :, :].rearrange("p c s -> p (c s)"), bank[7][:, :],
                                      xqT[k][:, HI, :, :].rearrange("p c s -> p (c s)"),
                                      ALU.subtract).then_inc(xq_lo, 1)

                def hidden_lo(q):
                    for v in range(2):
                        dve.wait_ge(hT_hi, 2 * q + v + 1)
                        dve.tensor_tensor(hT[:, LO, 4 * v:4 * v + 4, :].rearrange("p c s -> p (c s)"),
                                          bank[4 + v][:, :],
                                          hT[:, HI, 4 * v:4 * v + 4, :].rearrange("p c s -> p (c s)"),
                                          ALU.subtract).then_inc(hT_lo, 1)

                def add(t, k):
                    dve.wait_ge(y_ps, t + 1)
                    dve.wait_ge(xres_in[k], dma_count(t, k))
                    row = xres[k][:, :].rearrange("p (q r) -> p r q", r=4)
                    dve.scalar_tensor_tensor(out=row, in0=bank[6][:, :].rearrange("p (r q) -> p r q", r=4),
                                             scalar=gains[:, 3:4], in1=row, op0=ALU.mult, op1=ALU.add
                                             ).then_inc(y_done, 1)
                rows(0, 0)
                rows_lo(0, 0)

                def part(t, k):
                    for j in range(2):
                        q = 2 * t + j
                        for v in range(2):
                            dve.wait_ge(silu_done, 2 * q + v + 1)
                            dve.tensor_tensor(hraw[:, v * D:(v + 1) * D], act_g[v][:, :], bank[2 + v][:, :],
                                              ALU.mult).then_inc(h_done, 1)
                            if v == 0 and j == 0 and not last_of(t, NT):
                                rows(t + 1, 1 - k)
                            if v == 0 and j == 1:
                                if not last_of(t, NT):
                                    rows_lo(t + 1, 1 - k)
                                if later(t, 1):
                                    add(t - 1, 1 - k)
                        if later(t, 1) or j:
                            hidden_lo(q - 1)
                            dve.wait_ge(hdq_done, q)
                        dve.wait_ge(h_done, 2 * q + 2)
                        mx_scales(dve, st, hraw[:, :], hamax[:, :], hscale[:, :], hinv[:, :])
                        mx_round(dve, st, hraw[:, :], hinv[:, :], hr[:, :], hm[:, :])
                        dve.tensor_tensor(hr[:, :], hr[:, :], hm[:, :], ALU.subtract).then_inc(hround_done, 1)
                repeat(dve, st, NT, part, unroll=2, tail=1)
                hidden_lo(2 * NT - 1)
                add(NT - 1, (NT - 1) % 2)

            @block.tensor
            def _(pe):
                def turn_rows(t):
                    pe.wait_ge(xdq_done, t + 1)
                    if later(t, 1):
                        pe.wait_ge(xq_lo, t)
                    for c in range(DC):
                        ins = pe.transpose(bank[7][:, c * P:(c + 1) * P], xq[:, c * P:(c + 1) * P], ident[:, :])
                    ins.then_inc(x_ps, 1)

                def gate_up(t, k, j, v):
                    q = 2 * t + j
                    if later(t, 1) or j:
                        pe.wait_ge(h_done, 2 * q + v - 1)
                    i0 = j * HF + v * D
                    for u, w in enumerate((gateT, upT)):
                        n = 0
                        for c in range(DC):
                            for a, h in PAIRS:
                                ins = pe.matmul(bank[2 * u + v][:, :], xqT[k][:, a, c, :], w[:, h, c, i0:i0 + D],
                                                start=n == 0, stop=n == 11)
                                n += 1
                    ins.then_inc(gu_ps, 1)

                def turn_hidden(q):
                    pe.wait_ge(hdq_done, q + 1)
                    for v in range(2):
                        if later(q, 1):
                            pe.wait_ge(hT_lo, 2 * q - 1 + v)
                        for c in range(4):
                            at = (4 * v + c) * P
                            ins = pe.transpose(bank[4 + v][:, c * P:(c + 1) * P], hq[:, at:at + P], ident[:, :])
                        ins.then_inc(hT_ps, 1)

                def down(t, j):
                    pe.wait_ge(hT_hi, 4 * t + 2 * j + 2)
                    pe.wait_ge(hT_lo, 4 * t + 2 * j + 2)
                    if j == 0 and later(t, 1):
                        pe.wait_ge(y_done, t)
                    n = 0
                    for c in range(8):
                        for a, h in PAIRS:
                            ins = pe.matmul(bank[6][:, :].rearrange("p (r q) -> p r q", r=4), hT[:, a, c, :],
                                            downT[:, h, 2 * j + c // 4:16:4, c % 4, :],
                                            start=n == 0 and j == 0, stop=n == 23 and j == 1)
                            n += 1
                    if j == 1:
                        ins.then_inc(y_ps, 1)
                turn_rows(0)

                def part(t, k):
                    pe.wait_ge(xq_hi, t + 1)
                    pe.wait_ge(xq_lo, t + 1)
                    for j in range(2):
                        gate_up(t, k, j, 0)
                        if later(t, 1):
                            down(t - 1, j)
                        if j == 1 and not last_of(t, NT):
                            turn_rows(t + 1)
                        gate_up(t, k, j, 1)
                        if later(t, 1) or j:
                            turn_hidden(2 * t + j - 1)
                repeat(pe, Steps(pe, None), NT, part, unroll=2, tail=1)
                down(NT - 1, 0)
                turn_hidden(2 * NT - 1)
                down(NT - 1, 1)


_INS = ["x", "ctx_2048", "g_xattn", "g_ffn", "L0_xattn_decay", "L0_xattn_W_in", "L0_xattn_b_in",
        "L0_xattn_W_out", "L0_xattn_b_out", "L0_xattn_gamma", "L0_xattn_beta", "L0_ffn_gate_w",
        "L0_ffn_w_gate", "L0_ffn_w_up", "L0_ffn_w_down", "L0_ffn_ws_gate", "L0_ffn_ws_up",
        "L0_ffn_ws_down", "L1_xattn_wq", "L1_xattn_wk", "L1_xattn_wv", "L1_xattn_wo",
        "L1_ffn_gate_w", "L1_ffn_up_w", "L1_ffn_down_w"]


def kernel(**inputs):
    import numpy as np
    import concourse.bacc as bacc
    from concourse.bass_utils import run_bass_kernel_spmd

    nc = bacc.Bacc("TRN2", target_bir_lowering=False, num_devices=1)
    arrays, args = {}, []
    for name in _INS:
        a = np.ascontiguousarray(inputs[name])
        if a.ndim == 0:
            a = a.reshape(1)
        arrays[f"in_{name}"] = a
        args.append(nc.dram_tensor(f"in_{name}", a.shape, mybir.dt.from_np(a.dtype), kind="ExternalInput").ap())
    out = nc.dram_tensor("out_0", (B, S, D), F32, kind="ExternalOutput").ap()
    program(nc, *args, out)
    r = run_bass_kernel_spmd(nc, [arrays], core_ids=[0])
    return r.results[0]["out_0"]
```
